# Optimizing a Trainium2 kernel written in Bass

```python
import numpy as np
import jax
import jax.numpy as jnp

def _softmax(x, axis=-1):
    return jax.nn.softmax(x, axis=axis)

def _gelu(x):
    return jax.nn.gelu(x, approximate=True)

def _silu(x):
    return jax.nn.silu(x)

def _sigmoid(x):
    return jax.nn.sigmoid(x)

def _layernorm(x, axis=-1, eps=1e-05):
    m = jnp.mean(x, axis=axis, keepdims=True)
    v = jnp.var(x, axis=axis, keepdims=True)
    return (x - m) / jnp.sqrt(v + eps)

def _scatter_add(tgt, idx, src, axis=0):
    return tgt.at[idx].add(src)

def _segment_sum(src, seg, n):
    return jax.ops.segment_sum(src, seg, n)
kernel_name = 'mk_adaln_ffn_d2_seqx_r8_7c649d'

def setup_inputs(seed: int=0):
    np.random.seed(seed)
    _w = jnp.asarray

    def _rec_inputs():
        import jax
        import jax.numpy as jnp
        _rk = jax.random.key(seed)
        x = -0.0003929 + 0.9999 * jax.random.normal(jax.random.fold_in(_rk, 1), (64, 32, 512), jnp.float32)
        _lenS = 32 - jax.random.randint(jax.random.fold_in(_rk, 7), (64,), 0, max(1, 32 // 4) + 1, jnp.int32)
        _lenS2 = 32 - jax.random.randint(jax.random.fold_in(_rk, 8), (64,), 0, max(1, 32 // 4) + 1, jnp.int32)
        cond_512 = 0.00782532 + 1.00527 * jax.random.normal(jax.random.fold_in(_rk, 11), (64, 64), jnp.float32)
        return (x, cond_512)
    x, cond_512 = _rec_inputs()

    def _L0_cond_setup():
        import jax, jax.numpy as jnp
        from jax import lax
        import numpy as np
        CIN, COUT, K, STYLE_DIM = (32, 32, 3, 64)
        N_LAYERS = 4
        TYPES = ('same', 'upsample', 'same', 'downsample')
        SCALE = 1.0 / float(np.sqrt(CIN * K ** 2))
        EPS = 1e-08
        _BK = np.array([1.0, 3.0, 3.0, 1.0], dtype=np.float32)
        BLUR_K = _BK / _BK.sum()

        def _blur(x, kern, pad):
            B, C, _ = x.shape
            xp = jnp.pad(x, ((0, 0), (0, 0), (pad[0], pad[1])))
            w = jnp.broadcast_to(kern.astype(x.dtype)[None, None, :], (C, 1, kern.shape[0]))
            return lax.conv_general_dilated(xp, w, (1,), 'VALID', feature_group_count=C, dimension_numbers=('NCH', 'OIH', 'NCH'))

        def _conv_same(x, w):
            p = (K - 1) // 2
            return lax.conv_general_dilated(x[None], w, (1,), [(p, p)], dimension_numbers=('NCH', 'OIH', 'NCH'))[0]

        def _conv_down(x, w):
            return lax.conv_general_dilated(x[None], w, (2,), 'VALID', dimension_numbers=('NCH', 'OIH', 'NCH'))[0]

        def _conv_up(x, w_t):
            return lax.conv_transpose(x[None], w_t, (2,), 'VALID', dimension_numbers=('NCH', 'IOH', 'NCH'), transpose_kernel=True)[0]

        def _layer(x, style, w, b, mw, mb, typ):
            s = style @ mw.T + mb
            weight = SCALE * w * s[:, None, :, None]
            demod = lax.rsqrt(jnp.sum(weight * weight, axis=(2, 3)) + EPS)
            weight = weight * demod[:, :, None, None]
            blur_k = jnp.asarray(BLUR_K)
            if typ == 'same':
                out = jax.vmap(_conv_same)(x, weight) + b[None, :, None]
            elif typ == 'upsample':
                out = jax.vmap(_conv_up)(x, weight.transpose(0, 2, 1, 3)) + b[None, :, None]
                out = _blur(out, 2.0 * blur_k, (1, 1))
            elif typ == 'downsample':
                xb = _blur(x, blur_k, (2, 2))
                out = jax.vmap(_conv_down)(xb, weight) + b[None, :, None]
            else:
                raise NotImplementedError(typ)
            return out
        key = jax.random.key(seed)
        ks = jax.random.split(key, 6)
        B, L = (16, 512)
        return {'x': jax.random.normal(ks[0], (B, CIN, L), dtype=jnp.float32), 'style': jax.random.normal(ks[1], (B, STYLE_DIM), dtype=jnp.float32), 'weights': jax.random.normal(ks[2], (N_LAYERS, COUT, CIN, K), dtype=jnp.float32), 'biases': jax.random.normal(ks[3], (N_LAYERS, COUT), dtype=jnp.float32) * 0.1, 'mod_w': jax.random.normal(ks[4], (N_LAYERS, CIN, STYLE_DIM), dtype=jnp.float32) / np.sqrt(STYLE_DIM), 'mod_b': 1.0 + 0.1 * jax.random.normal(ks[5], (N_LAYERS, CIN), dtype=jnp.float32)}
    _L0_cond_all = _L0_cond_setup()
    _L0_cond_in = {k: v for k, v in _L0_cond_all.items() if k in ('weights', 'biases', 'mod_w', 'mod_b')}
    del _L0_cond_all

    def _L0_ffn_setup():
        import jax, jax.numpy as jnp
        import numpy as np
        H = 512
        I = 256
        E = 16
        TOPK = 4
        SI = 256
        key = jax.random.key(seed)
        ks = jax.random.split(key, 9)
        s = 0.02
        return {'hidden_states': jax.random.normal(ks[0], (2, 256, H), dtype=jnp.float32), 'gate_w': jax.random.normal(ks[1], (E, H), dtype=jnp.float32) * s, 'bias': jnp.zeros((E,), dtype=jnp.float32), 'Wg': jax.random.normal(ks[2], (E, I, H), dtype=jnp.float32) * s, 'Wu': jax.random.normal(ks[3], (E, I, H), dtype=jnp.float32) * s, 'Wd': jax.random.normal(ks[4], (E, H, I), dtype=jnp.float32) * s, 'Sg': jax.random.normal(ks[5], (SI, H), dtype=jnp.float32) * s, 'Su': jax.random.normal(ks[6], (SI, H), dtype=jnp.float32) * s, 'Sd': jax.random.normal(ks[7], (H, SI), dtype=jnp.float32) * s}
    _L0_ffn_all = _L0_ffn_setup()
    _L0_ffn_in = {k: v for k, v in _L0_ffn_all.items() if k in ('gate_w', 'bias', 'Wg', 'Wu', 'Wd', 'Sg', 'Su', 'Sd')}
    del _L0_ffn_all

    def _L1_cond_setup():
        import jax, jax.numpy as jnp
        from jax import lax
        import numpy as np
        CIN, COUT, K, STYLE_DIM = (32, 32, 3, 64)
        N_LAYERS = 4
        TYPES = ('same', 'upsample', 'same', 'downsample')
        SCALE = 1.0 / float(np.sqrt(CIN * K ** 2))
        EPS = 1e-08
        _BK = np.array([1.0, 3.0, 3.0, 1.0], dtype=np.float32)
        BLUR_K = _BK / _BK.sum()

        def _blur(x, kern, pad):
            B, C, _ = x.shape
            xp = jnp.pad(x, ((0, 0), (0, 0), (pad[0], pad[1])))
            w = jnp.broadcast_to(kern.astype(x.dtype)[None, None, :], (C, 1, kern.shape[0]))
            return lax.conv_general_dilated(xp, w, (1,), 'VALID', feature_group_count=C, dimension_numbers=('NCH', 'OIH', 'NCH'))

        def _conv_same(x, w):
            p = (K - 1) // 2
            return lax.conv_general_dilated(x[None], w, (1,), [(p, p)], dimension_numbers=('NCH', 'OIH', 'NCH'))[0]

        def _conv_down(x, w):
            return lax.conv_general_dilated(x[None], w, (2,), 'VALID', dimension_numbers=('NCH', 'OIH', 'NCH'))[0]

        def _conv_up(x, w_t):
            return lax.conv_transpose(x[None], w_t, (2,), 'VALID', dimension_numbers=('NCH', 'IOH', 'NCH'), transpose_kernel=True)[0]

        def _layer(x, style, w, b, mw, mb, typ):
            s = style @ mw.T + mb
            weight = SCALE * w * s[:, None, :, None]
            demod = lax.rsqrt(jnp.sum(weight * weight, axis=(2, 3)) + EPS)
            weight = weight * demod[:, :, None, None]
            blur_k = jnp.asarray(BLUR_K)
            if typ == 'same':
                out = jax.vmap(_conv_same)(x, weight) + b[None, :, None]
            elif typ == 'upsample':
                out = jax.vmap(_conv_up)(x, weight.transpose(0, 2, 1, 3)) + b[None, :, None]
                out = _blur(out, 2.0 * blur_k, (1, 1))
            elif typ == 'downsample':
                xb = _blur(x, blur_k, (2, 2))
                out = jax.vmap(_conv_down)(xb, weight) + b[None, :, None]
            else:
                raise NotImplementedError(typ)
            return out
        key = jax.random.key(seed)
        ks = jax.random.split(key, 6)
        B, L = (16, 512)
        return {'x': jax.random.normal(ks[0], (B, CIN, L), dtype=jnp.float32), 'style': jax.random.normal(ks[1], (B, STYLE_DIM), dtype=jnp.float32), 'weights': jax.random.normal(ks[2], (N_LAYERS, COUT, CIN, K), dtype=jnp.float32), 'biases': jax.random.normal(ks[3], (N_LAYERS, COUT), dtype=jnp.float32) * 0.1, 'mod_w': jax.random.normal(ks[4], (N_LAYERS, CIN, STYLE_DIM), dtype=jnp.float32) / np.sqrt(STYLE_DIM), 'mod_b': 1.0 + 0.1 * jax.random.normal(ks[5], (N_LAYERS, CIN), dtype=jnp.float32)}
    _L1_cond_all = _L1_cond_setup()
    _L1_cond_in = {k: v for k, v in _L1_cond_all.items() if k in ('weights', 'biases', 'mod_w', 'mod_b')}
    del _L1_cond_all

    def _L1_ffn_setup():
        import jax, jax.numpy as jnp
        import numpy as np
        BATCH, TOK, DIM, OUT = (4, 256, 512, 512)
        E, R, TOP_K = (8, 16, 2)
        SCALING = 16.0 / R
        key = jax.random.key(seed)
        ks = jax.random.split(key, 6)
        return {'x': jax.random.normal(ks[0], (BATCH, TOK, DIM), dtype=jnp.float32), 'W_base': jax.random.normal(ks[1], (OUT, DIM), dtype=jnp.float32) / np.sqrt(DIM), 'b_base': jax.random.normal(ks[2], (OUT,), dtype=jnp.float32) * 0.01, 'W_gate': jax.random.normal(ks[3], (E, DIM), dtype=jnp.float32) * 0.01, 'A': jax.random.normal(ks[4], (E, R, DIM), dtype=jnp.float32) / np.sqrt(DIM), 'B': jax.random.normal(ks[5], (OUT, OUT // OUT * R * 0 + R), dtype=jnp.float32)[None].repeat(E, 0) * 0.0 + jax.random.normal(ks[5], (E, OUT, R), dtype=jnp.float32) * 0.02}
    _L1_ffn_all = _L1_ffn_setup()
    _L1_ffn_in = {k: v for k, v in _L1_ffn_all.items() if k in ('W_base', 'b_base', 'W_gate', 'A', 'B')}
    del _L1_ffn_all
    return {'x': x, 'cond_512': cond_512, 'L0_cond_weights': _L0_cond_in['weights'], 'L0_cond_biases': _L0_cond_in['biases'], 'L0_cond_mod_w': _L0_cond_in['mod_w'], 'L0_cond_mod_b': _L0_cond_in['mod_b'], 'L0_ffn_gate_w': _L0_ffn_in['gate_w'], 'L0_ffn_bias': _L0_ffn_in['bias'], 'L0_ffn_Wg': _L0_ffn_in['Wg'], 'L0_ffn_Wu': _L0_ffn_in['Wu'], 'L0_ffn_Wd': _L0_ffn_in['Wd'], 'L0_ffn_Sg': _L0_ffn_in['Sg'], 'L0_ffn_Su': _L0_ffn_in['Su'], 'L0_ffn_Sd': _L0_ffn_in['Sd'], 'L1_cond_weights': _L1_cond_in['weights'], 'L1_cond_biases': _L1_cond_in['biases'], 'L1_cond_mod_w': _L1_cond_in['mod_w'], 'L1_cond_mod_b': _L1_cond_in['mod_b'], 'L1_ffn_W_base': _L1_ffn_in['W_base'], 'L1_ffn_b_base': _L1_ffn_in['b_base'], 'L1_ffn_W_gate': _L1_ffn_in['W_gate'], 'L1_ffn_A': _L1_ffn_in['A'], 'L1_ffn_B': _L1_ffn_in['B']}

def reference(x, cond_512, L0_cond_weights, L0_cond_biases, L0_cond_mod_w, L0_cond_mod_b, L0_ffn_gate_w, L0_ffn_bias, L0_ffn_Wg, L0_ffn_Wu, L0_ffn_Wd, L0_ffn_Sg, L0_ffn_Su, L0_ffn_Sd, L1_cond_weights, L1_cond_biases, L1_cond_mod_w, L1_cond_mod_b, L1_ffn_W_base, L1_ffn_b_base, L1_ffn_W_gate, L1_ffn_A, L1_ffn_B):
    import jax
    import jax.numpy as jnp

    def _L0_cond_ref(x, style, weights, biases, mod_w, mod_b):
        import jax, jax.numpy as jnp
        from jax import lax
        import numpy as np
        CIN, COUT, K, STYLE_DIM = (32, 32, 3, 64)
        N_LAYERS = 4
        TYPES = ('same', 'upsample', 'same', 'downsample')
        SCALE = 1.0 / float(np.sqrt(CIN * K ** 2))
        EPS = 1e-08
        _BK = np.array([1.0, 3.0, 3.0, 1.0], dtype=np.float32)
        BLUR_K = _BK / _BK.sum()

        def _blur(x, kern, pad):
            B, C, _ = x.shape
            xp = jnp.pad(x, ((0, 0), (0, 0), (pad[0], pad[1])))
            w = jnp.broadcast_to(kern.astype(x.dtype)[None, None, :], (C, 1, kern.shape[0]))
            return lax.conv_general_dilated(xp, w, (1,), 'VALID', feature_group_count=C, dimension_numbers=('NCH', 'OIH', 'NCH'))

        def _conv_same(x, w):
            p = (K - 1) // 2
            return lax.conv_general_dilated(x[None], w, (1,), [(p, p)], dimension_numbers=('NCH', 'OIH', 'NCH'))[0]

        def _conv_down(x, w):
            return lax.conv_general_dilated(x[None], w, (2,), 'VALID', dimension_numbers=('NCH', 'OIH', 'NCH'))[0]

        def _conv_up(x, w_t):
            return lax.conv_transpose(x[None], w_t, (2,), 'VALID', dimension_numbers=('NCH', 'IOH', 'NCH'), transpose_kernel=True)[0]

        def _layer(x, style, w, b, mw, mb, typ):
            s = style @ mw.T + mb
            weight = SCALE * w * s[:, None, :, None]
            demod = lax.rsqrt(jnp.sum(weight * weight, axis=(2, 3)) + EPS)
            weight = weight * demod[:, :, None, None]
            blur_k = jnp.asarray(BLUR_K)
            if typ == 'same':
                out = jax.vmap(_conv_same)(x, weight) + b[None, :, None]
            elif typ == 'upsample':
                out = jax.vmap(_conv_up)(x, weight.transpose(0, 2, 1, 3)) + b[None, :, None]
                out = _blur(out, 2.0 * blur_k, (1, 1))
            elif typ == 'downsample':
                xb = _blur(x, blur_k, (2, 2))
                out = jax.vmap(_conv_down)(xb, weight) + b[None, :, None]
            else:
                raise NotImplementedError(typ)
            return out
        out = x
        for i, typ in enumerate(TYPES):
            out = _layer(out, style, weights[i], biases[i], mod_w[i], mod_b[i], typ)
        return out

    def _L0_ffn_ref(hidden_states, gate_w, bias, Wg, Wu, Wd, Sg, Su, Sd):
        import jax, jax.numpy as jnp
        import numpy as np
        H = 512
        I = 256
        E = 16
        TOPK = 4
        SI = 256
        orig_shape = hidden_states.shape
        x = hidden_states.reshape(-1, orig_shape[-1])
        scores = jax.nn.sigmoid(x @ gate_w.T) + bias
        topk_w, topk_idx = jax.lax.top_k(scores, TOPK)
        topk_w = topk_w / (jnp.sum(topk_w, axis=-1, keepdims=True) + 1e-20)
        cw = jnp.sum(jax.nn.one_hot(topk_idx, E, dtype=x.dtype) * topk_w[..., None], axis=1)
        g = jnp.einsum('th,eih->eti', x, Wg)
        u = jnp.einsum('th,eih->eti', x, Wu)
        z = jax.nn.silu(g) * u
        zw = z * cw.T[:, :, None]
        out = jnp.einsum('eti,ehi->th', zw, Wd)
        out = out + jax.nn.silu(x @ Sg.T) * (x @ Su.T) @ Sd.T
        return out.reshape(orig_shape)

    def _L1_cond_ref(x, style, weights, biases, mod_w, mod_b):
        import jax, jax.numpy as jnp
        from jax import lax
        import numpy as np
        CIN, COUT, K, STYLE_DIM = (32, 32, 3, 64)
        N_LAYERS = 4
        TYPES = ('same', 'upsample', 'same', 'downsample')
        SCALE = 1.0 / float(np.sqrt(CIN * K ** 2))
        EPS = 1e-08
        _BK = np.array([1.0, 3.0, 3.0, 1.0], dtype=np.float32)
        BLUR_K = _BK / _BK.sum()

        def _blur(x, kern, pad):
            B, C, _ = x.shape
            xp = jnp.pad(x, ((0, 0), (0, 0), (pad[0], pad[1])))
            w = jnp.broadcast_to(kern.astype(x.dtype)[None, None, :], (C, 1, kern.shape[0]))
            return lax.conv_general_dilated(xp, w, (1,), 'VALID', feature_group_count=C, dimension_numbers=('NCH', 'OIH', 'NCH'))

        def _conv_same(x, w):
            p = (K - 1) // 2
            return lax.conv_general_dilated(x[None], w, (1,), [(p, p)], dimension_numbers=('NCH', 'OIH', 'NCH'))[0]

        def _conv_down(x, w):
            return lax.conv_general_dilated(x[None], w, (2,), 'VALID', dimension_numbers=('NCH', 'OIH', 'NCH'))[0]

        def _conv_up(x, w_t):
            return lax.conv_transpose(x[None], w_t, (2,), 'VALID', dimension_numbers=('NCH', 'IOH', 'NCH'), transpose_kernel=True)[0]

        def _layer(x, style, w, b, mw, mb, typ):
            s = style @ mw.T + mb
            weight = SCALE * w * s[:, None, :, None]
            demod = lax.rsqrt(jnp.sum(weight * weight, axis=(2, 3)) + EPS)
            weight = weight * demod[:, :, None, None]
            blur_k = jnp.asarray(BLUR_K)
            if typ == 'same':
                out = jax.vmap(_conv_same)(x, weight) + b[None, :, None]
            elif typ == 'upsample':
                out = jax.vmap(_conv_up)(x, weight.transpose(0, 2, 1, 3)) + b[None, :, None]
                out = _blur(out, 2.0 * blur_k, (1, 1))
            elif typ == 'downsample':
                xb = _blur(x, blur_k, (2, 2))
                out = jax.vmap(_conv_down)(xb, weight) + b[None, :, None]
            else:
                raise NotImplementedError(typ)
            return out
        out = x
        for i, typ in enumerate(TYPES):
            out = _layer(out, style, weights[i], biases[i], mod_w[i], mod_b[i], typ)
        return out

    def _L1_ffn_ref(x, W_base, b_base, W_gate, A, B):
        import jax, jax.numpy as jnp
        import numpy as np
        BATCH, TOK, DIM, OUT = (4, 256, 512, 512)
        E, R, TOP_K = (8, 16, 2)
        SCALING = 16.0 / R
        result = jnp.einsum('bnd,od->bno', x, W_base) + b_base
        logits = jnp.einsum('bnd,ed->bne', x, W_gate)
        probs = jax.nn.softmax(logits.astype(jnp.float32), axis=-1)
        top_p, top_i = jax.lax.top_k(probs, TOP_K)
        top_p = top_p / jnp.sum(top_p, axis=-1, keepdims=True)
        top_p = top_p.astype(x.dtype)
        route_w = jnp.sum(jax.nn.one_hot(top_i, E, dtype=x.dtype) * top_p[..., None], axis=-2)
        h = jnp.einsum('bnd,erd->bner', x, A)
        hw = h * route_w[..., None]
        delta = jnp.einsum('bner,eor->bno', hw, B)
        return result + delta * SCALING
    x = x + _L0_ffn_ref(_L0_cond_ref(x, cond_512, L0_cond_weights, L0_cond_biases, L0_cond_mod_w, L0_cond_mod_b), L0_ffn_gate_w, L0_ffn_bias, L0_ffn_Wg, L0_ffn_Wu, L0_ffn_Wd, L0_ffn_Sg, L0_ffn_Su, L0_ffn_Sd)
    x = x + _L1_ffn_ref(_L1_cond_ref(x, cond_512, L1_cond_weights, L1_cond_biases, L1_cond_mod_w, L1_cond_mod_b), L1_ffn_W_base, L1_ffn_b_base, L1_ffn_W_gate, L1_ffn_A, L1_ffn_B)
    return x

_drawn_inputs = setup_inputs


def setup_inputs(seed=0):
    import zlib

    import numpy as np

    out = dict(_drawn_inputs(seed))
    spreads = {'L0_ffn_bias': (0.0, 0.8)}
    factors = {'L0_cond_biases': 5.83,
     'L0_cond_mod_b': 8.0,
     'L0_ffn_gate_w': 7.535,
     'L0_ffn_Wg': 5.825,
     'L0_ffn_Wu': 5.69,
     'L0_ffn_Wd': 5.64,
     'L0_ffn_Sg': 2.962,
     'L0_ffn_Su': 2.86,
     'L0_ffn_Sd': 2.93,
     'L1_ffn_b_base': 55.88,
     'L1_cond_biases': 4.304}
    for name, (base, spread) in spreads.items():
        noise = np.random.default_rng([zlib.crc32(name.encode()), seed]).standard_normal(out[name].shape)
        drawn = base * np.exp(spread * noise) if base else spread * noise
        out[name] = jnp.asarray(drawn.astype(out[name].dtype))
    for name, factor in factors.items():
        out[name] = (out[name] * factor).astype(out[name].dtype)
    return out
```

```python
import numpy as np
from contextlib import ExitStack

import concourse.bass as bass
import concourse.mybir as mybir

P = 128
B, C, L = 64, 32, 512
SPG = P // C
NG = B * C // P
STYLE, LAYERS, TAPS = 64, 4, 3
NTAP = 18
HC = L // P
E0, TOP0, I0 = 16, 4, 256
IC = I0 // P
E1, R1, TOP1 = 8, 16, 2
GU = 2 * I0
PACK = HC * (L + E1 + E1 * R1) + L
DOWN = HC * GU
NPACK = 1 + E0 + 1
TILES = NG * TOP0 + E0
SPARE = TILES * P
ROWS = SPARE + E0 * P
PADDED = L + 2
CONV_SCALE = 1.0 / float(np.sqrt(C * TAPS ** 2))
EPS = 1e-8
BLUR = 0.125

C_ID, C_TRI, C_ONE = 0, P, 2 * P
C_E = 3 * P
C_T = C_E + E0
C_P = C_T + TILES
C_SP = C_P + 1
C_END = C_SP + E0


def build(nc, a, out):
    F, R, I, U = mybir.dt.float32, mybir.dt.float32r, mybir.dt.int32, mybir.dt.uint32
    ALU, ACT, AX = mybir.AluOpType, mybir.ActivationFunctionType, mybir.AxisListType
    ADD, SUB, MUL = ALU.add, ALU.subtract, ALU.mult
    ds = bass.ds

    ctx = ExitStack()
    with ctx:
        top = [nc.sbuf_base]

        def at(name, shape, dt, offset=None):
            size = int(np.prod(shape[1:])) * 4
            if offset is None:
                offset = (top[0] + 31) // 32 * 32
                top[0] = offset + size
            return nc.alloc_sbuf_tensor_at(name, shape, dt, offset=offset), offset

        def new(name, shape, dt=F):
            return at(name, shape, dt)[0]

        taps = [new(f"taps{c}", [P, 2, NTAP, P], R) for c in range(2)]
        in1 = new("in1", [P, 2, 2, PADDED], R)
        in2 = new("in2", [P, 2, 2, PADDED], R)
        in3, in3_at = at("in3", [P, 2, 2, 2, PADDED], R)
        in4, in4_at = at("in4", [P, 2, 2, 2, PADDED], R)
        val = new("val", [P, 2, L])
        xrow = new("xrow", [P, 2, L])
        crow = new("crow", [P, 2, L])
        xT = new("xT", [P, 2, 2, HC, P], R)
        tin, tin_at = at("tin", [P, 2, L], F)
        sg = new("sg", [P, 2, I0])
        z, z_at = at("z", [P, 2, I0], F)
        zT, zT_at = at("zT", [P, 2, 2, IC, P], R)
        ty, ty_at = at("ty", [P, 2, L], F)
        pack, pack_at = at("pack", [P, 2, 2, PACK], R)
        rawp, rawp_at = at("rawp", [P, 2, PACK], F)
        con = new("con", [P, C_END])
        ident = con[:, C_ID:C_ID + P]
        vec = new("vec", [P, 2, 2, LAYERS])
        styl = new("styl", [STYLE, B])
        mod_s = new("mod_s", [P, 2, LAYERS, NG])
        dem = new("dem", [P, 2, LAYERS, NG])
        dtmp = new("dtmp", [P, 2, LAYERS, NG])
        scl = new("scl", [P, 2, LAYERS, NG])
        bia = new("bia", [P, 2, LAYERS, NG])
        edge = new("edge", [P, 2, NG])
        gateF = new("gateF", [P, HC, E0])
        gateT = new("gateT", [P, 2, HC, E0], R)
        gbias = new("gbias", [P, E0])
        tg = new("tg", [P, 2, E0])
        sc = new("sc", [P, 2, E0])
        m8 = new("m8", [P, 2, 8])
        i8 = new("i8", [P, 2, 8], U)
        topv = new("topv", [P, NG, 8])
        topi = new("topi", [P, NG, 8])
        wtok = new("wtok", [P, NG, TOP0])
        slot = new("slot", [P, NG, TOP0], I)
        padi = new("padi", [P, E0], I)
        tabf = new("tabf", [1, 4, TILES])
        tab = new("tab", [1, 4, TILES], I)
        idx = new("idx", [P, 2, TOP0], I)
        bb = new("bb", [P, L])
        lg = new("lg", [P, 2, 64])
        i8b = new("i8b", [P, 2, 8], U)
        zero = new("zero", [P, L])
        o = pack_at
        craw, cf, cu, csq = [], [], [], []
        for c in range(2):
            t_, o_ = at(f"craw{c}", [P, 15, P], F, o); craw.append(t_); o += 15 * P * 4
            t_, o_ = at(f"cf{c}", [P, NTAP, P], F, o); cf.append(t_); o += NTAP * P * 4
            t_, o_ = at(f"cu{c}", [P, 2, 2, TAPS, P], F, o); cu.append(t_); o += 12 * P * 4
            t_, o_ = at(f"csq{c}", [P, 12, P], F, o); csq.append(t_); o += 12 * P * 4
        assert o <= rawp_at + 2 * PACK * 4, (o, rawp_at + 2 * PACK * 4)
        modT, _ = at("modT", [STYLE, 2, LAYERS, SPG, P], F, in3_at)
        o = in3_at
        GE = [P, NG, E0]
        oh = []
        for k in range(TOP0):
            oh.append(at(f"oh{k}", GE, F, o)[0]); o += NG * E0 * 4
        rt = []
        for k in range(9):
            rt.append(at(f"rt{k}", GE, F, o)[0]); o += NG * E0 * 4
        small = [at(f"rs{k}", [P, E0], F, o + k * E0 * 4)[0] for k in range(12)]
        smalli = [at(f"rsi{k}", [P, E0], I, o + (12 + k) * E0 * 4)[0] for k in range(4)]
        o += 16 * E0 * 4
        assert o <= in3_at + 2 * 2 * 2 * PADDED * 4
        cmp_t = at("cmp_t", [1, TILES, E0], F, in4_at)[0]
        res = at("res", [P, 2, L], F, tin_at)[0]
        hw = at("hw", [P, 2, P], F, z_at)[0]
        hwT = at("hwT", [P, 2, 2, P], R, zT_at)[0]
        yo = at("yo", [P, 2, L], F, ty_at)[0]
        gath = at("gath", [P, 2, TOP0 + 1, L], F, rawp_at)[0]
        assert top[0] <= nc.sbuf_usable_end, (top[0], nc.sbuf_usable_end)

        bank = [ctx.enter_context(nc.psum_tensor(f"bank{k}", [P, 512], F)) for k in range(8)]

        xtok = nc.dram_tensor("token_x", (NG * P, L), F).ap()
        ytok = nc.dram_tensor("token_y", (NG * P, L), F).ap()
        xs = nc.dram_tensor("sorted_x", (ROWS, L), F).ap()
        ys = nc.dram_tensor("sorted_y", (TILES * P, L), F).ap()
        x1d = nc.dram_tensor("x1_rows", (NG * P, L), F).ap()

        def hold(eng, semaphore, count):
            eng.wait_ge(semaphore, count)
            eng.nop(nofuse=True)

        def sem(name):
            return ctx.enter_context(nc.semaphore(name))

        s_setup_in = [sem(f"setup_in{k}") for k in range(3)]
        s_const = sem("const_in")
        s_chain = sem("dve_chain")
        s_pchain = sem("pool_chain")
        s_sty = sem("style_sums")
        s_sq = sem("style_squares")
        s_dsum = sem("demod_sums")
        s_dvar = sem("demod_var")
        s_root = sem("demod_root")
        s_scales = sem("scales_ready")
        s_taps = [sem(f"taps_ready{c}") for c in range(2)]
        s_pads = sem("pads_zeroed")
        s_x = [[sem(f"x_loaded{c}{u}") for u in range(2)] for c in range(2)]
        s_val = [sem(f"val_ready{c}") for c in range(2)]
        s_hi = [sem(f"high_part{c}") for c in range(2)]
        s_split = [sem(f"split_done{c}") for c in range(2)]
        s_conv = [sem(f"conv_bank{c}") for c in range(2)]
        s_crow = [sem(f"crow_ready{c}") for c in range(2)]
        s_xt = [sem(f"xt_bank{c}") for c in range(2)]
        s_xth = [sem(f"xt_high{c}") for c in range(2)]
        s_xtl = [sem(f"xt_low{c}") for c in range(2)]
        s_gate = [sem(f"gate_sums{c}") for c in range(2)]
        s_tanh = sem("gate_tanh")
        s_saved = [sem(f"crow_saved{u}") for u in range(2)]
        s_hot = sem("one_hots")
        s_cnt = sem("counts")
        s_route = sem("routing_ready")
        s_pool_in = [sem(f"scatter_rows_in{u}") for u in range(2)]
        s_idx = sem("index_columns")
        s_scat = sem("scattered")
        s_zero = sem("zero_rows")
        s_raw = [sem(f"raw_pack_in{u}") for u in range(2)]
        s_pk_hi = [sem(f"pack_high{u}") for u in range(2)]
        s_pk = sem("pack_ready")
        s_tx = [sem(f"tile_in{u}") for u in range(2)]
        s_txt = sem("tile_xt")
        s_txh = sem("tile_xt_high")
        s_txl = sem("tile_xt_low")
        s_tup = sem("tile_up")
        s_tsg = sem("tile_silu")
        s_tz = sem("tile_z")
        s_tzt = sem("tile_zt")
        s_tzh = sem("tile_zt_high")
        s_tzl = sem("tile_zt_low")
        s_tdn = sem("tile_down")
        s_ty = sem("tile_y")
        s_tys = [sem(f"tile_saved{u}") for u in range(2)]
        s_gsh = [sem(f"shared_rows_in{u}") for u in range(2)]
        s_gat = [sem(f"gathered{u}") for u in range(2)]
        s_comb = sem("combined")
        s_x1s = [sem(f"x1_saved{u}") for u in range(2)]
        s_res = [sem(f"residual_in{u}") for u in range(2)]
        s_lmax = sem("logit_max")
        s_exp = sem("logit_exp")
        s_rw = sem("low_rank_weighted")
        s_ht = sem("low_rank_transposed")
        s_hth = sem("low_rank_high")
        s_htl = sem("low_rank_low")
        s_sum = sem("layer1_sums")
        s_fin = sem("out_rows")
        s_out = [sem(f"out_saved{u}") for u in range(2)]

        block = ctx.enter_context(nc.Block())

        NB = NG // 2
        BANKS = 12
        CREDIT = 2

        def body_loop(eng, body, first=0):
            with eng.Fori(first, NB - 1) as i:
                body(i, False)
            body(NB - 1, True)

        @block.sync
        def _(sp):
            sp.dma_start(con[:, :], a["consts"]).then_inc(s_const, 16)
            sp.dma_start(styl[:, :], a["style_t"]).then_inc(s_setup_in[0], 16)
            sp.dma_start(modT[:, :, :, :, :], a["mod_t"]).then_inc(s_setup_in[0], 16)
            sp.dma_start(vec[:, :, :, :], a["vecs"]).then_inc(s_setup_in[0], 16)
            sp.dma_start(craw[0][:, :, :], a["conv0"]).then_inc(s_setup_in[1], 16)
            sp.dma_start(craw[1][:, :, :], a["conv1"]).then_inc(s_setup_in[2], 16)
            sp.dma_start(gateF[:, :, :], a["gate_t"]).then_inc(s_const, 16)
            sp.dma_start(gbias[:, :], a["gate_bias"]).then_inc(s_const, 16)
            sp.dma_start(bb[:, :], a["base_bias"]).then_inc(s_const, 16)
            for g in range(2):
                sp.dma_start(xrow[:, g, :], a["x"][g]).then_inc(s_x[0][g], 16)
            for u in range(2):
                sp.sem_inc(s_saved[u], 16)

            def chain0(i, last):
                if not last:
                    for u in range(2):
                        sp.wait_ge(s_val[0], BANKS * i + 1 + u)
                        sp.dma_start(xrow[:, u, :], a["x"][ds(2 * i + 2 + u, 1), :, :].rearrange("a p l -> p (a l)"))\
                          .then_inc(s_x[0][u], 16)
                for u in range(2):
                    sp.wait_ge(s_crow[0], 2 * i + u + 1)
                    sp.dma_start(xtok[ds((2 * i + u) * P, P), :], crow[:, u, :]).then_inc(s_saved[u], 16)

            body_loop(sp, chain0)
            for u in range(2):
                sp.wait_ge(s_saved[u], 16 * (NB + 1))

            def load(h, u, src, row, free=True):
                if free:
                    sp.wait_ge(s_txt, 2 * h + u - 1)
                sp.dma_start(tin[:, u, :], src[ds(row, P), :]).then_inc(s_tx[u], 16)

            for u in range(2):
                load(0, u, xtok, u * P, free=False)
            with sp.Fori(0, NG // 2 - 1) as i:
                for u in range(2):
                    load(i + 1, u, xtok, (2 * i + 2 + u) * P)
            sp.wait_ge(s_route, 1)
            sp.wait_ge(s_scat, 16 * (NG * TOP0 + E0))

            def block_of(t):
                return sp.value_load(tab[0:1, 2, ds(t, 1)], min_val=0, max_val=(TILES - 1) * P)

            for u in range(2):
                load(NG // 2, u, xs, block_of(u))
            with sp.Fori(0, TILES // 2 - 1) as i:
                for u in range(2):
                    load(NG // 2 + i + 1, u, xs, block_of(2 * i + 2 + u))
            for u in range(2):
                sp.wait_ge(s_tys[u], 16 * ((NG + TILES) // 2 + 1))

            sp.wait_ge(s_pk, NPACK)

            def load1(g, u):
                sp.dma_start(xrow[:, u, :], a["x"][ds(g, 1), :, :].rearrange("a p l -> p (a l)"))\
                  .then_inc(s_x[1][u], 16)
                sp.dma_start(gath[:, u, TOP0, :], ytok[ds(g * P, P), :]).then_inc(s_gsh[u], 16)

            def keep_x1(g, u):
                sp.wait_ge(s_comb, g + 1)
                sp.dma_start(x1d[ds(g * P, P), :], xrow[:, u, :]).then_inc(s_x1s[u], 16)

            for u in range(2):
                load1(u, u)
            for u in range(2):
                keep_x1(u, u)
            for u in range(2):
                sp.sem_inc(s_out[u], 16)

            def chain1(i, last):
                for u in range(2):
                    hold(sp, s_x1s[u], 16 * i + 16)
                    sp.wait_ge(s_fin, 2 * i + u + 1)
                    sp.dma_start(res[:, u, :], x1d[ds((2 * i + u) * P, P), :]).then_inc(s_res[u], 16)
                if not last:
                    for u in range(2):
                        sp.wait_ge(s_val[1], BANKS * i + 1 + u)
                        load1(2 * i + 2 + u, u)
                    for u in range(2):
                        keep_x1(2 * i + 2 + u, u)
                for u in range(2):
                    sp.wait_ge(s_fin, 2 * i + u + 1 + CREDIT)
                    sp.dma_start(out[ds((2 * i + u) * P, P), :], yo[:, u, :]).then_inc(s_out[u], 16)

            body_loop(sp, chain1)
            for u in range(2):
                sp.wait_ge(s_out[u], 16 * (NB + 1))

        def chain_scalar(act, c):
            def body(i, last):
                k = 0
                for layer, u, h in ([(0, 0, 0), (0, 1, 0)] + [(1, u, h) for u in range(2) for h in range(2)]
                                    + [(2, u, h) for u in range(2) for h in range(2)]):
                    g = 2 * i + u
                    k += 1
                    b = bank[BANK_OF[layer][u][h]]
                    act.wait_ge(s_split[c], BANKS * i + k)
                    hold(act, s_conv[c], BANKS * i + k)
                    v = val[:, (k + 1) % 2, :]
                    s_, b_ = scl[:, c, layer, ds(g, 1)], bia[:, c, layer, ds(g, 1)]
                    if layer == 1:
                        one, rest = (0, slice(1, L)) if h == 0 else (L - 1, slice(0, L - 1))
                        act.activation(v[:, one:one + 1], b[:, one:one + 1], ACT.Identity, scale=s_,
                                       bias=edge[:, c, ds(g, 1)])
                        act.activation(v[:, rest], b[:, rest], ACT.Identity, scale=s_, bias=b_)\
                           .then_inc(s_val[c], 1)
                    else:
                        act.activation(v, b[:, :], ACT.Identity, scale=s_, bias=b_).then_inc(s_val[c], 1)
                if not last:
                    for u in range(2):
                        k += 1
                        act.wait_ge(s_split[c], BANKS * i + k)
                        act.wait_ge(s_x[c][u], 16 * i + 32)
                        if c == 1:
                            act.wait_ge(s_comb, 2 * i + 3 + u)
                        act.activation(val[:, (k + 1) % 2, :], xrow[:, u, :], ACT.Copy,
                                       scale=mod_s[:, c, 0, ds(2 * i + 2 + u, 1)]).then_inc(s_val[c], 1)
                for u in range(2):
                    if c == 0:
                        act.wait_ge(s_saved[u], 16 * i + 16)
                    hold(act, s_conv[c], BANKS * i + 11 + u)
                    act.activation(crow[:, u, :], bank[BANK_OF[3][u][0]][:, :], ACT.Identity,
                                   scale=scl[:, c, 3, ds(2 * i + u, 1)], bias=vec[:, c, 1, 3:4])\
                       .then_inc(s_crow[c], 1)
                for u in range(2):
                    act.wait_ge(s_xt[c], 2 * i + u + 1)
                    act.activation(xT[:, u, 0, :, :].rearrange("p c t -> p (c t)"), bank[6 + u][:, :], ACT.Copy)\
                       .then_inc(s_xth[c], 1)

            for u in range(2):
                act.wait_ge(s_x[c][u], 16)
                if c == 1:
                    act.wait_ge(s_comb, u + 1)
                act.activation(val[:, u, :], xrow[:, u, :], ACT.Copy, scale=mod_s[:, c, 0, u:u + 1])\
                   .then_inc(s_val[c], 1)
            return body

        BANK_OF = {0: [[0], [1]], 1: [[2, 3], [4, 5]], 2: [[0, 1], [2, 3]], 3: [[4], [5]]}

        def split(dve, c, n, slot_, dst):
            dve.wait_ge(s_val[c], n)
            dve.tensor_copy(dst(0), val[:, slot_, :]).then_inc(s_hi[c], 1)
            dve.wait_ge(s_hi[c], n)
            dve.tensor_tensor(dst(1), val[:, slot_, :], dst(0).bitcast(F), SUB).then_inc(s_split[c], 1)

        def chain_vector(dve, c):
            def dst1(u):
                return lambda p: in1[:, u, p, 1:L + 1]

            def body(i, last, middle=None):
                k = 0
                for dst in ([(lambda p, u=u: in2[:, u, p, 1:L + 1]) for u in range(2)]
                            + [(lambda p, u=u, h=h: in3[:, u, h, p, 1:L + 1]) for u in range(2) for h in range(2)]
                            + [(lambda p, u=u, h=h: in4[:, u, h, p, 1:L + 1]) for u in range(2) for h in range(2)]):
                    k += 1
                    split(dve, c, BANKS * i + k + 2, (k + 1) % 2, dst)
                if not last:
                    if middle:
                        middle(i)
                    for u in range(2):
                        k += 1
                        split(dve, c, BANKS * i + k + 2, (k + 1) % 2, dst1(u))
                for u in range(2):
                    dve.wait_ge(s_xth[c], 2 * i + u + 1)
                    dve.tensor_tensor(xT[:, u, 1, :, :].rearrange("p c t -> p (c t)"), bank[6 + u][:, :],
                                      xT[:, u, 0, :, :].rearrange("p c t -> p (c t)").bitcast(F), SUB)\
                       .then_inc(s_xtl[c], 1)

            for u in range(2):
                split(dve, c, u + 1, u, dst1(u))
            return body

        PARTS = ((0, 0), (0, 1), (1, 0))

        def products(pe, dst, terms, start=True, stop=True):
            n = len(terms) * len(PARTS)
            k = 0
            for lhs, rhs in terms:
                for p, q in PARTS:
                    mm = pe.matmul(dst, lhs(p), rhs(q), start=start and k == 0, stop=stop and k == n - 1)
                    k += 1
            return mm

        def chain_tensor(pe, c):
            def tap(n):
                return lambda p: taps[c][:, p, n, :]

            def body(i, last):
                for u in range(2):
                    if c == 1:
                        pe.wait_ge(s_fin, 2 * i + u + 1)
                    pe.wait_ge(s_split[c], BANKS * i + 1 + u)
                    products(pe, bank[BANK_OF[0][u][0]][:, :],
                             [(tap(k), lambda p, u=u, k=k: in1[:, u, p, k:k + L]) for k in range(TAPS)])\
                        .then_inc(s_conv[c], 1)
                for u in range(2):
                    pe.wait_ge(s_split[c], BANKS * i + 3 + u)
                    for h in range(2):
                        products(pe, bank[BANK_OF[1][u][h]][:, :],
                                 [(tap(3 + 4 - 2 * k + h), lambda p, u=u, k=k: in2[:, u, p, k:k + L])
                                  for k in range(TAPS)]).then_inc(s_conv[c], 1)
                for u in range(2):
                    pe.wait_ge(s_split[c], BANKS * i + 6 + 2 * u)
                    for h, where in ((0, ((1, 0), (0, 1), (1, 1))), (1, ((0, 1), (1, 1), (0, 2)))):
                        products(pe, bank[BANK_OF[2][u][h]][:, :],
                                 [(tap(9 + k), lambda p, u=u, s=s, q=q: in3[:, u, s, p, q:q + L])
                                  for k, (s, q) in enumerate(where)]).then_inc(s_conv[c], 1)
                for u in range(2):
                    pe.wait_ge(s_split[c], BANKS * i + 10 + 2 * u)
                    products(pe, bank[BANK_OF[3][u][0]][:, :],
                             [(tap(12 + r), lambda p, u=u, r=r: in4[:, u, r % 2, p, r // 2:r // 2 + L])
                              for r in range(6)]).then_inc(s_conv[c], 1)
                for u in range(2):
                    pe.wait_ge(s_crow[c], 2 * i + u + 1)
                    for j in range(HC):
                        mm = pe.transpose(bank[6 + u][:, j * P:(j + 1) * P], crow[:, u, j * P:(j + 1) * P], ident)
                    mm.then_inc(s_xt[c], 1)
            return body

        def XT(u):
            return [(lambda p, j=j: xT[:, u, p, j, :]) for j in range(HC)]

        @block.scalar
        def _(act):
            act.wait_ge(s_dvar, 1)
            act.activation(dtmp[:, :, :, :], dem[:, :, :, :], ACT.Sqrt).then_inc(s_root, 1)
            act.wait_ge(s_scales, 1)
            body = chain_scalar(act, 0)

            def body0(i, last):
                body(i, last)
                for u in range(2):
                    act.wait_ge(s_gate[0], 2 * i + u + 1)
                    act.activation(tg[:, u, :], bank[4 + u][:, 0:E0], ACT.Tanh, scale=0.5).then_inc(s_tanh, 1)

            body_loop(act, body0)

            act.sem_inc(s_ty, CREDIT)

            def xt_high(h, u):
                act.wait_ge(s_txt, 2 * h + u + 1)
                act.activation(xT[:, u, 0, :, :].rearrange("p c t -> p (c t)"), bank[6 + u][:, :], ACT.Copy)\
                   .then_inc(s_txh, 1)

            def zt_high(h, u):
                act.wait_ge(s_tzt, 2 * h + u + 1)
                act.activation(zT[:, u, 0, :, :].rearrange("p c t -> p (c t)"), bank[2 + u][:, 0:I0], ACT.Copy)\
                   .then_inc(s_tzh, 1)

            def silu(h, u):
                act.wait_ge(s_tup, 2 * h + u + 1)
                act.activation(sg[:, u, :], bank[u][:, 0:I0], ACT.Silu).then_inc(s_tsg, 1)

            def rows(h, u):
                act.wait_ge(s_tdn, 2 * h + u + 1)
                act.wait_ge(s_tys[u], 16 * h + 16)
                act.activation(ty[:, u, :], bank[4 + u][:, :], ACT.Copy).then_inc(s_ty, 1)

            for u in range(2):
                act.sem_inc(s_tys[u], 16)

            def save(h, u, dst, k):
                hold(act, s_ty, 2 * h + u + 1 + CREDIT)
                act.dma_start(dst[ds(k * P, P), :], ty[:, u, :]).then_inc(s_tys[u], 16)

            def tiles(h0, n, dst):
                xt_high(h0, 0)
                xt_high(h0, 1)
                silu(h0, 0)
                with act.Fori(0, n - 1) as i:
                    h = h0 + i
                    xt_high(h + 1, 0)
                    zt_high(h, 0)
                    silu(h, 1)
                    rows(h, 0)
                    xt_high(h + 1, 1)
                    save(h, 0, dst, 2 * i)
                    zt_high(h, 1)
                    silu(h + 1, 0)
                    rows(h, 1)
                    save(h, 1, dst, 2 * i + 1)
                h = h0 + n - 1
                zt_high(h, 0)
                silu(h, 1)
                rows(h, 0)
                save(h, 0, dst, 2 * n - 2)
                zt_high(h, 1)
                rows(h, 1)
                save(h, 1, dst, 2 * n - 1)

            tiles(0, NG // 2, ytok)
            tiles(NG // 2, TILES // 2, ys)

            body1_ = chain_scalar(act, 1)

            def body1(i, last):
                body1_(i, last)
                for u in range(2):
                    act.wait_ge(s_lmax, 2 * i + u + 1)
                    act.activation(lg[:, u, 8:16], bank[2 + u][:, 0:E1], ACT.Exp, bias=lg[:, u, 1:2],
                                   accum_out=lg[:, u, 2:3]).then_inc(s_exp, 1)
                for u in range(2):
                    act.wait_ge(s_ht, 2 * i + u + 1)
                    act.activation(hwT[:, u, 0, :], bank[4 + u][:, 0:P], ACT.Copy).then_inc(s_hth, 1)

            body_loop(act, body1)

        @block.tensor
        def _(pe):
            pe.wait_ge(s_setup_in[0], 48)
            sview = styl[:, :].rearrange("k (g b) -> k b g", b=SPG)
            for c in range(2):
                for layer in range(LAYERS):
                    for b in range(SPG):
                        mm = pe.matmul(bank[0][:, (c * LAYERS + layer) * NG:(c * LAYERS + layer + 1) * NG],
                                       modT[:, c, layer, b, :], sview[:, b, :], start=b == 0, stop=b == SPG - 1)
            mm.then_inc(s_sty, 1)
            pe.wait_ge(s_sq, 1)
            for c in range(2):
                for layer in range(LAYERS):
                    n = (c * LAYERS + layer) * NG
                    mm = pe.matmul(bank[1][:, n:n + NG], csq[c][:, layer, :], dtmp[:, c, layer, :],
                                   start=True, stop=True)
            mm.then_inc(s_dsum, 1)

            body = chain_tensor(pe, 0)
            pe.wait_ge(s_taps[0], 1)
            pe.wait_ge(s_pads, 1)
            pe.wait_ge(s_const, 64)

            def body0(i, last):
                body(i, last)
                for u in range(2):
                    pe.wait_ge(s_xtl[0], 2 * i + u + 1)
                    products(pe, bank[4 + u][:, 0:E0],
                             [(x, lambda p, j=j: gateT[:, p, j, :]) for j, x in enumerate(XT(u))])\
                        .then_inc(s_gate[0], 1)

            body_loop(pe, body0)

            pe.wait_ge(s_hot, 1)
            hot = rt[0][:, :, :].rearrange("p g e -> p (g e)")
            pe.matmul(bank[0][:, 0:NG * E0], con[:, C_TRI:C_TRI + P], hot, start=True, stop=True)
            pe.matmul(bank[1][:, 0:NG * E0], con[:, C_ONE:C_ONE + P], hot, start=True, stop=True).then_inc(s_cnt, 1)

            def turn(h, u):
                pe.wait_ge(s_tx[u], 16 * h + 16)
                for j in range(HC):
                    mm = pe.transpose(bank[6 + u][:, j * P:(j + 1) * P], tin[:, u, j * P:(j + 1) * P], ident)
                mm.then_inc(s_txt, 1)

            def up(h, u, package, half):
                ready, where = package
                if half == 0:
                    hold(pe, s_pk, ready)
                    pe.wait_ge(s_txl, 2 * h + u + 1)
                js = range(HC // 2) if half == 0 else range(HC // 2, HC)
                mm = products(pe, bank[u][:, :],
                              [(XT(u)[j], lambda p, j=j: where(p, j * GU)) for j in js],
                              start=half == 0, stop=half == 1)
                if half == 1:
                    mm.then_inc(s_tup, 1)

            def turn_z(h, u):
                pe.wait_ge(s_tz, 2 * h + u + 1)
                for j in range(IC):
                    mm = pe.transpose(bank[2 + u][:, j * P:(j + 1) * P], z[:, u, j * P:(j + 1) * P], ident)
                mm.then_inc(s_tzt, 1)

            def down(h, u, package):
                where = package[1]
                pe.wait_ge(s_tzl, 2 * h + u + 1)
                pe.wait_ge(s_ty, 2 * h + u + 1)
                products(pe, bank[4 + u][:, :],
                         [(lambda p, j=j: zT[:, u, p, j, :], lambda p, j=j: where(p, DOWN + j * L))
                          for j in range(IC)]).then_inc(s_tdn, 1)

            def tiles(h0, n, package):
                turn(h0, 0)
                turn(h0, 1)
                w0 = package(0)
                up(h0, 0, w0, 0)
                up(h0, 0, w0, 1)
                with pe.Fori(0, n - 1) as i:
                    h = h0 + i
                    w0, w1, w2 = package(2 * i), package(2 * i + 1), package(2 * i + 2)
                    turn(h + 1, 0)
                    up(h, 1, w1, 0)
                    turn_z(h, 0)
                    up(h, 1, w1, 1)
                    down(h, 0, w0)
                    turn(h + 1, 1)
                    up(h + 1, 0, w2, 0)
                    turn_z(h, 1)
                    up(h + 1, 0, w2, 1)
                    down(h, 1, w1)
                h = h0 + n - 1
                w0, w1 = package(2 * n - 2), package(2 * n - 1)
                up(h, 1, w1, 0)
                turn_z(h, 0)
                up(h, 1, w1, 1)
                down(h, 0, w0)
                turn_z(h, 1)
                down(h, 1, w1)

            tiles(0, NG // 2, lambda k: (1, lambda p, n: pack[:, 0, p, n:n + 512]))

            pe.wait_ge(s_route, 1)
            flat = pack[:, :, :, :].rearrange("p s h n -> p (s h n)")

            def chosen(k):
                ready = pe.value_load(tab[0:1, 0, ds(k, 1)], min_val=2, max_val=NPACK)
                off = pe.value_load(tab[0:1, 1, ds(k, 1)], min_val=0, max_val=2 * PACK)
                return ready, lambda p, n: flat[:, ds(off + (p * PACK + n), 512)]

            tiles(NG // 2, TILES // 2, chosen)

            body_ = chain_tensor(pe, 1)
            pe.wait_ge(s_taps[1], 1)
            pe.wait_ge(s_pads, 2)
            pe.wait_ge(s_pk, NPACK)
            W1 = (NPACK - 1) % 2
            NA = E1 + E1 * R1

            def body1(i, last):
                body_(i, last)
                for u in range(2):
                    pe.wait_ge(s_xtl[1], 2 * i + u + 1)
                    products(pe, bank[2 + u][:, 0:NA],
                             [(x, lambda p, j=j: pack[:, W1, p, HC * L + j * NA:HC * L + (j + 1) * NA])
                              for j, x in enumerate(XT(u))]).then_inc(s_gate[1], 1)
                for u in range(2):
                    products(pe, bank[u][:, :],
                             [(x, lambda p, j=j: pack[:, W1, p, j * L:(j + 1) * L])
                              for j, x in enumerate(XT(u))], stop=False)
                for u in range(2):
                    pe.wait_ge(s_rw, 2 * i + u + 1)
                    pe.transpose(bank[4 + u][:, 0:P], hw[:, u, :], ident).then_inc(s_ht, 1)
                for u in range(2):
                    pe.wait_ge(s_htl, 2 * i + u + 1)
                    products(pe, bank[u][:, :],
                             [(lambda p, u=u: hwT[:, u, p, :], lambda p: pack[:, W1, p, HC * (L + NA):HC * (L + NA) + L])],
                             start=False).then_inc(s_sum, 1)

            body_loop(pe, body1)

        def build_taps(eng, c, link):
            w, f, u_ = craw[c], cf[c], cu[c]
            link(eng.tensor_scalar(w[:, :, :], w[:, :, :], CONV_SCALE, None, MUL))
            eng.tensor_copy(f[:, 0:3, :], w[:, 0:3, :])
            eng.tensor_copy(f[:, 9:12, :], w[:, 6:9, :])
            for n, (lay, gain) in enumerate(((1, 2 * BLUR), (3, BLUR))):
                link(eng.tensor_scalar(u_[:, n, 0, :, :], w[:, 3 * lay:3 * lay + 3, :], gain, None, MUL))
                link(eng.tensor_scalar(u_[:, n, 1, :, :], w[:, 3 * lay:3 * lay + 3, :], 3 * gain, None, MUL))
            for n, base in enumerate((3, 12)):
                one, three = u_[:, n, 0, :, :], u_[:, n, 1, :, :]
                t = [f[:, base + r, :] for r in range(6)]
                eng.tensor_copy(t[0], one[:, 0, :])
                eng.tensor_copy(t[5], one[:, 2, :])
                eng.tensor_tensor(t[1], three[:, 0, :], one[:, 1, :], ADD)
                eng.tensor_tensor(t[4], one[:, 1, :], three[:, 2, :], ADD)
                eng.tensor_tensor(t[2], three[:, 0, :], three[:, 1, :], ADD)
                link(eng.tensor_tensor(t[3], three[:, 1, :], three[:, 2, :], ADD))
                link(eng.tensor_tensor(t[2], t[2], one[:, 2, :], ADD))
                link(eng.tensor_tensor(t[3], t[3], one[:, 0, :], ADD))
            link(eng.tensor_copy(taps[c][:, 0, :, :], f[:, :, :]))
            eng.tensor_tensor(taps[c][:, 1, :, :], f[:, :, :], taps[c][:, 0, :, :].bitcast(F), SUB)\
               .then_inc(s_taps[c], 1)

        @block.vector
        def _(dve):
            count = [0]

            def link(ins):
                count[0] += 1
                ins.then_inc(s_chain, 1)
                dve.wait_ge(s_chain, count[0])

            tt, ts = dve.tensor_tensor, dve.tensor_scalar

            def clear_pads():
                for t_ in (in1, in2):
                    v = t_[:, :, :, :].rearrange("p u h n -> p (u h) n")
                    for n in (0, L + 1):
                        dve.memset(v[:, :, n:n + 1].bitcast(F), 0.0)
                for t_ in (in3, in4):
                    v = t_[:, :, :, :, :].rearrange("p u s h n -> p (u s h) n")
                    for n in (0, L + 1):
                        link(dve.memset(v[:, :, n:n + 1].bitcast(F), 0.0))

            for c in range(2):
                dve.wait_ge(s_setup_in[1 + c], 16)
                w, q = craw[c], csq[c]
                for lay, src in ((0, 0), (1, 12), (2, 6), (3, 9)):
                    for k in range(3):
                        ins = dve.scalar_tensor_tensor(out=q[:, 3 * lay + k, :], in0=w[:, src + k, :],
                                                       scalar=CONV_SCALE * CONV_SCALE, in1=w[:, src + k, :],
                                                       op0=MUL, op1=MUL)
                link(ins)
                qv = q[:, :, :].rearrange("p (l k) n -> p l k n", k=3)
                link(tt(qv[:, :, 0, :], qv[:, :, 0, :], qv[:, :, 1, :], ADD))
                link(tt(qv[:, :, 0, :], qv[:, :, 0, :], qv[:, :, 2, :], ADD))
                for lay in range(1, LAYERS):
                    link(dve.tensor_copy(q[:, lay, :], q[:, 3 * lay, :]))
            dve.wait_ge(s_sty, 1)
            dve.wait_ge(s_setup_in[0], 48)
            for c in range(2):
                for lay in range(LAYERS):
                    n = (c * LAYERS + lay) * NG
                    ins = ts(mod_s[:, c, lay, :], bank[0][:, n:n + NG], vec[:, c, 0, lay:lay + 1], None, ADD)
            link(ins)
            tt(dtmp[:, :, :, :], mod_s[:, :, :, :], mod_s[:, :, :, :], MUL).then_inc(s_sq, 1)
            dsum = dem[:, :, :, :].rearrange("p c l g -> p (c l g)")
            dve.wait_ge(s_dsum, 1)
            ts(dsum, bank[1][:, 0:2 * LAYERS * NG], EPS, None, ADD).then_inc(s_dvar, 1)
            dve.wait_ge(s_dvar, 1)
            dve.wait_ge(s_root, 1)
            root = dtmp[:, :, :, :].rearrange("p c l g -> p (c l g)")
            r2 = scl[:, :, :, :].rearrange("p c l g -> p (c l g)")
            link(dve.reciprocal(root, root))
            link(tt(r2, root, root, MUL))
            link(tt(r2, r2, dsum, MUL))
            link(ts(r2, r2, -0.5, 1.5, MUL, ADD))
            link(tt(dsum, r2, root, MUL))
            for c in range(2):
                into = [mod_s[:, c, 0, :], dem[:, c, 1, :], mod_s[:, c, 2, :], mod_s[:, c, 3, :]]
                outof = [dem[:, c, 0, :], mod_s[:, c, 1, :], dem[:, c, 2, :], dem[:, c, 3, :]]
                for lay in range(LAYERS - 1):
                    tt(scl[:, c, lay, :], outof[lay], into[lay + 1], MUL)
                    link(ts(bia[:, c, lay, :], into[lay + 1], vec[:, c, 1, lay:lay + 1],
                            2.0 if lay == 1 else 1.0, MUL, MUL))
                dve.tensor_copy(scl[:, c, 3, :], outof[3])
                link(ts(edge[:, c, :], bia[:, c, 1, :], 1.75 / 2.0, None, MUL))
            dve.wait_ge(s_const, 64)
            link(dve.tensor_copy(gateT[:, 0, :, :], gateF[:, :, :]))
            link(tt(gateT[:, 1, :, :], gateF[:, :, :], gateT[:, 0, :, :].bitcast(F), SUB))
            clear_pads()
            dve.memset(zero[:, :], 0.0).then_inc(s_zero, 1)
            dve.wait_ge(s_zero, 1)
            build_taps(dve, 0, link)
            dve.wait_ge(s_taps[0], 1)
            dve.tensor_copy(tg[:, 0, 0:1], zero[:, 0:1]).then_inc(s_scales, 1)
            dve.wait_ge(s_scales, 1)
            dve.tensor_copy(tg[:, 0, 0:1], zero[:, 0:1]).then_inc(s_pads, 1)

            body = chain_vector(dve, 0)
            STEPS = 8
            start = count[0]

            def body0(i, last):
                body(i, last)
                k = 0

                def step(ins):
                    nonlocal k
                    k += 1
                    ins.then_inc(s_chain, 1)
                    hold(dve, s_chain, start + STEPS * i + k)

                for u in range(2):
                    g = 2 * i + u
                    dve.wait_ge(s_tanh, g + 1)
                    step(ts(sc[:, u, :], tg[:, u, :], 0.5, 0.5, MUL, ADD))
                    step(tt(sc[:, u, :], sc[:, u, :], gbias[:, :], ADD))
                    step(dve.max(m8[:, u, :], sc[:, u, :]))
                    step(dve.max_index(i8[:, u, :], m8[:, u, :], sc[:, u, :]))
                    dve.tensor_copy(topv[:, ds(g, 1), :].rearrange("p a k -> p (a k)"), m8[:, u, :])
                    dve.tensor_copy(topi[:, ds(g, 1), :].rearrange("p a k -> p (a k)"), i8[:, u, :])

            body_loop(dve, body0)
            count[0] = start + STEPS * NB

            link(dve.tensor_copy(rt[8][:, :, :], con[:, C_E:C_E + E0].rearrange("p (a e) -> p a e", a=1)
                                 .broadcast_to([P, NG, E0])))
            den = small[0][:, :]
            link(dve.tensor_reduce(den, topv[:, :, 0:TOP0], AX.X, ADD))
            link(ts(den, den, 1e-20, None, ADD))
            link(dve.reciprocal(den, den))
            for k in range(TOP0):
                tt(wtok[:, :, k], topv[:, :, k], den, MUL)
                link(tt(oh[k][:, :, :], rt[8][:, :, :], topi[:, :, k:k + 1].broadcast_to([P, NG, E0]), ALU.is_equal))
            M, base, S, tmp, cnt, alt = rt[0], rt[1], rt[2], rt[3], rt[4], rt[5]
            link(tt(M[:, :, :], oh[0][:, :, :], oh[1][:, :, :], ADD))
            link(tt(M[:, :, :], M[:, :, :], oh[2][:, :, :], ADD))
            tt(M[:, :, :], M[:, :, :], oh[3][:, :, :], ADD).then_inc(s_hot, 1)
            dve.wait_ge(s_cnt, 1)
            link(dve.tensor_copy(cnt[:, :, :].rearrange("p g e -> p (g e)"), bank[1][:, 0:NG * E0]))
            src, dst, d = cnt, base, 1
            while d < NG:
                dve.tensor_copy(dst[:, 0:d, :], src[:, 0:d, :])
                link(tt(dst[:, d:NG, :], src[:, d:NG, :], src[:, 0:NG - d, :], ADD))
                src, dst, d = dst, (alt if src is cnt else src), 2 * d
            incl = src
            total = small[1][:, :]
            link(dve.tensor_copy(total, incl[:, NG - 1, :]))
            link(tt(S[:, :, :], incl[:, :, :], cnt[:, :, :], SUB))
            link(tt(S[:, :, :].rearrange("p g e -> p (g e)"), S[:, :, :].rearrange("p g e -> p (g e)"),
                    bank[0][:, 0:NG * E0], ADD))
            tiles_i, tiles_f = smalli[0][:, :], small[2][:, :]
            link(ts(small[3][:, :], total, float(P - 1), None, ADD))
            link(dve.tensor_copy(tiles_i, small[3][:, :]))
            link(ts(smalli[1][:, :], tiles_i, 7, None, ALU.logical_shift_right))
            link(dve.tensor_copy(tiles_f, smalli[1][:, :]))
            link(ts(tiles_f, tiles_f, 1.0, None, ALU.max))
            src, dst, d = small[2], small[4], 1
            while d < E0:
                dve.tensor_copy(dst[:, 0:d], src[:, 0:d])
                link(tt(dst[:, d:E0], src[:, d:E0], src[:, 0:E0 - d], ADD))
                src, dst, d = dst, (small[5] if src is small[2] else src), 2 * d
            ends = src
            starts = small[6]
            link(tt(starts[:, :], ends[:, :], tiles_f, SUB))
            first_row = small[7]
            link(ts(first_row[:, :], starts[:, :], float(P), None, MUL))
            link(tt(S[:, :, :], S[:, :, :], first_row[:, :].rearrange("p (a e) -> p a e", a=1)
                    .broadcast_to([P, NG, E0]), ADD))
            for k in range(TOP0):
                link(tt(tmp[:, :, :], oh[k][:, :, :], S[:, :, :], MUL))
                link(dve.tensor_reduce(small[8][:, :], tmp[:, :, :], AX.X, ADD))
                link(dve.tensor_copy(slot[:, :, k], small[8][:, :]))
            link(ts(small[8][:, :], total, con[:, C_P:C_P + 1], None, ADD))
            link(ts(small[9][:, :], tiles_f, float(P), None, MUL))
            link(tt(small[10][:, :], small[8][:, :], small[9][:, :], ALU.is_lt))
            link(tt(small[8][:, :], small[8][:, :], first_row[:, :], ADD))
            link(tt(small[8][:, :], small[8][:, :], con[:, C_SP:C_SP + E0], SUB))
            link(tt(small[8][:, :], small[8][:, :], small[10][:, :], MUL))
            link(tt(small[8][:, :], small[8][:, :], con[:, C_SP:C_SP + E0], ADD))
            link(dve.tensor_copy(padi[:, :], small[8][:, :]))
            t_iota = con[0:1, C_T:C_T + TILES]
            link(tt(cmp_t[:, :, :], t_iota.rearrange("p (t a) -> p t a", a=1).broadcast_to([1, TILES, E0]),
                    starts[0:1, :].rearrange("p (a e) -> p a e", a=1).broadcast_to([1, TILES, E0]), ALU.is_ge))
            link(dve.tensor_reduce(tabf[:, 0, :], cmp_t[:, :, :], AX.X, ADD))
            link(dve.tensor_copy(tab[:, 3, :], tabf[:, 0, :]))
            link(ts(tab[:, 3, :], tab[:, 3, :], 1, None, ALU.bitwise_and))
            link(dve.tensor_copy(tabf[:, 1, :], tab[:, 3, :]))
            link(ts(tabf[:, 1, :], tabf[:, 1, :], float(2 * PACK), None, MUL))
            link(ts(tabf[:, 0, :], tabf[:, 0, :], 1.0, None, ADD))
            link(ts(small[11][:, 0:1], ends[:, E0 - 1:E0], -1.0, None, ADD))
            link(ts(tabf[:, 2, :], t_iota, small[11][0:1, 0:1], float(P), ALU.min, MUL))
            link(ts(tabf[:, 3, 0:E0], starts[0:1, :], float(NG), None, ADD))
            link(dve.tensor_copy(tab[:, 0:3, :], tabf[:, 0:3, :]))
            dve.tensor_copy(tab[:, 3, 0:E0], tabf[:, 3, 0:E0]).then_inc(s_route, 1)
            dve.wait_ge(s_route, 1)

            def xt_low(h, u):
                dve.wait_ge(s_txh, 2 * h + u + 1)
                tt(xT[:, u, 1, :, :].rearrange("p c t -> p (c t)"), bank[6 + u][:, :],
                   xT[:, u, 0, :, :].rearrange("p c t -> p (c t)").bitcast(F), SUB).then_inc(s_txl, 1)

            def zt_low(h, u):
                dve.wait_ge(s_tzh, 2 * h + u + 1)
                tt(zT[:, u, 1, :, :].rearrange("p c t -> p (c t)"), bank[2 + u][:, 0:I0],
                   zT[:, u, 0, :, :].rearrange("p c t -> p (c t)").bitcast(F), SUB).then_inc(s_tzl, 1)

            def gated(h, u):
                dve.wait_ge(s_tsg, 2 * h + u + 1)
                tt(z[:, u, :], bank[u][:, I0:GU], sg[:, u, :], MUL).then_inc(s_tz, 1)

            def tiles(h0, n):
                xt_low(h0, 0)
                xt_low(h0, 1)
                gated(h0, 0)
                with dve.Fori(0, n - 1) as i:
                    h = h0 + i
                    xt_low(h + 1, 0)
                    zt_low(h, 0)
                    gated(h, 1)
                    xt_low(h + 1, 1)
                    zt_low(h, 1)
                    gated(h + 1, 0)
                h = h0 + n - 1
                zt_low(h, 0)
                gated(h, 1)
                zt_low(h, 1)

            tiles(0, NG // 2)
            tiles(NG // 2, TILES // 2)

            clear_pads()
            dve.tensor_copy(tg[:, 0, 0:1], zero[:, 0:1]).then_inc(s_pads, 1)
            dve.sem_inc(s_fin, CREDIT)
            STEPS1 = 34
            start1 = count[0] + 2 * TOP0

            def combine(h, u, step):
                g = 2 * h + u
                dve.wait_ge(s_x[1][u], 16 * h + 16)
                dve.wait_ge(s_gsh[u], 16 * h + 16)
                step(tt(xrow[:, u, :], xrow[:, u, :], gath[:, u, TOP0, :], ADD))
                dve.wait_ge(s_gat[u], 16 * TOP0 * (h + 1))
                for k in range(TOP0):
                    ins = dve.scalar_tensor_tensor(out=xrow[:, u, :], in0=gath[:, u, k, :],
                                                   scalar=wtok[:, ds(g, 1), k], in1=xrow[:, u, :],
                                                   op0=MUL, op1=ADD)
                    if k < TOP0 - 1:
                        step(ins)
                ins.then_inc(s_comb, 1)

            for u in range(2):
                combine(0, u, link)
            body_ = chain_vector(dve, 1)

            def body1(i, last):
                k = 0

                def step(ins):
                    nonlocal k
                    k += 1
                    ins.then_inc(s_chain, 1)
                    hold(dve, s_chain, start1 + STEPS1 * i + k)

                def middle(i_):
                    for u in range(2):
                        combine(i_ + 1, u, step)

                body_(i, last, middle)
                for u in range(2):
                    g = 2 * i + u
                    l_ = lambda a_, b_: lg[:, u, a_:b_]
                    dve.wait_ge(s_gate[1], g + 1)
                    step(dve.tensor_reduce(l_(0, 1), bank[2 + u][:, 0:E1], AX.X, ALU.max))
                    ts(l_(1, 2), l_(0, 1), -1.0, None, MUL).then_inc(s_lmax, 1)
                for u in range(2):
                    g = 2 * i + u
                    l_ = lambda a_, b_: lg[:, u, a_:b_]
                    dve.wait_ge(s_exp, g + 1)
                    step(dve.reciprocal(l_(3, 4), l_(2, 3)))
                    step(ts(l_(16, 24), l_(8, 16), l_(3, 4), None, MUL))
                    step(dve.max(l_(24, 32), l_(16, 24)))
                    step(dve.max_index(i8b[:, u, :], l_(24, 32), l_(16, 24)))
                    step(dve.tensor_copy(l_(32, 40), i8b[:, u, :]))
                    step(tt(l_(4, 5), l_(24, 25), l_(25, 26), ADD))
                    step(dve.reciprocal(l_(5, 6), l_(4, 5)))
                    step(ts(l_(6, 8), l_(24, 26), l_(5, 6), None, MUL))
                    e_iota = con[:, C_E:C_E + E1]
                    step(ts(l_(40, 48), e_iota, l_(32, 33), l_(6, 7), ALU.is_equal, MUL))
                    step(ts(l_(48, 56), e_iota, l_(33, 34), l_(7, 8), ALU.is_equal, MUL))
                    step(tt(l_(56, 64), l_(40, 48), l_(48, 56), ADD))
                    tt(hw[:, u, :].rearrange("p (e r) -> p e r", r=R1),
                       bank[2 + u][:, E1:E1 + E1 * R1].rearrange("p (e r) -> p e r", r=R1),
                       l_(56, 64).rearrange("p (e a) -> p e a", a=1).broadcast_to([P, E1, R1]), MUL)\
                        .then_inc(s_rw, 1)
                for u in range(2):
                    dve.wait_ge(s_hth, 2 * i + u + 1)
                    tt(hwT[:, u, 1, :], bank[4 + u][:, 0:P], hwT[:, u, 0, :].bitcast(F), SUB).then_inc(s_htl, 1)
                for u in range(2):
                    g = 2 * i + u
                    dve.wait_ge(s_sum, g + 1)
                    dve.wait_ge(s_out[u], 16 * i + 16)
                    step(tt(yo[:, u, :], bank[u][:, :], bb[:, :], ADD))
                    dve.wait_ge(s_res[u], 16 * i + 16)
                    tt(yo[:, u, :], yo[:, u, :], res[:, u, :], ADD).then_inc(s_fin, 1)

            body_loop(dve, body1)

        @block.gpsimd
        def _(pool):
            count = [0]

            def link(ins):
                count[0] += 1
                ins.then_inc(s_pchain, 1)
                pool.wait_ge(s_pchain, count[0])

            pool.wait_ge(s_setup_in[2], 16)
            pool.wait_ge(s_sq, 1)
            build_taps(pool, 1, link)
            pool.wait_ge(s_taps[1], 1)
            pool.wait_ge(s_dsum, 1)
            pool.wait_ge(s_taps[0], 1)

            def load_pack(h, b):
                pool.dma_start(rawp[:, b, :], a["packs"][ds(2 * h + b, 1), :, :].rearrange("a p n -> p (a n)"))\
                    .then_inc(s_raw[b], 16)

            def high_pack(h, b):
                pool.dma_start(pack[:, b, 0, :], a["packs"][ds(2 * h + b, 1), :, :].rearrange("a p n -> p (a n)"))\
                    .then_inc(s_pk_hi[b], 16)

            def split_pack(h, b):
                hold(pool, s_raw[b], 16 * h + 16)
                hold(pool, s_pk_hi[b], 16 * h + 16)
                pool.tensor_tensor(pack[:, b, 1, :], rawp[:, b, :], pack[:, b, 0, :].bitcast(F), SUB)\
                    .then_inc(s_pk, 1)
                pool.wait_ge(s_pk, 2 * h + b + 1)

            pool.wait_ge(s_val[0], 1)
            for b in range(2):
                load_pack(0, b)
                high_pack(0, b)
            for b in range(2):
                split_pack(0, b)
                load_pack(1, b)

            pool.wait_ge(s_route, 1)
            for u in range(2):
                pool.wait_ge(s_saved[u], 16 * (NB + 1))
                pool.dma_start(xrow[:, u, :], xtok[u * P:(u + 1) * P, :]).then_inc(s_pool_in[u], 16)
            for e in range(E0):
                pool.indirect_dma_start(out=xs, out_offset=bass.IndirectOffsetOnAxis(ap=padi[:, e:e + 1], axis=0),
                                        in_=zero[:, :], in_offset=None).then_inc(s_scat, 16)

            def scatters(i, last):
                for u in range(2):
                    g = 2 * i + u
                    pool.tensor_copy(idx[:, u, :], slot[:, ds(g, 1), :].rearrange("p a k -> p (a k)"))\
                        .then_inc(s_idx, 1)
                    pool.wait_ge(s_idx, g + 1)
                    hold(pool, s_pool_in[u], 16 * i + 16)
                    for k in range(TOP0):
                        pool.indirect_dma_start(out=xs,
                                                out_offset=bass.IndirectOffsetOnAxis(ap=idx[:, u, k:k + 1], axis=0),
                                                in_=xrow[:, u, :], in_offset=None).then_inc(s_scat, 16)
                    hold(pool, s_scat, 16 * (E0 + TOP0) + 16 * TOP0 * g)
                    if not last:
                        pool.dma_start(xrow[:, u, :], xtok[ds((g + 2) * P, P), :]).then_inc(s_pool_in[u], 16)

            body_loop(pool, scatters)

            def package(h, b, more):
                through = pool.value_load(tab[0:1, 3, ds(2 * h - 2 + b, 1)], min_val=NG, max_val=NG + TILES)
                hold(pool, s_tdn, through)
                high_pack(h, b)
                split_pack(h, b)
                if more:
                    load_pack(h + 1, b)

            with pool.Fori(0, NPACK // 2 - 2) as j:
                for b in range(2):
                    package(j + 1, b, True)
            for b in range(2):
                package(NPACK // 2 - 1, b, False)

            for u in range(2):
                pool.wait_ge(s_tys[u], 16 * ((NG + TILES) // 2 + 1))

            def gather(g, u):
                pool.tensor_copy(idx[:, u, :], slot[:, ds(g, 1), :].rearrange("p a k -> p (a k)"))\
                    .then_inc(s_idx, 1)
                hold(pool, s_idx, NG + g + 1)
                for k in range(TOP0):
                    pool.indirect_dma_start(out=gath[:, u, k, :], out_offset=None, in_=ys,
                                            in_offset=bass.IndirectOffsetOnAxis(ap=idx[:, u, k:k + 1], axis=0))\
                        .then_inc(s_gat[u], 16)

            for u in range(2):
                gather(u, u)
            with pool.Fori(0, NB - 1) as i:
                for u in range(2):
                    pool.wait_ge(s_comb, 2 * i + u + 1)
                    gather(2 * i + 2 + u, u)



def laid_out(x, cond_512, w):
    f = np.float32
    arr = {}
    arr["x"] = np.ascontiguousarray(x).reshape(NG, P, L)
    con = np.zeros((P, C_END), f)
    con[:, C_ID:C_ID + P] = np.eye(P)
    con[:, C_TRI:C_TRI + P] = np.triu(np.ones((P, P)), 1)
    con[:, C_ONE:C_ONE + P] = 1
    con[:, C_E:C_E + E0] = np.arange(E0)
    con[:, C_T:C_T + TILES] = np.arange(TILES)
    con[:, C_P] = np.arange(P)
    con[:, C_SP:C_SP + E0] = SPARE + np.arange(E0) * P + np.arange(P)[:, None]
    arr["consts"] = con
    arr["style_t"] = np.ascontiguousarray(cond_512.T)
    mod = np.zeros((STYLE, 2, LAYERS, SPG, P), f)
    vec = np.zeros((P, 2, 2, LAYERS), f)
    for c in range(2):
        mw, mb = w[f"L{c}_cond_mod_w"], w[f"L{c}_cond_mod_b"]
        for b in range(SPG):
            mod[:, c, :, b, b * C:(b + 1) * C] = mw.transpose(2, 0, 1)
            vec[b * C:(b + 1) * C, c, 0, :] = mb.T
            vec[b * C:(b + 1) * C, c, 1, :] = w[f"L{c}_cond_biases"].T
        cw = w[f"L{c}_cond_weights"]
        conv = np.zeros((P, 15, P), f)
        for n, (layer, turned) in enumerate(((0, 1), (1, 0), (2, 1), (3, 1), (1, 1))):
            for k in range(TAPS):
                m = cw[layer, :, :, k].T if turned else cw[layer, :, :, k]
                for b in range(SPG):
                    conv[b * C:(b + 1) * C, 3 * n + k, b * C:(b + 1) * C] = m
        arr[f"conv{c}"] = conv
    arr["mod_t"], arr["vecs"] = mod, vec

    def rows(m, chunks):
        return m.reshape(chunks, P, -1).transpose(1, 0, 2)

    arr["gate_t"] = np.ascontiguousarray(rows(w["L0_ffn_gate_w"].T, HC))
    arr["gate_bias"] = np.ascontiguousarray(np.broadcast_to(w["L0_ffn_bias"], (P, E0)))
    arr["base_bias"] = np.ascontiguousarray(np.broadcast_to(w["L1_ffn_b_base"], (P, L)))
    packs = np.zeros((NPACK, P, PACK), f)

    def expert(m, wg, wu, wd):
        gu = np.concatenate([rows(wg.T, HC), rows(wu.T, HC)], axis=2)
        packs[m, :, 0:DOWN] = gu.reshape(P, -1)
        packs[m, :, DOWN:DOWN + IC * L] = rows(wd.T, IC).reshape(P, -1)

    expert(0, w["L0_ffn_Sg"], w["L0_ffn_Su"], w["L0_ffn_Sd"])
    for e in range(E0):
        expert(1 + e, w["L0_ffn_Wg"][e], w["L0_ffn_Wu"][e], w["L0_ffn_Wd"][e])
    low = np.concatenate([w["L1_ffn_W_gate"], w["L1_ffn_A"].reshape(E1 * R1, L)], axis=0)
    packs[NPACK - 1] = np.concatenate([
        rows(w["L1_ffn_W_base"].T, HC).reshape(P, -1), rows(low.T, HC).reshape(P, -1),
        w["L1_ffn_B"].transpose(0, 2, 1).reshape(E1 * R1, L)], axis=1)
    arr["packs"] = packs
    return arr


def kernel(x, cond_512, **weights):
    import concourse.bacc as bacc
    from concourse.bass_utils import run_bass_kernel_spmd

    w = {k: np.asarray(v) for k, v in weights.items()}
    arrays = laid_out(np.asarray(x), np.asarray(cond_512), w)
    nc = bacc.Bacc("TRN2", target_bir_lowering=False, num_devices=1)
    a = {k: nc.dram_tensor(f"in_{k}", v.shape, mybir.dt.float32, kind="ExternalInput").ap()
         for k, v in arrays.items()}
    out = nc.dram_tensor("out", (NG * P, L), mybir.dt.float32, kind="ExternalOutput").ap()
    build(nc, a, out)
    r = run_bass_kernel_spmd(nc, [{f"in_{k}": v for k, v in arrays.items()}], core_ids=[0])
    return r.results[0]["out"].reshape(B, C, L)
```

```python
import numpy as np
from contextlib import ExitStack

import concourse.bass as bass
import concourse.mybir as mybir

P = 128
B, C, L = 64, 32, 512
SPG = P // C
NG = B * C // P
STYLE, LAYERS, TAPS = 64, 4, 3
NTAP = 18
HC = L // P
E0, TOP0, I0 = 16, 4, 256
IC = I0 // P
E1, R1, TOP1 = 8, 16, 2
GU = 2 * I0
PACK = HC * (L + E1 + E1 * R1) + L
DOWN = HC * GU
NPACK = 1 + E0 + 1
TILES = NG * TOP0 + E0
SPARE = TILES * P
ROWS = SPARE + E0 * P
PADDED = L + 2
CONV_SCALE = 1.0 / float(np.sqrt(C * TAPS ** 2))
EPS = 1e-8
BLUR = 0.125

C_ID, C_TRI, C_ONE = 0, P, 2 * P
C_E = 3 * P
C_T = C_E + E0
C_P = C_T + TILES
C_SP = C_P + 1
C_END = C_SP + E0


def build(nc, a, out):
    F, R, I, U = mybir.dt.float32, mybir.dt.float32r, mybir.dt.int32, mybir.dt.uint32
    ALU, ACT, AX = mybir.AluOpType, mybir.ActivationFunctionType, mybir.AxisListType
    ADD, SUB, MUL = ALU.add, ALU.subtract, ALU.mult
    ds = bass.ds

    ctx = ExitStack()
    with ctx:
        top = [nc.sbuf_base]

        def at(name, shape, dt, offset=None):
            size = int(np.prod(shape[1:])) * 4
            if offset is None:
                offset = (top[0] + 31) // 32 * 32
                top[0] = offset + size
            return nc.alloc_sbuf_tensor_at(name, shape, dt, offset=offset), offset

        def new(name, shape, dt=F):
            return at(name, shape, dt)[0]

        taps = [new(f"taps{c}", [P, 2, NTAP, P], R) for c in range(2)]
        in1, in1_at = at("in1", [P, 2, 2, PADDED], R)
        in2 = new("in2", [P, 2, 2, PADDED], R)
        in3, in3_at = at("in3", [P, 2, 2, 2, PADDED], R)
        in4, in4_at = at("in4", [P, 2, 2, 2, PADDED], R)
        SLOT = 2 * PACK
        in34_end = top[0]
        pack, pack_at = at("pack", [P, 3, 2, PACK], R, (in34_end - SLOT * 4) // 32 * 32)
        assert pack_at >= in3_at
        top[0] = pack_at + 3 * SLOT * 4
        rawp, rawp_at = at("rawp", [P, 2, PACK], F)
        raw1, _ = at("raw1", [P, PACK], F, in1_at)
        assert in1_at + PACK * 4 <= in3_at
        raws = [rawp[:, 0, :], raw1[:, :], rawp[:, 1, :]]
        val = new("val", [P, 2, L])
        xrow = new("xrow", [P, 2, L])
        crow = new("crow", [P, 2, L])
        xT = new("xT", [P, 2, 2, HC, P], R)
        tin, tin_at = at("tin", [P, 2, L], F)
        sg = new("sg", [P, 2, I0])
        z, z_at = at("z", [P, 2, I0], F)
        zT, zT_at = at("zT", [P, 2, 2, IC, P], R)
        ty, ty_at = at("ty", [P, 2, L], F)
        con = new("con", [P, C_END])
        ident = con[:, C_ID:C_ID + P]
        vec = new("vec", [P, 2, 2, LAYERS])
        styl = new("styl", [STYLE, B])
        mod_s = new("mod_s", [P, 2, LAYERS, NG])
        dem = new("dem", [P, 2, LAYERS, NG])
        dtmp = new("dtmp", [P, 2, LAYERS, NG])
        scl = new("scl", [P, 2, LAYERS, NG])
        bia = new("bia", [P, 2, LAYERS, NG])
        edge = new("edge", [P, 2, NG])
        gateF = new("gateF", [P, HC, E0])
        gateT = new("gateT", [P, 2, HC, E0], R)
        gbias = new("gbias", [P, E0])
        tg = new("tg", [P, 2, E0])
        sc = new("sc", [P, 2, E0])
        m8 = new("m8", [P, 2, 8])
        i8 = new("i8", [P, 2, 8], U)
        topv = new("topv", [P, NG, 8])
        topi = new("topi", [P, NG, 8])
        wtok = new("wtok", [P, NG, TOP0])
        slot = new("slot", [P, NG, TOP0], I)
        padi = new("padi", [P, E0], I)
        tabf = new("tabf", [1, 3, TILES])
        tab = new("tab", [1, 3, TILES], I)
        idx = new("idx", [P, 2, TOP0], I)
        bb = new("bb", [P, L])
        lg = new("lg", [P, 2, 64])
        i8b = new("i8b", [P, 2, 8], U)
        zero = new("zero", [P, L])
        warm = new("warm", [P, 2])
        o = in34_end
        craw, cf, cu, csq = [], [], [], []
        for c in range(2):
            t_, o_ = at(f"craw{c}", [P, 15, P], F, o); craw.append(t_); o += 15 * P * 4
            t_, o_ = at(f"cf{c}", [P, NTAP, P], F, o); cf.append(t_); o += NTAP * P * 4
            t_, o_ = at(f"cu{c}", [P, 2, 2, TAPS, P], F, o); cu.append(t_); o += 12 * P * 4
            t_, o_ = at(f"csq{c}", [P, 12, P], F, o); csq.append(t_); o += 12 * P * 4
        assert o <= rawp_at + 2 * PACK * 4, (o, rawp_at + 2 * PACK * 4)
        modT, _ = at("modT", [STYLE, 2, LAYERS, SPG, P], F, in3_at)
        o = in3_at
        GE = [P, NG, E0]
        oh = []
        for k in range(TOP0):
            oh.append(at(f"oh{k}", GE, F, o)[0]); o += NG * E0 * 4
        rt = []
        for k in range(9):
            rt.append(at(f"rt{k}", GE, F, o)[0]); o += NG * E0 * 4
        small = [at(f"rs{k}", [P, E0], F, o + k * E0 * 4)[0] for k in range(12)]
        smalli = [at(f"rsi{k}", [P, E0], I, o + (12 + k) * E0 * 4)[0] for k in range(4)]
        o += 16 * E0 * 4
        assert o <= in3_at + 2 * 2 * 2 * PADDED * 4
        cmp_t = at("cmp_t", [1, TILES, E0], F, in4_at)[0]
        res = at("res", [P, 2, L], F, tin_at)[0]
        hw = at("hw", [P, 2, P], F, z_at)[0]
        hwT = at("hwT", [P, 2, 2, P], R, zT_at)[0]
        yo = at("yo", [P, 2, L], F, ty_at)[0]
        gath = at("gath", [P, 2, TOP0 + 1, L], F, rawp_at)[0]
        assert top[0] <= nc.sbuf_usable_end, (top[0], nc.sbuf_usable_end)

        bank = [ctx.enter_context(nc.psum_tensor(f"bank{k}", [P, 512], F)) for k in range(8)]

        xtok = nc.dram_tensor("token_x", (NG * P, L), F).ap()
        ytok = nc.dram_tensor("token_y", (NG * P, L), F).ap()
        xs = nc.dram_tensor("sorted_x", (ROWS, L), F).ap()
        ys = nc.dram_tensor("sorted_y", (TILES * P, L), F).ap()
        x1d = nc.dram_tensor("x1_rows", (NG * P, L), F).ap()

        HT = 2 * P

        def place(package):
            return (package + 2) % 3

        def hold(eng, semaphore, count):
            eng.wait_ge(semaphore, count)
            eng.nop(nofuse=True)

        def sem(name):
            return ctx.enter_context(nc.semaphore(name))

        s_setup_in = [sem(f"setup_in{k}") for k in range(3)]
        s_const = sem("const_in")
        s_chain = sem("dve_chain")
        s_pchain = sem("pool_chain")
        s_sty = sem("style_sums")
        s_sq = sem("style_squares")
        s_dsum = sem("demod_sums")
        s_dvar = sem("demod_var")
        s_root = sem("demod_root")
        s_scales = sem("scales_ready")
        s_taps = [sem(f"taps_ready{c}") for c in range(2)]
        s_pads = sem("pads_zeroed")
        s_x = [[sem(f"x_loaded{c}{u}") for u in range(2)] for c in range(2)]
        s_val = [sem(f"val_ready{c}") for c in range(2)]
        s_hi = [sem(f"high_part{c}") for c in range(2)]
        s_split = [sem(f"split_done{c}") for c in range(2)]
        s_conv = [sem(f"conv_bank{c}") for c in range(2)]
        s_crow = [sem(f"crow_ready{c}") for c in range(2)]
        s_xt = [sem(f"xt_bank{c}") for c in range(2)]
        s_xth = [sem(f"xt_high{c}") for c in range(2)]
        s_xtl = [sem(f"xt_low{c}") for c in range(2)]
        s_gate = [sem(f"gate_sums{c}") for c in range(2)]
        s_tanh = sem("gate_tanh")
        s_score = sem("score_steps")
        s_low = sem("low_rank_steps")
        s_saved = [sem(f"crow_saved{u}") for u in range(2)]
        s_hot = sem("one_hots")
        s_cnt = sem("counts")
        s_route = sem("routing_ready")
        s_pool_in = [sem(f"scatter_rows_in{u}") for u in range(2)]
        s_idx = sem("index_columns")
        s_scat = sem("scattered")
        s_zero = sem("zero_rows")
        s_raw = [sem(f"raw_pack_in{u}") for u in range(3)]
        s_pk_hi = [sem(f"pack_high{u}") for u in range(3)]
        s_pk = sem("pack_ready")
        s_tx = [sem(f"tile_in{u}") for u in range(2)]
        s_txt = sem("tile_xt")
        s_txh = sem("tile_xt_high")
        s_txl = sem("tile_xt_low")
        s_tup = sem("tile_up")
        s_tsg = sem("tile_silu")
        s_tz = sem("tile_z")
        s_tzt = sem("tile_zt")
        s_tzh = sem("tile_zt_high")
        s_tzl = sem("tile_zt_low")
        s_tdn = sem("tile_down")
        s_ty = sem("tile_y")
        s_tys = [sem(f"tile_saved{u}") for u in range(2)]
        s_gsh = [sem(f"shared_rows_in{u}") for u in range(2)]
        s_gat = [sem(f"gathered{u}") for u in range(2)]
        s_comb = sem("combined")
        s_x1s = [sem(f"x1_saved{u}") for u in range(2)]
        s_res = [sem(f"residual_in{u}") for u in range(2)]
        s_lmax = sem("logit_max")
        s_exp = sem("logit_exp")
        s_rw = sem("low_rank_weighted")
        s_ht = sem("low_rank_transposed")
        s_hth = sem("low_rank_high")
        s_htl = sem("low_rank_low")
        s_sum = sem("layer1_sums")
        s_fin = sem("out_rows")
        s_out = [sem(f"out_saved{u}") for u in range(2)]

        block = ctx.enter_context(nc.Block())

        NB = NG // 2
        BANKS = 12
        CREDIT = 2

        def body_loop(eng, body, first=0):
            with eng.Fori(first, NB - 1) as i:
                body(i, False)
            body(NB - 1, True)

        def nothing(k):
            pass

        def staggered(eng, body, late):
            body(0, False, nothing)
            with eng.Fori(1, NB - 1) as i:
                body(i, False, late(i - 1))
            body(NB - 1, True, late(NB - 2))
            rest = late(NB - 1)
            for k in range(1, BANKS + 2):
                rest(k)

        @block.sync
        def _(sp):
            sp.dma_start(con[:, :], a["consts"]).then_inc(s_const, 16)
            sp.dma_start(styl[:, :], a["style_t"]).then_inc(s_setup_in[0], 16)
            sp.dma_start(modT[:, :, :, :, :], a["mod_t"]).then_inc(s_setup_in[0], 16)
            sp.dma_start(vec[:, :, :, :], a["vecs"]).then_inc(s_setup_in[0], 16)
            sp.dma_start(craw[0][:, :, :], a["conv0"]).then_inc(s_setup_in[1], 16)
            sp.dma_start(craw[1][:, :, :], a["conv1"]).then_inc(s_setup_in[2], 16)
            sp.dma_start(gateF[:, :, :], a["gate_t"]).then_inc(s_const, 16)
            sp.dma_start(gbias[:, :], a["gate_bias"]).then_inc(s_const, 16)
            sp.dma_start(bb[:, :], a["base_bias"]).then_inc(s_const, 16)
            for g in range(2):
                sp.dma_start(xrow[:, g, :], a["x"][g]).then_inc(s_x[0][g], 16)
            for u in range(2):
                sp.sem_inc(s_saved[u], 16)

            def chain0(i, last):
                if not last:
                    for u in range(2):
                        sp.wait_ge(s_val[0], BANKS * i + 1 + u)
                        sp.dma_start(xrow[:, u, :], a["x"][ds(2 * i + 2 + u, 1), :, :].rearrange("a p l -> p (a l)"))\
                          .then_inc(s_x[0][u], 16)
                for u in range(2):
                    sp.wait_ge(s_crow[0], 2 * i + u + 1)
                    sp.dma_start(xtok[ds((2 * i + u) * P, P), :], crow[:, u, :]).then_inc(s_saved[u], 16)

            body_loop(sp, chain0)
            for u in range(2):
                sp.wait_ge(s_saved[u], 16 * (NB + 1))

            def load(h, u, src, row, free=True):
                if free:
                    sp.wait_ge(s_txt, 2 * h + u - 1)
                sp.dma_start(tin[:, u, :], src[ds(row, P), :]).then_inc(s_tx[u], 16)

            for u in range(2):
                load(0, u, xtok, u * P, free=False)
            with sp.Fori(0, NG // 2 - 1) as i:
                for u in range(2):
                    load(i + 1, u, xtok, (2 * i + 2 + u) * P)
            sp.wait_ge(s_route, 1)
            sp.wait_ge(s_scat, 16 * (NG * TOP0 + E0))

            def block_of(t):
                return sp.value_load(tab[0:1, 1, ds(t, 1)], min_val=0, max_val=(TILES - 1) * P)

            for u in range(2):
                load(NG // 2, u, xs, block_of(u))
            with sp.Fori(0, TILES // 2 - 1) as i:
                for u in range(2):
                    load(NG // 2 + i + 1, u, xs, block_of(2 * i + 2 + u))
            for u in range(2):
                sp.wait_ge(s_tys[u], 16 * ((NG + TILES) // 2 + 1))

            sp.wait_ge(s_pk, NPACK)

            def load1(g, u):
                sp.dma_start(xrow[:, u, :], a["x"][ds(g, 1), :, :].rearrange("a p l -> p (a l)"))\
                  .then_inc(s_x[1][u], 16)
                sp.dma_start(gath[:, u, TOP0, :], ytok[ds(g * P, P), :]).then_inc(s_gsh[u], 16)

            def keep_x1(g, u):
                sp.wait_ge(s_comb, g + 1)
                sp.dma_start(x1d[ds(g * P, P), :], xrow[:, u, :]).then_inc(s_x1s[u], 16)

            for u in range(2):
                load1(u, u)
            for u in range(2):
                keep_x1(u, u)
            for u in range(2):
                sp.sem_inc(s_out[u], 16)

            def residual(i):
                for u in range(2):
                    hold(sp, s_x1s[u], 16 * i + 16)
                    sp.wait_ge(s_fin, 2 * i + u + 1)
                    sp.dma_start(res[:, u, :], x1d[ds((2 * i + u) * P, P), :]).then_inc(s_res[u], 16)

            def store_out(i):
                for u in range(2):
                    sp.wait_ge(s_fin, 2 * i + u + 1 + CREDIT)
                    sp.dma_start(out[ds((2 * i + u) * P, P), :], yo[:, u, :]).then_inc(s_out[u], 16)

            def next_in(i):
                for u in range(2):
                    hold(sp, s_x1s[u], 16 * i + 16)
                    sp.wait_ge(s_val[1], BANKS * i + 1 + u)
                    load1(2 * i + 2 + u, u)
                for u in range(2):
                    keep_x1(2 * i + 2 + u, u)

            next_in(0)
            with sp.Fori(1, NB - 1) as i:
                residual(i - 1)
                next_in(i)
                store_out(i - 1)
            for i in (NB - 2, NB - 1):
                residual(i)
                store_out(i)
            for u in range(2):
                sp.wait_ge(s_out[u], 16 * (NB + 1))

        def chain_scalar(act, c):
            def body(i, last, late):
                k = 0
                for layer, u, h in ([(0, 0, 0), (0, 1, 0)] + [(1, u, h) for u in range(2) for h in range(2)]
                                    + [(2, u, h) for u in range(2) for h in range(2)]):
                    g = 2 * i + u
                    k += 1
                    b = bank[BANK_OF[layer][u][h]]
                    act.wait_ge(s_split[c], BANKS * i + k)
                    hold(act, s_conv[c], BANKS * i + k)
                    v = val[:, (k + 1) % 2, :]
                    s_, b_ = scl[:, c, layer, ds(g, 1)], bia[:, c, layer, ds(g, 1)]
                    if layer == 1:
                        one, rest = (0, slice(1, L)) if h == 0 else (L - 1, slice(0, L - 1))
                        act.activation(v[:, one:one + 1], b[:, one:one + 1], ACT.Identity, scale=s_,
                                       bias=edge[:, c, ds(g, 1)])
                        act.activation(v[:, rest], b[:, rest], ACT.Identity, scale=s_, bias=b_)\
                           .then_inc(s_val[c], 1)
                    else:
                        act.activation(v, b[:, :], ACT.Identity, scale=s_, bias=b_).then_inc(s_val[c], 1)
                    late(k)
                if not last:
                    for u in range(2):
                        k += 1
                        act.wait_ge(s_split[c], BANKS * i + k)
                        act.wait_ge(s_x[c][u], 16 * i + 32)
                        if c == 1:
                            act.wait_ge(s_comb, 2 * i + 3 + u)
                        act.activation(val[:, (k + 1) % 2, :], xrow[:, u, :], ACT.Copy,
                                       scale=mod_s[:, c, 0, ds(2 * i + 2 + u, 1)]).then_inc(s_val[c], 1)
                for u in range(2):
                    if c == 0:
                        act.wait_ge(s_saved[u], 16 * i + 16)
                    hold(act, s_conv[c], BANKS * i + 11 + u)
                    act.activation(crow[:, u, :], bank[BANK_OF[3][u][0]][:, :], ACT.Identity,
                                   scale=scl[:, c, 3, ds(2 * i + u, 1)], bias=vec[:, c, 1, 3:4])\
                       .then_inc(s_crow[c], 1)

            for u in range(2):
                act.wait_ge(s_x[c][u], 16)
                if c == 1:
                    act.wait_ge(s_comb, u + 1)
                act.activation(val[:, u, :], xrow[:, u, :], ACT.Copy, scale=mod_s[:, c, 0, u:u + 1])\
                   .then_inc(s_val[c], 1)
            return body

        def chain_xt_high(act, c, i):
            for u in range(2):
                act.wait_ge(s_xt[c], 2 * i + u + 1)
                act.activation(xT[:, u, 0, :, :].rearrange("p c t -> p (c t)"), bank[6 + u][:, :], ACT.Copy)\
                   .then_inc(s_xth[c], 1)

        BANK_OF = {0: [[0], [1]], 1: [[2, 3], [4, 5]], 2: [[0, 1], [2, 3]], 3: [[4], [5]]}

        def split(dve, c, n, slot_, dst):
            dve.wait_ge(s_val[c], n)
            dve.tensor_copy(dst(0), val[:, slot_, :]).then_inc(s_hi[c], 1)
            dve.wait_ge(s_hi[c], n)
            dve.tensor_tensor(dst(1), val[:, slot_, :], dst(0).bitcast(F), SUB).then_inc(s_split[c], 1)

        def chain_xt_low(dve, c, i):
            for u in range(2):
                dve.wait_ge(s_xth[c], 2 * i + u + 1)
                dve.tensor_tensor(xT[:, u, 1, :, :].rearrange("p c t -> p (c t)"), bank[6 + u][:, :],
                                  xT[:, u, 0, :, :].rearrange("p c t -> p (c t)").bitcast(F), SUB)\
                   .then_inc(s_xtl[c], 1)

        def chain_vector(dve, c):
            def dst1(u):
                return lambda p: in1[:, u, p, 1:L + 1]

            def body(i, last, late, middle=None):
                k = 0
                for dst in ([(lambda p, u=u: in2[:, u, p, 1:L + 1]) for u in range(2)]
                            + [(lambda p, u=u, h=h: in3[:, u, h, p, 1:L + 1]) for u in range(2) for h in range(2)]
                            + [(lambda p, u=u, h=h: in4[:, u, h, p, 1:L + 1]) for u in range(2) for h in range(2)]):
                    k += 1
                    split(dve, c, BANKS * i + k + 2, (k + 1) % 2, dst)
                    late(k)
                if not last:
                    if middle:
                        middle(i)
                    for u in range(2):
                        k += 1
                        split(dve, c, BANKS * i + k + 2, (k + 1) % 2, dst1(u))
                late(BANKS)

            for u in range(2):
                split(dve, c, u + 1, u, dst1(u))
            return body

        PARTS = ((0, 0), (0, 1), (1, 0))

        def products(pe, dst, terms, start=True, stop=True):
            n = len(terms) * len(PARTS)
            k = 0
            for lhs, rhs in terms:
                for p, q in PARTS:
                    mm = pe.matmul(dst, lhs(p), rhs(q), start=start and k == 0, stop=stop and k == n - 1)
                    k += 1
            return mm

        def chain_tensor(pe, c):
            def tap(n):
                return lambda p: taps[c][:, p, n, :]

            def body(i, last, late):
                for u in range(2):
                    pe.wait_ge(s_split[c], BANKS * i + 1 + u)
                    products(pe, bank[BANK_OF[0][u][0]][:, :],
                             [(tap(k), lambda p, u=u, k=k: in1[:, u, p, k:k + L]) for k in range(TAPS)])\
                        .then_inc(s_conv[c], 1)
                    late(1 + u)
                for u in range(2):
                    pe.wait_ge(s_split[c], BANKS * i + 3 + u)
                    for h in range(2):
                        products(pe, bank[BANK_OF[1][u][h]][:, :],
                                 [(tap(3 + 4 - 2 * k + h), lambda p, u=u, k=k: in2[:, u, p, k:k + L])
                                  for k in range(TAPS)]).then_inc(s_conv[c], 1)
                    late(4 + 2 * u)
                for u in range(2):
                    pe.wait_ge(s_split[c], BANKS * i + 6 + 2 * u)
                    for h, where in ((0, ((1, 0), (0, 1), (1, 1))), (1, ((0, 1), (1, 1), (0, 2)))):
                        products(pe, bank[BANK_OF[2][u][h]][:, :],
                                 [(tap(9 + k), lambda p, u=u, s=s, q=q: in3[:, u, s, p, q:q + L])
                                  for k, (s, q) in enumerate(where)]).then_inc(s_conv[c], 1)
                    late(8 + 2 * u)
                for u in range(2):
                    pe.wait_ge(s_split[c], BANKS * i + 10 + 2 * u)
                    products(pe, bank[BANK_OF[3][u][0]][:, :],
                             [(tap(12 + r), lambda p, u=u, r=r: in4[:, u, r % 2, p, r // 2:r // 2 + L])
                              for r in range(6)]).then_inc(s_conv[c], 1)
                    late(11 + u)
            return body

        def chain_turn(pe, c, i):
            for u in range(2):
                if c == 1:
                    pe.wait_ge(s_fin, 2 * i + u + 1)
                pe.wait_ge(s_crow[c], 2 * i + u + 1)
                for j in range(HC):
                    mm = pe.transpose(bank[6 + u][:, j * P:(j + 1) * P], crow[:, u, j * P:(j + 1) * P], ident)
                mm.then_inc(s_xt[c], 1)

        def XT(u):
            return [(lambda p, j=j: xT[:, u, p, j, :]) for j in range(HC)]

        @block.scalar
        def _(act):
            act.wait_ge(s_dvar, 1)
            act.activation(dtmp[:, :, :, :], dem[:, :, :, :], ACT.Sqrt).then_inc(s_root, 1)
            act.wait_ge(s_scales, 1)

            def late0(i):
                def late(k):
                    if k == 2:
                        chain_xt_high(act, 0, i)
                    if k == 6:
                        for u in range(2):
                            act.wait_ge(s_gate[0], 2 * i + u + 1)
                            act.activation(tg[:, u, :], bank[6 + u][:, 0:E0], ACT.Tanh, scale=0.5)\
                               .then_inc(s_tanh, 1)
                return late

            act.wait_ge(s_const, 64)
            act.activation(warm[:, 0:1], ident[:, 0:1], ACT.Tanh)
            staggered(act, chain_scalar(act, 0), late0)

            act.sem_inc(s_ty, CREDIT)

            def xt_high(h, u):
                act.wait_ge(s_txt, 2 * h + u + 1)
                act.activation(xT[:, u, 0, :, :].rearrange("p c t -> p (c t)"), bank[6 + u][:, :], ACT.Copy)\
                   .then_inc(s_txh, 1)

            def zt_high(h, u):
                act.wait_ge(s_tzt, 2 * h + u + 1)
                act.activation(zT[:, u, 0, :, :].rearrange("p c t -> p (c t)"), bank[2 + u][:, 0:I0], ACT.Copy)\
                   .then_inc(s_tzh, 1)

            def silu(h, u):
                act.wait_ge(s_tup, 2 * h + u + 1)
                act.activation(sg[:, u, :], bank[u][:, 0:I0], ACT.Silu).then_inc(s_tsg, 1)

            def rows(h, u):
                act.wait_ge(s_tdn, 2 * h + u + 1)
                act.wait_ge(s_tys[u], 16 * h + 16)
                act.activation(ty[:, u, :], bank[4 + u][:, :], ACT.Copy).then_inc(s_ty, 1)

            for u in range(2):
                act.sem_inc(s_tys[u], 16)

            def save(h, u, dst, k):
                hold(act, s_ty, 2 * h + u + 1 + CREDIT)
                act.dma_start(dst[ds(k * P, P), :], ty[:, u, :]).then_inc(s_tys[u], 16)

            def tiles(h0, n, dst):
                xt_high(h0, 0)
                xt_high(h0, 1)
                silu(h0, 0)
                with act.Fori(0, n - 1) as i:
                    h = h0 + i
                    xt_high(h + 1, 0)
                    zt_high(h, 0)
                    silu(h, 1)
                    rows(h, 0)
                    xt_high(h + 1, 1)
                    save(h, 0, dst, 2 * i)
                    zt_high(h, 1)
                    silu(h + 1, 0)
                    rows(h, 1)
                    save(h, 1, dst, 2 * i + 1)
                h = h0 + n - 1
                zt_high(h, 0)
                silu(h, 1)
                rows(h, 0)
                save(h, 0, dst, 2 * n - 2)
                zt_high(h, 1)
                rows(h, 1)
                save(h, 1, dst, 2 * n - 1)

            tiles(0, NG // 2, ytok)
            tiles(NG // 2, TILES // 2, ys)

            def late1(i):
                def late(k):
                    if k == 2:
                        chain_xt_high(act, 1, i)
                    if k == 6:
                        for u in range(2):
                            act.wait_ge(s_lmax, 2 * i + u + 1)
                            act.activation(lg[:, u, 8:16], bank[6 + u][:, 0:E1], ACT.Exp, bias=lg[:, u, 1:2],
                                           accum_out=lg[:, u, 2:3]).then_inc(s_exp, 1)
                    if k == 10:
                        for u in range(2):
                            act.wait_ge(s_ht, 2 * i + u + 1)
                            act.activation(hwT[:, u, 0, :], bank[6 + u][:, HT:HT + P], ACT.Copy).then_inc(s_hth, 1)
                return late

            act.activation(warm[:, 1:2], ident[:, 0:1], ACT.Exp)
            staggered(act, chain_scalar(act, 1), late1)

        @block.tensor
        def _(pe):
            pe.wait_ge(s_setup_in[0], 48)
            sview = styl[:, :].rearrange("k (g b) -> k b g", b=SPG)
            for c in range(2):
                for layer in range(LAYERS):
                    for b in range(SPG):
                        mm = pe.matmul(bank[0][:, (c * LAYERS + layer) * NG:(c * LAYERS + layer + 1) * NG],
                                       modT[:, c, layer, b, :], sview[:, b, :], start=b == 0, stop=b == SPG - 1)
            mm.then_inc(s_sty, 1)
            pe.wait_ge(s_sq, 1)
            for c in range(2):
                for layer in range(LAYERS):
                    n = (c * LAYERS + layer) * NG
                    mm = pe.matmul(bank[1][:, n:n + NG], csq[c][:, layer, :], dtmp[:, c, layer, :],
                                   start=True, stop=True)
            mm.then_inc(s_dsum, 1)

            pe.wait_ge(s_taps[0], 1)
            pe.wait_ge(s_pads, 1)
            pe.wait_ge(s_const, 64)

            def late0(i):
                def late(k):
                    if k == 2:
                        chain_turn(pe, 0, i)
                    if k == 4:
                        for u in range(2):
                            pe.wait_ge(s_xtl[0], 2 * i + u + 1)
                            products(pe, bank[6 + u][:, 0:E0],
                                     [(x, lambda p, j=j: gateT[:, p, j, :]) for j, x in enumerate(XT(u))])\
                                .then_inc(s_gate[0], 1)
                return late

            staggered(pe, chain_tensor(pe, 0), late0)

            pe.wait_ge(s_hot, 1)
            hot = rt[0][:, :, :].rearrange("p g e -> p (g e)")
            pe.matmul(bank[0][:, 0:NG * E0], con[:, C_TRI:C_TRI + P], hot, start=True, stop=True)
            pe.matmul(bank[1][:, 0:NG * E0], con[:, C_ONE:C_ONE + P], hot, start=True, stop=True).then_inc(s_cnt, 1)

            def turn(h, u):
                pe.wait_ge(s_tx[u], 16 * h + 16)
                for j in range(HC):
                    mm = pe.transpose(bank[6 + u][:, j * P:(j + 1) * P], tin[:, u, j * P:(j + 1) * P], ident)
                mm.then_inc(s_txt, 1)

            def up(h, u, package, half):
                ready, where = package
                if half == 0:
                    hold(pe, s_pk, ready)
                    pe.wait_ge(s_txl, 2 * h + u + 1)
                js = range(HC // 2) if half == 0 else range(HC // 2, HC)
                mm = products(pe, bank[u][:, :],
                              [(XT(u)[j], lambda p, j=j: where(p, j * GU)) for j in js],
                              start=half == 0, stop=half == 1)
                if half == 1:
                    mm.then_inc(s_tup, 1)

            def turn_z(h, u):
                pe.wait_ge(s_tz, 2 * h + u + 1)
                for j in range(IC):
                    mm = pe.transpose(bank[2 + u][:, j * P:(j + 1) * P], z[:, u, j * P:(j + 1) * P], ident)
                mm.then_inc(s_tzt, 1)

            def down(h, u, package):
                where = package[1]
                pe.wait_ge(s_tzl, 2 * h + u + 1)
                pe.wait_ge(s_ty, 2 * h + u + 1)
                products(pe, bank[4 + u][:, :],
                         [(lambda p, j=j: zT[:, u, p, j, :], lambda p, j=j: where(p, DOWN + j * L))
                          for j in range(IC)]).then_inc(s_tdn, 1)

            def tiles(h0, n, package):
                turn(h0, 0)
                turn(h0, 1)
                w0 = package(0)
                up(h0, 0, w0, 0)
                up(h0, 0, w0, 1)
                with pe.Fori(0, n - 1) as i:
                    h = h0 + i
                    turn(h + 1, 0)
                    w1 = package(2 * i + 1)
                    up(h, 1, w1, 0)
                    turn_z(h, 0)
                    w0 = package(2 * i)
                    up(h, 1, w1, 1)
                    down(h, 0, w0)
                    turn(h + 1, 1)
                    w2 = package(2 * i + 2)
                    up(h + 1, 0, w2, 0)
                    turn_z(h, 1)
                    up(h + 1, 0, w2, 1)
                    down(h, 1, w1)
                h = h0 + n - 1
                w0, w1 = package(2 * n - 2), package(2 * n - 1)
                up(h, 1, w1, 0)
                turn_z(h, 0)
                up(h, 1, w1, 1)
                down(h, 0, w0)
                turn_z(h, 1)
                down(h, 1, w1)

            tiles(0, NG // 2, lambda k: (1, lambda p, n: pack[:, place(0), p, n:n + 512]))

            pe.wait_ge(s_route, 1)
            flat = pack[:, :, :, :].rearrange("p s h n -> p (s h n)")

            def chosen(k):
                number = pe.value_load(tab[0:1, 0, ds(k, 1)], min_val=1, max_val=E0)
                off = place(number) * SLOT
                return number + 1, lambda p, n: flat[:, ds(off + (p * PACK + n), 512)]

            tiles(NG // 2, TILES // 2, chosen)

            pe.wait_ge(s_taps[1], 1)
            pe.wait_ge(s_pads, 2)
            pe.wait_ge(s_pk, NPACK)
            W1 = place(NPACK - 1)
            NA = E1 + E1 * R1

            def late1(i):
                def late(k):
                    if k == 2:
                        chain_turn(pe, 1, i)
                    if k == 4:
                        for u in range(2):
                            pe.wait_ge(s_xtl[1], 2 * i + u + 1)
                            products(pe, bank[6 + u][:, 0:NA],
                                     [(x, lambda p, j=j: pack[:, W1, p, HC * L + j * NA:HC * L + (j + 1) * NA])
                                      for j, x in enumerate(XT(u))]).then_inc(s_gate[1], 1)
                    if k == 10:
                        for u in range(2):
                            pe.wait_ge(s_rw, 2 * i + u + 1)
                            pe.transpose(bank[6 + u][:, HT:HT + P], hw[:, u, :], ident).then_inc(s_ht, 1)
                    if k in (11, 12):
                        u = k - 11
                        pe.wait_ge(s_htl, 2 * i + u + 1)
                        products(pe, bank[6 + u][:, :],
                                 [(x, lambda p, j=j: pack[:, W1, p, j * L:(j + 1) * L])
                                  for j, x in enumerate(XT(u))]
                                 + [(lambda p: hwT[:, u, p, :],
                                     lambda p: pack[:, W1, p, HC * (L + NA):HC * (L + NA) + L])])\
                            .then_inc(s_sum, 1)
                return late

            staggered(pe, chain_tensor(pe, 1), late1)

        def build_taps(eng, c, link):
            w, f, u_ = craw[c], cf[c], cu[c]
            link(eng.tensor_scalar(w[:, :, :], w[:, :, :], CONV_SCALE, None, MUL))
            eng.tensor_copy(f[:, 0:3, :], w[:, 0:3, :])
            eng.tensor_copy(f[:, 9:12, :], w[:, 6:9, :])
            for n, (lay, gain) in enumerate(((1, 2 * BLUR), (3, BLUR))):
                link(eng.tensor_scalar(u_[:, n, 0, :, :], w[:, 3 * lay:3 * lay + 3, :], gain, None, MUL))
                link(eng.tensor_scalar(u_[:, n, 1, :, :], w[:, 3 * lay:3 * lay + 3, :], 3 * gain, None, MUL))
            for n, base in enumerate((3, 12)):
                one, three = u_[:, n, 0, :, :], u_[:, n, 1, :, :]
                t = [f[:, base + r, :] for r in range(6)]
                eng.tensor_copy(t[0], one[:, 0, :])
                eng.tensor_copy(t[5], one[:, 2, :])
                eng.tensor_tensor(t[1], three[:, 0, :], one[:, 1, :], ADD)
                eng.tensor_tensor(t[4], one[:, 1, :], three[:, 2, :], ADD)
                eng.tensor_tensor(t[2], three[:, 0, :], three[:, 1, :], ADD)
                link(eng.tensor_tensor(t[3], three[:, 1, :], three[:, 2, :], ADD))
                link(eng.tensor_tensor(t[2], t[2], one[:, 2, :], ADD))
                link(eng.tensor_tensor(t[3], t[3], one[:, 0, :], ADD))
            link(eng.tensor_copy(taps[c][:, 0, :, :], f[:, :, :]))
            eng.tensor_tensor(taps[c][:, 1, :, :], f[:, :, :], taps[c][:, 0, :, :].bitcast(F), SUB)\
               .then_inc(s_taps[c], 1)

        @block.vector
        def _(dve):
            count = [0]

            def link(ins):
                count[0] += 1
                ins.then_inc(s_chain, 1)
                dve.wait_ge(s_chain, count[0])

            tt, ts = dve.tensor_tensor, dve.tensor_scalar

            def clear_pads():
                for t_ in (in1, in2):
                    v = t_[:, :, :, :].rearrange("p u h n -> p (u h) n")
                    for n in (0, L + 1):
                        dve.memset(v[:, :, n:n + 1].bitcast(F), 0.0)
                for t_ in (in3, in4):
                    v = t_[:, :, :, :, :].rearrange("p u s h n -> p (u s h) n")
                    for n in (0, L + 1):
                        link(dve.memset(v[:, :, n:n + 1].bitcast(F), 0.0))

            for c in range(2):
                dve.wait_ge(s_setup_in[1 + c], 16)
                w, q = craw[c], csq[c]
                for lay, src in ((0, 0), (1, 12), (2, 6), (3, 9)):
                    for k in range(3):
                        ins = dve.scalar_tensor_tensor(out=q[:, 3 * lay + k, :], in0=w[:, src + k, :],
                                                       scalar=CONV_SCALE * CONV_SCALE, in1=w[:, src + k, :],
                                                       op0=MUL, op1=MUL)
                link(ins)
                qv = q[:, :, :].rearrange("p (l k) n -> p l k n", k=3)
                link(tt(qv[:, :, 0, :], qv[:, :, 0, :], qv[:, :, 1, :], ADD))
                link(tt(qv[:, :, 0, :], qv[:, :, 0, :], qv[:, :, 2, :], ADD))
                for lay in range(1, LAYERS):
                    link(dve.tensor_copy(q[:, lay, :], q[:, 3 * lay, :]))
            dve.wait_ge(s_sty, 1)
            dve.wait_ge(s_setup_in[0], 48)
            for c in range(2):
                for lay in range(LAYERS):
                    n = (c * LAYERS + lay) * NG
                    ins = ts(mod_s[:, c, lay, :], bank[0][:, n:n + NG], vec[:, c, 0, lay:lay + 1], None, ADD)
            link(ins)
            tt(dtmp[:, :, :, :], mod_s[:, :, :, :], mod_s[:, :, :, :], MUL).then_inc(s_sq, 1)
            dsum = dem[:, :, :, :].rearrange("p c l g -> p (c l g)")
            dve.wait_ge(s_dsum, 1)
            ts(dsum, bank[1][:, 0:2 * LAYERS * NG], EPS, None, ADD).then_inc(s_dvar, 1)
            dve.wait_ge(s_dvar, 1)
            dve.wait_ge(s_root, 1)
            root = dtmp[:, :, :, :].rearrange("p c l g -> p (c l g)")
            r2 = scl[:, :, :, :].rearrange("p c l g -> p (c l g)")
            link(dve.reciprocal(root, root))
            link(tt(r2, root, root, MUL))
            link(tt(r2, r2, dsum, MUL))
            link(ts(r2, r2, -0.5, 1.5, MUL, ADD))
            link(tt(dsum, r2, root, MUL))
            for c in range(2):
                into = [mod_s[:, c, 0, :], dem[:, c, 1, :], mod_s[:, c, 2, :], mod_s[:, c, 3, :]]
                outof = [dem[:, c, 0, :], mod_s[:, c, 1, :], dem[:, c, 2, :], dem[:, c, 3, :]]
                for lay in range(LAYERS - 1):
                    tt(scl[:, c, lay, :], outof[lay], into[lay + 1], MUL)
                    link(ts(bia[:, c, lay, :], into[lay + 1], vec[:, c, 1, lay:lay + 1],
                            2.0 if lay == 1 else 1.0, MUL, MUL))
                dve.tensor_copy(scl[:, c, 3, :], outof[3])
                link(ts(edge[:, c, :], bia[:, c, 1, :], 1.75 / 2.0, None, MUL))
            dve.wait_ge(s_const, 64)
            link(dve.tensor_copy(gateT[:, 0, :, :], gateF[:, :, :]))
            link(tt(gateT[:, 1, :, :], gateF[:, :, :], gateT[:, 0, :, :].bitcast(F), SUB))
            clear_pads()
            dve.memset(zero[:, :], 0.0).then_inc(s_zero, 1)
            dve.wait_ge(s_zero, 1)
            build_taps(dve, 0, link)
            dve.wait_ge(s_taps[0], 1)
            dve.tensor_copy(tg[:, 0, 0:1], zero[:, 0:1]).then_inc(s_scales, 1)
            dve.wait_ge(s_scales, 1)
            dve.tensor_copy(tg[:, 0, 0:1], zero[:, 0:1]).then_inc(s_pads, 1)

            STEPS = 8

            def late0(i):
                def late(k):
                    n = 0

                    def step(ins):
                        nonlocal n
                        n += 1
                        ins.then_inc(s_score, 1)
                        hold(dve, s_score, STEPS * i + n)

                    if k == 2:
                        chain_xt_low(dve, 0, i)
                    if k == 8:
                        for u in range(2):
                            g = 2 * i + u
                            dve.wait_ge(s_tanh, g + 1)
                            step(ts(sc[:, u, :], tg[:, u, :], 0.5, 0.5, MUL, ADD))
                            step(tt(sc[:, u, :], sc[:, u, :], gbias[:, :], ADD))
                            step(dve.max(m8[:, u, :], sc[:, u, :]))
                            step(dve.max_index(i8[:, u, :], m8[:, u, :], sc[:, u, :]))
                            dve.tensor_copy(topv[:, ds(g, 1), :].rearrange("p a k -> p (a k)"), m8[:, u, :])
                            dve.tensor_copy(topi[:, ds(g, 1), :].rearrange("p a k -> p (a k)"), i8[:, u, :])
                return late

            staggered(dve, chain_vector(dve, 0), late0)

            link(dve.tensor_copy(rt[8][:, :, :], con[:, C_E:C_E + E0].rearrange("p (a e) -> p a e", a=1)
                                 .broadcast_to([P, NG, E0])))
            den = small[0][:, :]
            link(dve.tensor_reduce(den, topv[:, :, 0:TOP0], AX.X, ADD))
            link(ts(den, den, 1e-20, None, ADD))
            link(dve.reciprocal(den, den))
            for k in range(TOP0):
                tt(wtok[:, :, k], topv[:, :, k], den, MUL)
                link(tt(oh[k][:, :, :], rt[8][:, :, :], topi[:, :, k:k + 1].broadcast_to([P, NG, E0]), ALU.is_equal))
            M, base, S, tmp, cnt, alt = rt[0], rt[1], rt[2], rt[3], rt[4], rt[5]
            link(tt(M[:, :, :], oh[0][:, :, :], oh[1][:, :, :], ADD))
            link(tt(M[:, :, :], M[:, :, :], oh[2][:, :, :], ADD))
            tt(M[:, :, :], M[:, :, :], oh[3][:, :, :], ADD).then_inc(s_hot, 1)
            dve.wait_ge(s_cnt, 1)
            link(dve.tensor_copy(cnt[:, :, :].rearrange("p g e -> p (g e)"), bank[1][:, 0:NG * E0]))
            src, dst, d = cnt, base, 1
            while d < NG:
                dve.tensor_copy(dst[:, 0:d, :], src[:, 0:d, :])
                link(tt(dst[:, d:NG, :], src[:, d:NG, :], src[:, 0:NG - d, :], ADD))
                src, dst, d = dst, (alt if src is cnt else src), 2 * d
            incl = src
            total = small[1][:, :]
            link(dve.tensor_copy(total, incl[:, NG - 1, :]))
            link(tt(S[:, :, :], incl[:, :, :], cnt[:, :, :], SUB))
            link(tt(S[:, :, :].rearrange("p g e -> p (g e)"), S[:, :, :].rearrange("p g e -> p (g e)"),
                    bank[0][:, 0:NG * E0], ADD))
            tiles_i, tiles_f = smalli[0][:, :], small[2][:, :]
            link(ts(small[3][:, :], total, float(P - 1), None, ADD))
            link(dve.tensor_copy(tiles_i, small[3][:, :]))
            link(ts(smalli[1][:, :], tiles_i, 7, None, ALU.logical_shift_right))
            link(dve.tensor_copy(tiles_f, smalli[1][:, :]))
            link(ts(tiles_f, tiles_f, 1.0, None, ALU.max))
            src, dst, d = small[2], small[4], 1
            while d < E0:
                dve.tensor_copy(dst[:, 0:d], src[:, 0:d])
                link(tt(dst[:, d:E0], src[:, d:E0], src[:, 0:E0 - d], ADD))
                src, dst, d = dst, (small[5] if src is small[2] else src), 2 * d
            ends = src
            starts = small[6]
            link(tt(starts[:, :], ends[:, :], tiles_f, SUB))
            first_row = small[7]
            link(ts(first_row[:, :], starts[:, :], float(P), None, MUL))
            link(tt(S[:, :, :], S[:, :, :], first_row[:, :].rearrange("p (a e) -> p a e", a=1)
                    .broadcast_to([P, NG, E0]), ADD))
            for k in range(TOP0):
                link(tt(tmp[:, :, :], oh[k][:, :, :], S[:, :, :], MUL))
                link(dve.tensor_reduce(small[8][:, :], tmp[:, :, :], AX.X, ADD))
                link(dve.tensor_copy(slot[:, :, k], small[8][:, :]))
            link(ts(small[8][:, :], total, con[:, C_P:C_P + 1], None, ADD))
            link(ts(small[9][:, :], tiles_f, float(P), None, MUL))
            link(tt(small[10][:, :], small[8][:, :], small[9][:, :], ALU.is_lt))
            link(tt(small[8][:, :], small[8][:, :], first_row[:, :], ADD))
            link(tt(small[8][:, :], small[8][:, :], con[:, C_SP:C_SP + E0], SUB))
            link(tt(small[8][:, :], small[8][:, :], small[10][:, :], MUL))
            link(tt(small[8][:, :], small[8][:, :], con[:, C_SP:C_SP + E0], ADD))
            link(dve.tensor_copy(padi[:, :], small[8][:, :]))
            t_iota = con[0:1, C_T:C_T + TILES]
            link(tt(cmp_t[:, :, :], t_iota.rearrange("p (t a) -> p t a", a=1).broadcast_to([1, TILES, E0]),
                    starts[0:1, :].rearrange("p (a e) -> p a e", a=1).broadcast_to([1, TILES, E0]), ALU.is_ge))
            dve.tensor_reduce(tabf[:, 0, :], cmp_t[:, :, :], AX.X, ADD)
            link(ts(small[11][:, 0:1], ends[:, E0 - 1:E0], -1.0, None, ADD))
            ts(tabf[:, 1, :], t_iota, small[11][0:1, 0:1], float(P), ALU.min, MUL)
            dve.memset(tabf[:, 2, E0:TILES], 0.0)
            link(ts(tabf[:, 2, 0:E0], starts[0:1, :], float(NG), None, ADD))
            dve.tensor_copy(tab[:, :, :], tabf[:, :, :]).then_inc(s_route, 1)
            dve.wait_ge(s_route, 1)

            def xt_low(h, u):
                dve.wait_ge(s_txh, 2 * h + u + 1)
                tt(xT[:, u, 1, :, :].rearrange("p c t -> p (c t)"), bank[6 + u][:, :],
                   xT[:, u, 0, :, :].rearrange("p c t -> p (c t)").bitcast(F), SUB).then_inc(s_txl, 1)

            def zt_low(h, u):
                dve.wait_ge(s_tzh, 2 * h + u + 1)
                tt(zT[:, u, 1, :, :].rearrange("p c t -> p (c t)"), bank[2 + u][:, 0:I0],
                   zT[:, u, 0, :, :].rearrange("p c t -> p (c t)").bitcast(F), SUB).then_inc(s_tzl, 1)

            def gated(h, u):
                dve.wait_ge(s_tsg, 2 * h + u + 1)
                tt(z[:, u, :], bank[u][:, I0:GU], sg[:, u, :], MUL).then_inc(s_tz, 1)

            def tiles(h0, n):
                xt_low(h0, 0)
                xt_low(h0, 1)
                gated(h0, 0)
                with dve.Fori(0, n - 1) as i:
                    h = h0 + i
                    xt_low(h + 1, 0)
                    zt_low(h, 0)
                    gated(h, 1)
                    xt_low(h + 1, 1)
                    zt_low(h, 1)
                    gated(h + 1, 0)
                h = h0 + n - 1
                zt_low(h, 0)
                gated(h, 1)
                zt_low(h, 1)

            tiles(0, NG // 2)
            tiles(NG // 2, TILES // 2)

            dve.wait_ge(s_pk, NPACK)
            dve.wait_ge(s_tdn, NG + TILES)
            clear_pads()
            dve.tensor_copy(tg[:, 0, 0:1], zero[:, 0:1]).then_inc(s_pads, 1)
            dve.sem_inc(s_fin, CREDIT)
            start1 = count[0] + 2 * TOP0
            LOW_STEPS = 12

            def combine(h, u, step):
                g = 2 * h + u
                dve.wait_ge(s_x[1][u], 16 * h + 16)
                dve.wait_ge(s_gsh[u], 16 * h + 16)
                step(tt(xrow[:, u, :], xrow[:, u, :], gath[:, u, TOP0, :], ADD))
                dve.wait_ge(s_gat[u], 16 * TOP0 * (h + 1))
                for k in range(TOP0):
                    ins = dve.scalar_tensor_tensor(out=xrow[:, u, :], in0=gath[:, u, k, :],
                                                   scalar=wtok[:, ds(g, 1), k], in1=xrow[:, u, :],
                                                   op0=MUL, op1=ADD)
                    if k < TOP0 - 1:
                        step(ins)
                ins.then_inc(s_comb, 1)

            for u in range(2):
                combine(0, u, link)
            chain1 = chain_vector(dve, 1)
            def body1(i, last, late):
                k = 0

                def step(ins):
                    nonlocal k
                    k += 1
                    ins.then_inc(s_chain, 1)
                    hold(dve, s_chain, start1 + 2 * TOP0 * i + k)

                def middle(i_):
                    for u in range(2):
                        combine(i_ + 1, u, step)

                chain1(i, last, late, middle)

            def late1(i):
                n = 0

                def step(ins):
                    nonlocal n
                    n += 1
                    ins.then_inc(s_low, 1)
                    hold(dve, s_low, LOW_STEPS * i + n)

                def largest(u):
                    dve.wait_ge(s_gate[1], 2 * i + u + 1)
                    step(dve.tensor_reduce(lg[:, u, 0:1], bank[6 + u][:, 0:E1], AX.X, ALU.max))
                    ts(lg[:, u, 1:2], lg[:, u, 0:1], -1.0, None, MUL).then_inc(s_lmax, 1)

                def weigh():
                    both = lambda a_, b_: lg[:, :, a_:b_]
                    one = lambda u, a_, b_: lg[:, u, a_:b_]
                    e_iota = con[:, C_E:C_E + E1]

                    def each(make):
                        make(0)
                        step(make(1))

                    dve.wait_ge(s_exp, 2 * i + 2)
                    step(dve.reciprocal(both(3, 4), both(2, 3)))
                    each(lambda u: ts(one(u, 16, 24), one(u, 8, 16), one(u, 3, 4), None, MUL))
                    each(lambda u: dve.max(one(u, 24, 32), one(u, 16, 24)))
                    tt(both(4, 5), both(24, 25), both(25, 26), ADD)
                    each(lambda u: dve.max_index(i8b[:, u, :], one(u, 24, 32), one(u, 16, 24)))
                    dve.reciprocal(both(5, 6), both(4, 5))
                    step(dve.tensor_copy(both(32, 40), i8b[:, :, :]))
                    each(lambda u: ts(one(u, 6, 8), one(u, 24, 26), one(u, 5, 6), None, MUL))
                    for u in range(2):
                        ts(one(u, 40, 48), e_iota, one(u, 32, 33), one(u, 6, 7), ALU.is_equal, MUL)
                    each(lambda u: ts(one(u, 48, 56), e_iota, one(u, 33, 34), one(u, 7, 8), ALU.is_equal, MUL))
                    step(tt(both(56, 64), both(40, 48), both(48, 56), ADD))
                    for u in range(2):
                        tt(hw[:, u, :].rearrange("p (e r) -> p e r", r=R1),
                           bank[6 + u][:, E1:E1 + E1 * R1].rearrange("p (e r) -> p e r", r=R1),
                           one(u, 56, 64).rearrange("p (e a) -> p e a", a=1).broadcast_to([P, E1, R1]), MUL)\
                            .then_inc(s_rw, 1)

                def rank_low(u):
                    dve.wait_ge(s_hth, 2 * i + u + 1)
                    tt(hwT[:, u, 1, :], bank[6 + u][:, HT:HT + P], hwT[:, u, 0, :].bitcast(F), SUB)\
                        .then_inc(s_htl, 1)

                def result(u):
                    dve.wait_ge(s_sum, 2 * i + u + 1)
                    dve.wait_ge(s_out[u], 16 * i + 16)
                    step(tt(yo[:, u, :], bank[6 + u][:, :], bb[:, :], ADD))
                    dve.wait_ge(s_res[u], 16 * i + 16)
                    tt(yo[:, u, :], yo[:, u, :], res[:, u, :], ADD).then_inc(s_fin, 1)

                def late(k):
                    if k == 2:
                        chain_xt_low(dve, 1, i)
                    if k == 6:
                        weigh()
                    for at_, part in ((4, largest), (10, rank_low), (BANKS, result)):
                        if k == at_:
                            for u in range(2):
                                part(u)
                return late

            staggered(dve, body1, late1)

        @block.gpsimd
        def _(pool):
            count = [0]

            def link(ins):
                count[0] += 1
                ins.then_inc(s_pchain, 1)
                pool.wait_ge(s_pchain, count[0])

            pool.wait_ge(s_setup_in[2], 16)
            pool.wait_ge(s_sq, 1)
            build_taps(pool, 1, link)
            pool.wait_ge(s_taps[1], 1)
            pool.wait_ge(s_dsum, 1)
            pool.wait_ge(s_taps[0], 1)

            def whole(number):
                return a["packs"][ds(number, 1), :, :].rearrange("a p n -> p (a n)")

            def load_pack(h, b):
                pool.dma_start(raws[b], whole(3 * h + b)).then_inc(s_raw[b], 16)

            def high_pack(h, b):
                pool.dma_start(pack[:, place(b), 0, :], whole(3 * h + b)).then_inc(s_pk_hi[b], 16)

            def split_pack(h, b):
                hold(pool, s_raw[b], 16 * h + 16)
                hold(pool, s_pk_hi[b], 16 * h + 16)
                pool.tensor_tensor(pack[:, place(b), 1, :], raws[b], pack[:, place(b), 0, :].bitcast(F), SUB)\
                    .then_inc(s_pk, 1)
                pool.wait_ge(s_pk, 3 * h + b + 1)

            pool.wait_ge(s_val[0], 1)
            for b in (0, 2):
                load_pack(0, b)
                high_pack(0, b)
            split_pack(0, 0)
            load_pack(1, 0)
            pool.wait_ge(s_conv[0], BANKS * NB)
            pool.wait_ge(s_split[0], BANKS * NB)
            pool.wait_ge(s_route, 1)
            load_pack(0, 1)
            high_pack(0, 1)
            for b in (1, 2):
                split_pack(0, b)
                load_pack(1, b)

            pool.wait_ge(s_route, 1)
            for u in range(2):
                pool.wait_ge(s_saved[u], 16 * (NB + 1))
                pool.dma_start(xrow[:, u, :], xtok[u * P:(u + 1) * P, :]).then_inc(s_pool_in[u], 16)
            for e in range(E0):
                pool.indirect_dma_start(out=xs, out_offset=bass.IndirectOffsetOnAxis(ap=padi[:, e:e + 1], axis=0),
                                        in_=zero[:, :], in_offset=None).then_inc(s_scat, 16)

            def scatters(i, last):
                for u in range(2):
                    g = 2 * i + u
                    pool.tensor_copy(idx[:, u, :], slot[:, ds(g, 1), :].rearrange("p a k -> p (a k)"))\
                        .then_inc(s_idx, 1)
                    pool.wait_ge(s_idx, g + 1)
                    hold(pool, s_pool_in[u], 16 * i + 16)
                    for k in range(TOP0):
                        pool.indirect_dma_start(out=xs,
                                                out_offset=bass.IndirectOffsetOnAxis(ap=idx[:, u, k:k + 1], axis=0),
                                                in_=xrow[:, u, :], in_offset=None).then_inc(s_scat, 16)
                    hold(pool, s_scat, 16 * (E0 + TOP0) + 16 * TOP0 * g)
                    if not last:
                        pool.dma_start(xrow[:, u, :], xtok[ds((g + 2) * P, P), :]).then_inc(s_pool_in[u], 16)

            body_loop(pool, scatters)

            def package(h, b, more):
                through = pool.value_load(tab[0:1, 2, ds(3 * h - 3 + b, 1)], min_val=NG, max_val=NG + TILES)
                hold(pool, s_tdn, through)
                high_pack(h, b)
                split_pack(h, b)
                if more:
                    load_pack(h + 1, b)

            with pool.Fori(0, NPACK // 3 - 2) as j:
                for b in range(3):
                    package(j + 1, b, True)
            for b in range(3):
                package(NPACK // 3 - 1, b, False)

            for u in range(2):
                pool.wait_ge(s_tys[u], 16 * ((NG + TILES) // 2 + 1))

            def gather(g, u):
                pool.tensor_copy(idx[:, u, :], slot[:, ds(g, 1), :].rearrange("p a k -> p (a k)"))\
                    .then_inc(s_idx, 1)
                hold(pool, s_idx, NG + g + 1)
                for k in range(TOP0):
                    pool.indirect_dma_start(out=gath[:, u, k, :], out_offset=None, in_=ys,
                                            in_offset=bass.IndirectOffsetOnAxis(ap=idx[:, u, k:k + 1], axis=0))\
                        .then_inc(s_gat[u], 16)

            for u in range(2):
                gather(u, u)
            with pool.Fori(0, NB - 1) as i:
                for u in range(2):
                    pool.wait_ge(s_comb, 2 * i + u + 1)
                    gather(2 * i + 2 + u, u)



def laid_out(x, cond_512, w):
    f = np.float32
    arr = {}
    arr["x"] = np.ascontiguousarray(x).reshape(NG, P, L)
    con = np.zeros((P, C_END), f)
    con[:, C_ID:C_ID + P] = np.eye(P)
    con[:, C_TRI:C_TRI + P] = np.triu(np.ones((P, P)), 1)
    con[:, C_ONE:C_ONE + P] = 1
    con[:, C_E:C_E + E0] = np.arange(E0)
    con[:, C_T:C_T + TILES] = np.arange(TILES)
    con[:, C_P] = np.arange(P)
    con[:, C_SP:C_SP + E0] = SPARE + np.arange(E0) * P + np.arange(P)[:, None]
    arr["consts"] = con
    arr["style_t"] = np.ascontiguousarray(cond_512.T)
    mod = np.zeros((STYLE, 2, LAYERS, SPG, P), f)
    vec = np.zeros((P, 2, 2, LAYERS), f)
    for c in range(2):
        mw, mb = w[f"L{c}_cond_mod_w"], w[f"L{c}_cond_mod_b"]
        for b in range(SPG):
            mod[:, c, :, b, b * C:(b + 1) * C] = mw.transpose(2, 0, 1)
            vec[b * C:(b + 1) * C, c, 0, :] = mb.T
            vec[b * C:(b + 1) * C, c, 1, :] = w[f"L{c}_cond_biases"].T
        cw = w[f"L{c}_cond_weights"]
        conv = np.zeros((P, 15, P), f)
        for n, (layer, turned) in enumerate(((0, 1), (1, 0), (2, 1), (3, 1), (1, 1))):
            for k in range(TAPS):
                m = cw[layer, :, :, k].T if turned else cw[layer, :, :, k]
                for b in range(SPG):
                    conv[b * C:(b + 1) * C, 3 * n + k, b * C:(b + 1) * C] = m
        arr[f"conv{c}"] = conv
    arr["mod_t"], arr["vecs"] = mod, vec

    def rows(m, chunks):
        return m.reshape(chunks, P, -1).transpose(1, 0, 2)

    arr["gate_t"] = np.ascontiguousarray(rows(w["L0_ffn_gate_w"].T, HC))
    arr["gate_bias"] = np.ascontiguousarray(np.broadcast_to(w["L0_ffn_bias"], (P, E0)))
    arr["base_bias"] = np.ascontiguousarray(np.broadcast_to(w["L1_ffn_b_base"], (P, L)))
    packs = np.zeros((NPACK, P, PACK), f)

    def expert(m, wg, wu, wd):
        gu = np.concatenate([rows(wg.T, HC), rows(wu.T, HC)], axis=2)
        packs[m, :, 0:DOWN] = gu.reshape(P, -1)
        packs[m, :, DOWN:DOWN + IC * L] = rows(wd.T, IC).reshape(P, -1)

    expert(0, w["L0_ffn_Sg"], w["L0_ffn_Su"], w["L0_ffn_Sd"])
    for e in range(E0):
        expert(1 + e, w["L0_ffn_Wg"][e], w["L0_ffn_Wu"][e], w["L0_ffn_Wd"][e])
    low = np.concatenate([w["L1_ffn_W_gate"], w["L1_ffn_A"].reshape(E1 * R1, L)], axis=0)
    packs[NPACK - 1] = np.concatenate([
        rows(w["L1_ffn_W_base"].T, HC).reshape(P, -1), rows(low.T, HC).reshape(P, -1),
        w["L1_ffn_B"].transpose(0, 2, 1).reshape(E1 * R1, L)], axis=1)
    arr["packs"] = packs
    return arr


def kernel(x, cond_512, **weights):
    import concourse.bacc as bacc
    from concourse.bass_utils import run_bass_kernel_spmd

    w = {k: np.asarray(v) for k, v in weights.items()}
    arrays = laid_out(np.asarray(x), np.asarray(cond_512), w)
    nc = bacc.Bacc("TRN2", target_bir_lowering=False, num_devices=1)
    a = {k: nc.dram_tensor(f"in_{k}", v.shape, mybir.dt.float32, kind="ExternalInput").ap()
         for k, v in arrays.items()}
    out = nc.dram_tensor("out", (NG * P, L), mybir.dt.float32, kind="ExternalOutput").ap()
    build(nc, a, out)
    r = run_bass_kernel_spmd(nc, [{f"in_{k}": v for k, v in arrays.items()}], core_ids=[0])
    return r.results[0]["out"].reshape(B, C, L)
```

```python
import numpy as np
from contextlib import ExitStack

import concourse.bass as bass
import concourse.mybir as mybir

P = 128
B, C, L = 64, 32, 512
SPG = P // C
NG = B * C // P
STYLE, LAYERS, TAPS = 64, 4, 3
NTAP = 17
HC = L // P
E0, TOP0, I0 = 16, 4, 256
IC = I0 // P
E1, R1, TOP1 = 8, 16, 2
GU = 2 * I0
NA = E1 + E1 * R1
PACK = HC * (L + NA) + L
DOWN = HC * GU
NPACK = 1 + E0 + 1
TILES = NG * TOP0 + E0
CAP = NG * P
SPARE = E0 * CAP
ROWS = SPARE + E0 * P
PADDED = L + 2
CONV_SCALE = 1.0 / float(np.sqrt(C * TAPS ** 2))
EPS = 1e-8
BLUR = 0.125

C_ID = 0
C_E = P
C_P = C_E + E0
C_SP = C_P + 1
C_FIRST = C_SP + E0
C_TRI = (C_FIRST + E0 + 7) // 8 * 8
C_ONE = C_TRI + P
C_T = C_ONE + P
C_END = C_T + TILES


def build(nc, a, out):
    F, R, I, U = mybir.dt.float32, mybir.dt.float32r, mybir.dt.int32, mybir.dt.uint32
    ALU, ACT, AX = mybir.AluOpType, mybir.ActivationFunctionType, mybir.AxisListType
    ADD, SUB, MUL = ALU.add, ALU.subtract, ALU.mult
    ds = bass.ds

    ctx = ExitStack()
    with ctx:
        top = [nc.sbuf_base]

        def at(name, shape, dt, offset=None):
            size = int(np.prod(shape[1:])) * 4
            if offset is None:
                offset = (top[0] + 31) // 32 * 32
                top[0] = offset + size
            return nc.alloc_sbuf_tensor_at(name, shape, dt, offset=offset), offset

        def new(name, shape, dt=F):
            return at(name, shape, dt)[0]

        taps = [new(f"taps{c}", [P, 2, NTAP, P], R) for c in range(2)]
        in1, in1_at = at("in1", [P, 2, 2, PADDED], R)
        in2 = new("in2", [P, 2, 2, PADDED], R)
        in3, in3_at = at("in3", [P, 2, 2, 2, PADDED], R)
        in4, in4_at = at("in4", [P, 2, 2, 2, PADDED], R)
        SLOT = 2 * PACK
        in34_end = top[0]
        pack, pack_at = at("pack", [P, 3, 2, PACK], R, (in34_end - SLOT * 4) // 32 * 32)
        assert pack_at >= in3_at
        top[0] = pack_at + 3 * SLOT * 4
        rawp, rawp_at = at("rawp", [P, 2, PACK], F)
        raw1, _ = at("raw1", [P, PACK], F, in1_at)
        assert in1_at + PACK * 4 <= in3_at
        raws = [rawp[:, 0, :], raw1[:, :], rawp[:, 1, :]]
        val, val_at = at("val", [P, 2, PADDED], F)
        pair_odd = new("pair_odd", [P, L + 2])
        xrow, xrow_at = at("xrow", [P, 2, L], F)
        crow, crow_at = at("crow", [P, 2, L], F)
        xT = new("xT", [P, 2, 2, HC, P], R)
        tin, tin_at = at("tin", [P, 2, L], F)
        sg, sg_at = at("sg", [P, 2, I0], F)
        pair_even = at("pair_even", [P, L], F, sg_at)[0]
        z, z_at = at("z", [P, 2, I0], F)
        zT, zT_at = at("zT", [P, 2, 2, IC, P], R)
        ty = at("ty", [P, 2, L], F, crow_at)[0]
        con, con_at = at("con", [P, C_END], F)
        ident = con[:, C_ID:C_ID + P]
        vec = new("vec", [P, 2, 2, LAYERS])
        styl = new("styl", [STYLE, B])
        mod_s = new("mod_s", [P, 2, LAYERS, NG])
        dem = new("dem", [P, 2, LAYERS, NG])
        dtmp = new("dtmp", [P, 2, LAYERS, NG])
        scl = new("scl", [P, 2, LAYERS, NG])
        bia = new("bia", [P, 2, LAYERS, NG])
        edge = new("edge", [P, 2, NG])
        gateF = new("gateF", [P, HC, E0])
        gateT = new("gateT", [P, 2, HC, E0], R)
        gbias = new("gbias", [P, E0])
        logit = new("logit", [P, 2, E0])
        tg = new("tg", [P, 2, E0])
        sc = new("sc", [P, 2, E0])
        m8 = new("m8", [P, 2, 8])
        i8 = new("i8", [P, 2, 8], U)
        topv = new("topv", [P, NG, 8])
        topi = new("topi", [P, NG, TOP0])
        slots_f = new("slots_f", [P, NG, TOP0])
        moved = new("moved", [P, NG, TOP0])
        yslot = new("yslot", [P, NG, TOP0], I)
        itop = new("itop", [P, 2, 8])
        hot = new("hot", [P, 2, TOP0, E0])
        picked = new("picked", [P, 2, E0])
        before = new("before", [P, E0])
        rank = new("rank", [P, 2, E0])
        slotf = new("slotf", [P, 2, TOP0])
        prow, prow_at = at("prow", [P, 2, L], F)
        counts = new("counts", [P, E0])
        plan = new("plan", [P, 10, E0])
        plani = new("plani", [P, 2, E0], I)
        wsum = new("wsum", [P, NG])
        wtok = new("wtok", [P, NG, TOP0])
        wnow = new("wnow", [P, 2, TOP0])
        slot = new("slot", [P, NG, TOP0], I)
        padi = new("padi", [P, E0], I)
        tabf = new("tabf", [1, 3, TILES])
        tab = new("tab", [1, 3, TILES], I)
        idx = new("idx", [P, 2, TOP0], I)
        bb = new("bb", [P, L])
        lg = new("lg", [P, 2, 64])
        i8b = new("i8b", [P, 2, 8], U)
        nil = new("nil", [P, 1])
        warm = new("warm", [P, 2])
        o = in34_end
        craw, cf, cu, csq = [], [], [], []
        for c in range(2):
            t_, o_ = at(f"craw{c}", [P, 15, P], F, o); craw.append(t_); o += 15 * P * 4
            t_, o_ = at(f"cf{c}", [P, NTAP, P], F, o); cf.append(t_); o += NTAP * P * 4
            t_, o_ = at(f"cu{c}", [P, 3, TAPS, P], F, o); cu.append(t_); o += 9 * P * 4
            t_, o_ = at(f"csq{c}", [P, 12, P], F, o); csq.append(t_); o += 12 * P * 4
        assert o <= rawp_at + 2 * PACK * 4, (o, rawp_at + 2 * PACK * 4)
        modT, _ = at("modT", [STYLE, 2, LAYERS, SPG, P], F, in3_at)
        low = at("low", [P, 2, NA], F, con_at + C_TRI * 4)[0]
        assert 2 * NA <= C_END - C_TRI
        res = at("res", [P, 2, L], F, tin_at)[0]
        hw = at("hw", [P, 2, P], F, z_at)[0]
        hwT = at("hwT", [P, 2, 2, P], R, zT_at)[0]
        yo = at("yo", [P, 2, L], F, prow_at)[0]
        hot_all = at("hot_all", [P, NG, TOP0, E0], F, val_at)[0]
        zero = at("zero", [P, L], F, xrow_at + L * 4)[0]
        cmp_t = at("cmp_t", [1, TILES, E0], F, val_at)[0]
        gath = at("gath", [P, 2, TOP0 + 1, L], F, rawp_at)[0]
        assert top[0] <= nc.sbuf_usable_end, (top[0], nc.sbuf_usable_end)

        bank = [ctx.enter_context(nc.psum_tensor(f"bank{k}", [P, 512], F)) for k in range(8)]

        xtok = nc.dram_tensor("token_x", (NG * P, L), F).ap()
        ytok = nc.dram_tensor("token_y", (NG * P, L), F).ap()
        xs = nc.dram_tensor("sorted_x", (ROWS, L), F).ap()
        ys = nc.dram_tensor("tile_y", (TILES * P, L), F).ap()
        x1d = nc.dram_tensor("x1_rows", (NG * P, L), F).ap()

        LAST = 4
        RANK = P
        HT = 3 * P

        def place(package):
            return (package + 2) % 3

        def hold(eng, semaphore, count):
            eng.wait_ge(semaphore, count)
            eng.nop(nofuse=True)

        def wait(eng, semaphore, count):
            eng.wait_ge(semaphore, count)

        def sem(name):
            return ctx.enter_context(nc.semaphore(name))

        s_setup_in = [sem(f"setup_in{k}") for k in range(3)]
        s_const = sem("const_in")
        s_chain = sem("dve_chain")
        s_pchain = sem("pool_chain")
        s_sty = sem("style_sums")
        s_squared = sem("weights_squared")
        s_sq = sem("style_squares")
        s_dsum = sem("demod_sums")
        s_dvar = sem("demod_var")
        s_root = sem("demod_root")
        s_scales = sem("scales_ready")
        s_taps = [sem(f"taps_ready{c}") for c in range(2)]
        s_pads = sem("pads_zeroed")
        s_x = [[sem(f"x_loaded{c}{u}") for u in range(2)] for c in range(2)]
        s_val = [sem(f"val_ready{c}") for c in range(2)]
        s_pairs = [sem(f"position_pairs{c}") for c in range(2)]
        s_hi = [sem(f"high_part{c}") for c in range(2)]
        s_split = [sem(f"split_done{c}") for c in range(2)]
        s_conv = [sem(f"conv_bank{c}") for c in range(2)]
        s_crow = [sem(f"crow_ready{c}") for c in range(2)]
        s_xt = [sem(f"xt_bank{c}") for c in range(2)]
        s_xth = [sem(f"xt_high{c}") for c in range(2)]
        s_xtl = [sem(f"xt_low{c}") for c in range(2)]
        s_gate = [sem(f"gate_sums{c}") for c in range(2)]
        s_logit = sem("gate_logits")
        s_tanh = sem("gate_tanh")
        s_score = sem("score_steps")
        s_low = sem("low_rank_steps")
        s_saved = [sem(f"crow_saved{u}") for u in range(2)]
        s_hot = sem("one_hots")
        s_rank = sem("ranks")
        s_slots = sem("slots_ready")
        s_padi = sem("padding_rows")
        s_yslot = sem("result_rows")
        s_cnt = sem("counts_summed")
        s_route = sem("routing_ready")
        s_pool_in = [sem(f"scatter_rows_in{u}") for u in range(2)]
        s_idx = sem("index_columns")
        s_scat = [sem(f"scattered{u}") for u in range(2)]
        s_padded = sem("padding_scattered")
        s_zero = sem("zero_rows")
        s_raw = [sem(f"raw_pack_in{u}") for u in range(3)]
        s_pk_hi = [[sem(f"pack_high{u}{k}") for k in range(2)] for u in range(3)]
        s_pk = sem("pack_ready")
        s_tx = [sem(f"tile_in{u}") for u in range(2)]
        s_txt = sem("tile_xt")
        s_txh = sem("tile_xt_high")
        s_txl = sem("tile_xt_low")
        s_tup = sem("tile_up")
        s_tsg = sem("tile_silu")
        s_tz = sem("tile_z")
        s_tzt = sem("tile_zt")
        s_tzh = sem("tile_zt_high")
        s_tzl = sem("tile_zt_low")
        s_tdn = sem("tile_down")
        s_ty = sem("tile_y")
        s_tys = [sem(f"tile_saved{u}") for u in range(2)]
        s_gsh = [sem(f"shared_rows_in{u}") for u in range(2)]
        s_gat = [sem(f"gathered{u}") for u in range(2)]
        s_first = [[sem(f"first_gathered{u}{k}") for k in range(TOP0)] for u in range(2)]
        s_comb = sem("combined")
        s_x1s = [sem(f"x1_saved{u}") for u in range(2)]
        s_res = [sem(f"residual_in{u}") for u in range(2)]
        s_xsum = sem("x_and_shared_rows")
        s_bias = sem("residual_and_bias")
        s_lmax = sem("logit_max")
        s_exp = sem("logit_exp")
        s_rw = sem("low_rank_weighted")
        s_ht = sem("low_rank_transposed")
        s_hth = sem("low_rank_high")
        s_htl = sem("low_rank_low")
        s_sum = sem("layer1_sums")
        s_fin = sem("out_rows")
        s_out = [sem(f"out_saved{u}") for u in range(2)]

        block = ctx.enter_context(nc.Block())

        NB = NG // 2
        BANKS = 12
        CREDIT = 2

        def nothing(k):
            pass

        def staggered(eng, body, late):
            body(0, False, nothing)
            with eng.Fori(1, NB - 1) as i:
                body(i, False, late(i - 1))
            body(NB - 1, True, late(NB - 2))

        @block.sync
        def _(sp):
            sp.dma_start(con[:, :], a["consts"]).then_inc(s_const, 16)
            sp.dma_start(styl[:, :], a["style_t"]).then_inc(s_setup_in[0], 16)
            sp.dma_start(modT[:, :, :, :, :], a["mod_t"]).then_inc(s_setup_in[0], 16)
            sp.dma_start(vec[:, :, :, :], a["vecs"]).then_inc(s_setup_in[0], 16)
            sp.dma_start(craw[0][:, :, :], a["conv0"]).then_inc(s_setup_in[1], 16)
            sp.dma_start(craw[1][:, :, :], a["conv1"]).then_inc(s_setup_in[2], 16)
            sp.dma_start(gateF[:, :, :], a["gate_t"]).then_inc(s_const, 16)
            sp.dma_start(gbias[:, :], a["gate_bias"]).then_inc(s_const, 16)
            sp.dma_start(bb[:, :], a["base_bias"]).then_inc(s_const, 16)
            for g in range(2):
                sp.dma_start(xrow[:, g, :], a["x"][g]).then_inc(s_x[0][g], 16)
            for u in range(2):
                sp.sem_inc(s_saved[u], 16)

            def chain0(i, last):
                if not last:
                    for u in range(2):
                        sp.wait_ge(s_val[0], BANKS * i + 1 + u)
                        sp.dma_start(xrow[:, u, :], a["x"][ds(2 * i + 2 + u, 1), :, :].rearrange("a p l -> p (a l)"))\
                          .then_inc(s_x[0][u], 16)
                for u in range(2):
                    sp.wait_ge(s_crow[0], 2 * i + u + 1)
                    sp.dma_start(xtok[ds((2 * i + u) * P, P), :], crow[:, u, :]).then_inc(s_saved[u], 16)

            with sp.Fori(0, NB - 1) as i:
                chain0(i, False)
            def load(h, u, src, row, free=True):
                if free:
                    sp.wait_ge(s_txt, 2 * h + u - 1)
                sp.dma_start(tin[:, u, :], src[ds(row, P), :]).then_inc(s_tx[u], 16)

            for u in range(2):
                sp.wait_ge(s_saved[u], 16 * NB)
                load(0, u, xtok, u * P, free=False)
            chain0(NB - 1, True)
            for u in range(2):
                sp.wait_ge(s_saved[u], 16 * (NB + 1))
            with sp.Fori(0, NG // 2 - 1) as i:
                for u in range(2):
                    load(i + 1, u, xtok, (2 * i + 2 + u) * P)
            sp.wait_ge(s_route, 1)
            for u in range(2):
                sp.wait_ge(s_scat[u], 16 * TOP0 * NB)
            sp.wait_ge(s_padded, 16 * E0)

            def block_of(t):
                return sp.value_load(tab[0:1, 1, ds(t, 1)], min_val=0, max_val=SPARE - P)

            for u in range(2):
                load(NG // 2, u, xs, block_of(u))
            with sp.Fori(0, TILES // 2 - 1) as i:
                for u in range(2):
                    load(NG // 2 + i + 1, u, xs, block_of(2 * i + 2 + u))

            sp.wait_ge(s_pk, 2 * NPACK)

            def load1(g, u):
                sp.dma_start(xrow[:, u, :], a["x"][ds(g, 1), :, :].rearrange("a p l -> p (a l)"))\
                  .then_inc(s_x[1][u], 16)
                sp.dma_start(gath[:, u, TOP0, :], ytok[ds(g * P, P), :]).then_inc(s_gsh[u], 16)

            def keep_x1(g, u):
                sp.wait_ge(s_comb, g + 1)
                sp.dma_start(x1d[ds(g * P, P), :], xrow[:, u, :]).then_inc(s_x1s[u], 16)

            for u in range(2):
                load1(u, u)
            for u in range(2):
                keep_x1(u, u)
            for u in range(2):
                sp.sem_inc(s_out[u], 16)

            def residual(i):
                for u in range(2):
                    hold(sp, s_x1s[u], 16 * i + 16)
                    sp.wait_ge(s_fin, 2 * i + u + 1)
                    sp.dma_start(res[:, u, :], x1d[ds((2 * i + u) * P, P), :]).then_inc(s_res[u], 16)

            def store_out(i):
                for u in range(2):
                    sp.wait_ge(s_fin, 2 * i + u + 1 + CREDIT)
                    sp.dma_start(out[ds((2 * i + u) * P, P), :], yo[:, u, :]).then_inc(s_out[u], 16)

            def next_in(i):
                for u in range(2):
                    hold(sp, s_x1s[u], 16 * i + 16)
                    sp.wait_ge(s_val[1], BANKS * i + 1 + u)
                    load1(2 * i + 2 + u, u)
                for u in range(2):
                    keep_x1(2 * i + 2 + u, u)

            next_in(0)
            with sp.Fori(1, NB - 1) as i:
                residual(i - 1)
                next_in(i)
                store_out(i - 1)
            for i in (NB - 2, NB - 1):
                residual(i)
                store_out(i)
            for u in range(2):
                sp.wait_ge(s_out[u], 16 * (NB + 1))

        def chain_scalar(act, c):
            def body(i, last, late):
                k = 0
                for layer, u, h in ([(0, 0, 0), (0, 1, 0)] + [(1, u, h) for u in range(2) for h in range(2)]
                                    + [(2, u, h) for u in range(2) for h in range(2)]):
                    g = 2 * i + u
                    k += 1
                    b = bank[BANK_OF[layer][u][h]]
                    if (layer, u) == (2, 1):
                        act.wait_ge(s_pairs[c], 2 * i + 1)
                    else:
                        act.wait_ge(s_split[c], BANKS * i + k)
                    hold(act, s_conv[c], BANKS * i + k)
                    v = val[:, (k + 1) % 2, 1:L + 1]
                    s_, b_ = scl[:, c, layer, ds(g, 1)], bia[:, c, layer, ds(g, 1)]
                    if layer == 1:
                        one, rest = (0, slice(1, L)) if h == 0 else (L - 1, slice(0, L - 1))
                        act.activation(v[:, one:one + 1], b[:, one:one + 1], ACT.Identity, scale=s_,
                                       bias=edge[:, c, ds(g, 1)])
                        act.activation(v[:, rest], b[:, rest], ACT.Identity, scale=s_, bias=b_)\
                           .then_inc(s_val[c], 1)
                    else:
                        act.activation(v, b[:, :], ACT.Identity, scale=s_, bias=b_).then_inc(s_val[c], 1)
                    late(k)
                if not last:
                    for u in range(2):
                        k += 1
                        act.wait_ge(s_pairs[c], 2 * i + 2)
                        act.wait_ge(s_x[c][u], 16 * i + 32)
                        if c == 1:
                            act.wait_ge(s_comb, 2 * i + 3 + u)
                        act.activation(val[:, (k + 1) % 2, 1:L + 1], xrow[:, u, :], ACT.Copy,
                                       scale=mod_s[:, c, 0, ds(2 * i + 2 + u, 1)]).then_inc(s_val[c], 1)
                for u in range(2):
                    if c == 0:
                        act.wait_ge(s_saved[u], 16 * i + 16)
                    hold(act, s_conv[c], BANKS * i + 11 + u)
                    act.activation(crow[:, u, :], bank[BANK_OF[3][u][0]][:, :], ACT.Identity,
                                   scale=scl[:, c, 3, ds(2 * i + u, 1)], bias=vec[:, c, 1, 3:4])\
                       .then_inc(s_crow[c], 1)

            for u in range(2):
                act.wait_ge(s_x[c][u], 16)
                if c == 1:
                    act.wait_ge(s_comb, u + 1)
                act.activation(val[:, u, 1:L + 1], xrow[:, u, :], ACT.Copy, scale=mod_s[:, c, 0, u:u + 1])\
                   .then_inc(s_val[c], 1)
            return body

        def chain_xt_high(act, c, i):
            for u in range(2):
                act.wait_ge(s_xt[c], 2 * i + u + 1)
                act.activation(xT[:, u, 0, :, :].rearrange("p c t -> p (c t)"), bank[6 + u][:, :], ACT.Copy)\
                   .then_inc(s_xth[c], 1)

        BANK_OF = {0: [[0], [1]], 1: [[2, 3], [4, 5]], 2: [[0, 1], [2, 3]], 3: [[4], [5]]}

        def split_of(dve, c, n, src, dst):
            dve.tensor_copy(dst(0), src).then_inc(s_hi[c], 1)
            dve.wait_ge(s_hi[c], n)
            dve.tensor_tensor(dst(1), src, dst(0).bitcast(F), SUB).then_inc(s_split[c], 1)

        def split(dve, c, n, slot_, dst):
            dve.wait_ge(s_val[c], n)
            split_of(dve, c, n, val[:, slot_, 1:L + 1], dst)

        def pair_split(dve, c, i, u):
            n = BANKS * i + 9 + 2 * u
            even, odd = val[:, 0, :], val[:, 1, :]
            dve.wait_ge(s_val[c], n + 1)
            dve.wait_ge(s_split[c], n - 1)
            dve.tensor_tensor(pair_even[:, :], even[:, 1:L + 1], odd[:, 1:L + 1], ADD)
            dve.tensor_tensor(pair_odd[:, 0:L + 1], odd[:, 0:L + 1], even[:, 1:L + 2], ADD).then_inc(s_pairs[c], 1)
            dve.wait_ge(s_pairs[c], 2 * i + u + 1)
            split_of(dve, c, n, pair_even[:, :], lambda p: in4[:, u, 0, p, 1:L + 1])
            split_of(dve, c, n + 1, pair_odd[:, 0:L + 1], lambda p: in4[:, u, 1, p, 0:L + 1])

        def chain_xt_low(dve, c, i):
            for u in range(2):
                dve.wait_ge(s_xth[c], 2 * i + u + 1)
                dve.tensor_tensor(xT[:, u, 1, :, :].rearrange("p c t -> p (c t)"), bank[6 + u][:, :],
                                  xT[:, u, 0, :, :].rearrange("p c t -> p (c t)").bitcast(F), SUB)\
                   .then_inc(s_xtl[c], 1)

        def chain_vector(dve, c, ahead=None):
            def dst1(u):
                return lambda p: in1[:, u, p, 1:L + 1]

            def body(i, last, late, middle=None):
                k = 0
                for dst in ([(lambda p, u=u: in2[:, u, p, 1:L + 1]) for u in range(2)]
                            + [(lambda p, u=u, h=h: in3[:, u, h, p, 1:L + 1]) for u in range(2) for h in range(2)]):
                    k += 1
                    split(dve, c, BANKS * i + k + 2, (k + 1) % 2, dst)
                    late(k)
                for u in range(2):
                    k += 2
                    pair_split(dve, c, i, u)
                    late(k)
                if not last:
                    if middle:
                        middle(i)
                    for u in range(2):
                        k += 1
                        split(dve, c, BANKS * i + k + 2, (k + 1) % 2, dst1(u))
                late(BANKS)

            for u in range(2):
                if ahead:
                    ahead(u)
                split(dve, c, u + 1, u, dst1(u))
            return body

        PARTS = ((0, 0), (0, 1), (1, 0))

        def products(pe, dst, terms, start=True, stop=True):
            n = len(terms) * len(PARTS)
            k = 0
            for lhs, rhs in terms:
                for p, q in PARTS:
                    mm = pe.matmul(dst, lhs(p), rhs(q), start=start and k == 0, stop=stop and k == n - 1)
                    k += 1
            return mm

        def products_aside(pe, dst, terms):
            for n, (lhs, rhs) in enumerate(terms):
                pe.matmul(dst, lhs(0), rhs(slice(0, 2)), start=n == 0, stop=False)
                mm = pe.matmul(dst[:, 0, :], lhs(1), rhs(0), start=False, stop=n == len(terms) - 1)
            return mm

        def chain_tensor(pe, c):
            def tap(n):
                return lambda p: taps[c][:, p, n, :]

            def body(i, last, late):
                for u in range(2):
                    pe.wait_ge(s_split[c], BANKS * i + 1 + u)
                    products(pe, bank[BANK_OF[0][u][0]][:, :],
                             [(tap(k), lambda p, u=u, k=k: in1[:, u, p, k:k + L]) for k in range(TAPS)])\
                        .then_inc(s_conv[c], 1)
                    late(1 + u)
                for u in range(2):
                    pe.wait_ge(s_split[c], BANKS * i + 3 + u)
                    for h in range(2):
                        products(pe, bank[BANK_OF[1][u][h]][:, :],
                                 [(tap(3 + 4 - 2 * k + h), lambda p, u=u, k=k: in2[:, u, p, k:k + L])
                                  for k in range(TAPS)]).then_inc(s_conv[c], 1)
                    late(4 + 2 * u)
                for u in range(2):
                    pe.wait_ge(s_split[c], BANKS * i + 6 + 2 * u)
                    for h, where in ((0, ((1, 0), (0, 1), (1, 1))), (1, ((0, 1), (1, 1), (0, 2)))):
                        products(pe, bank[BANK_OF[2][u][h]][:, :],
                                 [(tap(9 + k), lambda p, u=u, s=s, q=q: in3[:, u, s, p, q:q + L])
                                  for k, (s, q) in enumerate(where)]).then_inc(s_conv[c], 1)
                        late(7 + 2 * u + h)
                for u in range(2):
                    pe.wait_ge(s_split[c], BANKS * i + 10 + 2 * u)
                    products(pe, bank[BANK_OF[3][u][0]][:, :],
                             [(tap(12 + k), lambda p, u=u, s=s, q=q: in4[:, u, s, p, q:q + L])
                              for k, (s, q) in enumerate(((0, 0), (1, 0), (0, 1), (1, 1), (0, 2)))]).then_inc(s_conv[c], 1)
                    late(11 + u)
            return body

        def chain_turn(pe, c, i):
            for u in range(2):
                if c == 0:
                    pe.wait_ge(s_slots, i + 1)
                else:
                    pe.wait_ge(s_fin, 2 * i + u + 1)
                pe.wait_ge(s_crow[c], 2 * i + u + 1)
                for j in range(HC):
                    mm = pe.transpose(bank[6 + u][:, j * P:(j + 1) * P], crow[:, u, j * P:(j + 1) * P], ident)
                mm.then_inc(s_xt[c], 1)

        def XT(u):
            return [(lambda p, j=j: xT[:, u, p, j, :]) for j in range(HC)]

        @block.scalar
        def _(act):
            for c in range(2):
                act.wait_ge(s_setup_in[1 + c], 16)
                for lay, src in ((0, 0), (1, 12), (2, 6), (3, 9)):
                    ins = act.activation(csq[c][:, 3 * lay:3 * lay + 3, :], craw[c][:, src:src + 3, :], ACT.Square,
                                         scale=CONV_SCALE)
                ins.then_inc(s_squared, 1)
            act.wait_ge(s_sq, 1)
            chain0 = chain_scalar(act, 0)
            act.wait_ge(s_dvar, 1)
            act.activation(dtmp[:, :, :, :], dem[:, :, :, :], ACT.Sqrt).then_inc(s_root, 1)
            act.wait_ge(s_scales, 1)

            def gate_tanh(i):
                act.wait_ge(s_logit, i + 1)
                act.activation(tg[:, :, :], logit[:, :, :], ACT.Tanh, scale=0.5).then_inc(s_tanh, 1)

            def late0(i):
                def late(k):
                    if k == 2:
                        chain_xt_high(act, 0, i)
                    if k == 4:
                        gate_tanh(i)
                return late

            act.wait_ge(s_const, 64)
            act.activation(warm[:, 0:1], ident[:, 0:1], ACT.Tanh)
            staggered(act, chain0, late0)
            chain_xt_high(act, 0, NB - 1)
            gate_tanh(NB - 1)

            act.sem_inc(s_ty, CREDIT)

            def xt_high(h, u):
                act.wait_ge(s_txt, 2 * h + u + 1)
                act.activation(xT[:, u, 0, :, :].rearrange("p c t -> p (c t)"), bank[6 + u][:, :], ACT.Copy)\
                   .then_inc(s_txh, 1)

            def zt_high(h, u):
                act.wait_ge(s_tzt, 2 * h + u + 1)
                act.activation(zT[:, u, 0, :, :].rearrange("p c t -> p (c t)"), bank[2 + u][:, 0:I0], ACT.Copy)\
                   .then_inc(s_tzh, 1)

            def silu(h, u):
                act.wait_ge(s_tup, 2 * h + u + 1)
                act.activation(sg[:, u, :], bank[u][:, 0:I0], ACT.Silu).then_inc(s_tsg, 1)

            def rows(h, u):
                act.wait_ge(s_tdn, 2 * h + u + 1)
                act.wait_ge(s_tys[u], 16 * h + 16)
                act.activation(ty[:, u, :], bank[4 + u][:, :], ACT.Copy).then_inc(s_ty, 1)

            for u in range(2):
                act.sem_inc(s_tys[u], 16)

            def save(h, u, dst, k):
                hold(act, s_ty, 2 * h + u + 1 + CREDIT)
                act.dma_start(dst[ds(k * P, P), :], ty[:, u, :]).then_inc(s_tys[u], 16)

            def tiles(h0, n, dst):
                xt_high(h0, 0)
                xt_high(h0, 1)
                silu(h0, 0)
                with act.Fori(0, n - 1) as i:
                    h = h0 + i
                    xt_high(h + 1, 0)
                    zt_high(h, 0)
                    silu(h, 1)
                    rows(h, 0)
                    xt_high(h + 1, 1)
                    save(h, 0, dst, 2 * i)
                    zt_high(h, 1)
                    silu(h + 1, 0)
                    rows(h, 1)
                    save(h, 1, dst, 2 * i + 1)
                h = h0 + n - 1
                zt_high(h, 0)
                silu(h, 1)
                rows(h, 0)
                save(h, 0, dst, 2 * n - 2)
                zt_high(h, 1)
                rows(h, 1)
                save(h, 1, dst, 2 * n - 1)

            tiles(0, NG // 2, ytok)
            tiles(NG // 2, TILES // 2, ys)

            def late1(i):
                def late(k):
                    if k == 2:
                        chain_xt_high(act, 1, i)
                    if k == 4:
                        for u in range(2):
                            act.wait_ge(s_lmax, i + 1)
                            act.activation(lg[:, u, 8:16], low[:, u, 0:E1], ACT.Exp, bias=lg[:, u, 1:2],
                                           accum_out=lg[:, u, 2:3]).then_inc(s_exp, 1)
                    if k == 8:
                        for u in range(2):
                            act.wait_ge(s_ht, 2 * i + u + 1)
                            act.activation(hwT[:, u, 0, :], bank[6 + u][:, HT:HT + P], ACT.Copy).then_inc(s_hth, 1)
                return late

            act.activation(warm[:, 1:2], ident[:, 0:1], ACT.Exp)
            staggered(act, chain_scalar(act, 1), late1)
            rest = late1(NB - 1)
            for k in range(BANKS + 1):
                rest(k)

        @block.tensor
        def _(pe):
            pe.wait_ge(s_setup_in[0], 48)
            sview = styl[:, :].rearrange("k (g b) -> k b g", b=SPG)
            for c in range(2):
                for layer in range(LAYERS):
                    for b in range(SPG):
                        mm = pe.matmul(bank[0][:, (c * LAYERS + layer) * NG:(c * LAYERS + layer + 1) * NG],
                                       modT[:, c, layer, b, :], sview[:, b, :], start=b == 0, stop=b == SPG - 1)
            mm.then_inc(s_sty, 1)
            pe.wait_ge(s_sq, 1)
            for c in range(2):
                for layer in range(LAYERS):
                    n = (c * LAYERS + layer) * NG
                    mm = pe.matmul(bank[7][:, n:n + NG], csq[c][:, 3 * layer, :], dtmp[:, c, layer, :],
                                   start=True, stop=True)
            mm.then_inc(s_dsum, 1)

            pe.wait_ge(s_taps[0], 1)
            pe.wait_ge(s_pads, 1)
            pe.wait_ge(s_const, 64)

            def gate(i, first=6):
                for u in range(2):
                    pe.wait_ge(s_xtl[0], 2 * i + u + 1)
                    products_aside(pe, bank[first + u][:, 0:2 * E0].rearrange("p (a e) -> p a e", a=2),
                                   [(x, lambda p, j=j: gateT[:, p, j, :]) for j, x in enumerate(XT(u))])\
                        .then_inc(s_gate[0], 1)

            def ranks(i, b=6):
                pe.wait_ge(s_hot, i + 1)
                for u in range(2):
                    dst = bank[b][:, RANK + u * E0:RANK + (u + 1) * E0]
                    pe.matmul(dst, con[:, C_TRI:C_TRI + P], picked[:, u, :], start=True, stop=False)
                    if u == 1:
                        pe.matmul(dst, con[:, C_ONE:C_ONE + P], picked[:, 0, :], start=False, stop=False)
                    mm = pe.matmul(dst, con[:, C_ONE:C_ONE + P], before[:, :], start=False, stop=True)
                mm.then_inc(s_rank, 1)

            def late0(i):
                def late(k):
                    if k == 2:
                        chain_turn(pe, 0, i)
                    if k == 4:
                        gate(i)
                    if k == 10:
                        ranks(i)
                return late

            staggered(pe, chain_tensor(pe, 0), late0)
            chain_turn(pe, 0, NB - 1)
            gate(NB - 1, LAST)

            def last_ranks():
                pe.wait_ge(s_ty, CREDIT + 2)
                ranks(NB - 1, LAST + 1)

            def total():
                pe.wait_ge(s_slots, NB + 1)
                pe.wait_ge(s_ty, CREDIT + 4)
                pe.matmul(bank[LAST + 1][:, 0:E0], con[:, C_ONE:C_ONE + P], before[:, :], start=True, stop=True)\
                  .then_inc(s_cnt, 1)

            def turn(h, u):
                pe.wait_ge(s_tx[u], 16 * h + 16)
                for j in range(HC):
                    mm = pe.transpose(bank[6 + u][:, j * P:(j + 1) * P], tin[:, u, j * P:(j + 1) * P], ident)
                mm.then_inc(s_txt, 1)

            def up(h, u, package, half):
                ready, where = package
                if half == 0:
                    hold(pe, s_pk, ready)
                    pe.wait_ge(s_txl, 2 * h + u + 1)
                js = range(HC // 2) if half == 0 else range(HC // 2, HC)
                mm = products(pe, bank[u][:, :],
                              [(XT(u)[j], lambda p, j=j: where(p, j * GU)) for j in js],
                              start=half == 0, stop=half == 1)
                if half == 1:
                    mm.then_inc(s_tup, 1)

            def turn_z(h, u):
                pe.wait_ge(s_tz, 2 * h + u + 1)
                for j in range(IC):
                    mm = pe.transpose(bank[2 + u][:, j * P:(j + 1) * P], z[:, u, j * P:(j + 1) * P], ident)
                mm.then_inc(s_tzt, 1)

            def down(h, u, package):
                where = package[1]
                pe.wait_ge(s_tzl, 2 * h + u + 1)
                pe.wait_ge(s_ty, 2 * h + u + 1)
                products(pe, bank[4 + u][:, :],
                         [(lambda p, j=j: zT[:, u, p, j, :], lambda p, j=j: where(p, DOWN + j * L))
                          for j in range(IC)]).then_inc(s_tdn, 1)

            def tiles(h0, n, package, between=()):
                def pair(i):
                    h = h0 + i
                    w1 = package(2 * i + 1)
                    turn(h + 1, 0)
                    up(h, 1, w1, 0)
                    w0 = package(2 * i)
                    turn_z(h, 0)
                    up(h, 1, w1, 1)
                    down(h, 0, w0)
                    w2 = package(2 * i + 2)
                    turn(h + 1, 1)
                    up(h + 1, 0, w2, 0)
                    turn_z(h, 1)
                    up(h + 1, 0, w2, 1)
                    down(h, 1, w1)

                turn(h0, 0)
                turn(h0, 1)
                w0 = package(0)
                up(h0, 0, w0, 0)
                up(h0, 0, w0, 1)
                for k, part in enumerate(between):
                    pair(k)
                    part()
                with pe.Fori(len(between), n - 1) as i:
                    pair(i)
                h = h0 + n - 1
                w0, w1 = package(2 * n - 2), package(2 * n - 1)
                up(h, 1, w1, 0)
                turn_z(h, 0)
                up(h, 1, w1, 1)
                down(h, 0, w0)
                turn_z(h, 1)
                down(h, 1, w1)

            tiles(0, NG // 2, lambda k: (2, lambda p, n: pack[:, place(0), p, n:n + 512]), (last_ranks, total))

            pe.wait_ge(s_route, 1)
            flat = pack[:, :, :, :].rearrange("p s h n -> p (s h n)")

            def chosen(k):
                number = pe.value_load(tab[0:1, 0, ds(k, 1)], min_val=1, max_val=E0)
                off = place(number) * SLOT
                return number * 2 + 2, lambda p, n: flat[:, ds(off + (p * PACK + n), 512)]

            tiles(NG // 2, TILES // 2, chosen)

            pe.wait_ge(s_taps[1], 1)
            pe.wait_ge(s_pads, 2)
            pe.wait_ge(s_pk, 2 * NPACK)
            W1 = place(NPACK - 1)

            def late1(i):
                def late(k):
                    if k == 2:
                        chain_turn(pe, 1, i)
                    if k == 4:
                        for u in range(2):
                            pe.wait_ge(s_xtl[1], 2 * i + u + 1)
                            products_aside(pe, bank[6 + u][:, 0:2 * NA].rearrange("p (a e) -> p a e", a=2),
                                           [(x, lambda p, j=j: pack[:, W1, p, HC * L + j * NA:HC * L + (j + 1) * NA])
                                            for j, x in enumerate(XT(u))]).then_inc(s_gate[1], 1)
                    if k == 9:
                        for u in range(2):
                            pe.wait_ge(s_rw, 2 * i + u + 1)
                            pe.transpose(bank[6 + u][:, HT:HT + P], hw[:, u, :], ident).then_inc(s_ht, 1)
                    if k in (10, 12):
                        u = (k - 10) // 2
                        pe.wait_ge(s_htl, 2 * i + u + 1)
                        base_products(u, 6)
                        low_products(i, u, 6)
                return late

            def base_products(u, first):
                products(pe, bank[first + u][:, :],
                         [(x, lambda p, j=j: pack[:, W1, p, j * L:(j + 1) * L]) for j, x in enumerate(XT(u))],
                         stop=False)

            def low_products(i, u, first):
                pe.wait_ge(s_htl, 2 * i + u + 1)
                products(pe, bank[first + u][:, :],
                         [(lambda p: hwT[:, u, p, :], lambda p: pack[:, W1, p, HC * (L + NA):HC * (L + NA) + L])],
                         start=False).then_inc(s_sum, 1)

            staggered(pe, chain_tensor(pe, 1), late1)
            rest = late1(NB - 1)
            for k in range(5):
                rest(k)
            for u in range(2):
                base_products(u, 0)
            rest(9)
            for u in range(2):
                low_products(NB - 1, u, 0)

        def build_taps(eng, c, link):
            w, f, u_ = craw[c], cf[c], cu[c]
            eng.tensor_scalar(f[:, 0:3, :], w[:, 0:3, :], CONV_SCALE, None, MUL)
            eng.tensor_scalar(f[:, 9:12, :], w[:, 6:9, :], CONV_SCALE, None, MUL)
            gain = 2 * BLUR * CONV_SCALE
            eng.tensor_scalar(u_[:, 0, :, :], w[:, 3:6, :], gain, None, MUL)
            eng.tensor_scalar(u_[:, 2, :, :], w[:, 9:12, :], BLUR * CONV_SCALE, None, MUL)
            link(eng.tensor_scalar(u_[:, 1, :, :], w[:, 3:6, :], 3 * gain, None, MUL))
            one, three = u_[:, 0, :, :], u_[:, 1, :, :]
            t = [f[:, 3 + r, :] for r in range(6)]
            eng.tensor_copy(t[0], one[:, 0, :])
            eng.tensor_copy(t[5], one[:, 2, :])
            eng.tensor_tensor(t[1], three[:, 0, :], one[:, 1, :], ADD)
            eng.tensor_tensor(t[4], one[:, 1, :], three[:, 2, :], ADD)
            eng.tensor_tensor(t[2], three[:, 0, :], three[:, 1, :], ADD)
            down = [f[:, 12 + r, :] for r in range(5)]
            w4 = [u_[:, 2, r, :] for r in range(3)]
            eng.tensor_copy(down[0], w4[0])
            eng.tensor_copy(down[4], w4[2])
            eng.tensor_tensor(down[1], w4[0], w4[1], ADD)
            eng.tensor_tensor(down[3], w4[1], w4[2], ADD)
            link(eng.tensor_tensor(t[3], three[:, 1, :], three[:, 2, :], ADD))
            eng.tensor_tensor(down[2], down[1], down[3], ADD)
            eng.tensor_tensor(t[2], t[2], one[:, 2, :], ADD)
            eng.tensor_tensor(down[1], down[1], w4[0], ADD)
            link(eng.tensor_tensor(down[3], down[3], w4[2], ADD))
            link(eng.tensor_tensor(t[3], t[3], one[:, 0, :], ADD))
            link(eng.tensor_copy(taps[c][:, 0, :, :], f[:, :, :]))
            eng.tensor_tensor(taps[c][:, 1, :, :], f[:, :, :], taps[c][:, 0, :, :].bitcast(F), SUB)\
               .then_inc(s_taps[c], 1)

        @block.vector
        def _(dve):
            count = [0]

            def link(ins):
                count[0] += 1
                ins.then_inc(s_chain, 1)
                dve.wait_ge(s_chain, count[0])

            tt, ts = dve.tensor_tensor, dve.tensor_scalar

            def clear_pads():
                for n in (0, L + 1):
                    dve.memset(val[:, :, n:n + 1], 0.0)
                for t_ in (in1, in2):
                    v = t_[:, :, :, :].rearrange("p u h n -> p (u h) n")
                    for n in (0, L + 1):
                        dve.memset(v[:, :, n:n + 1].bitcast(F), 0.0)
                for t_ in (in3, in4):
                    v = t_[:, :, :, :, :].rearrange("p u s h n -> p (u s h) n")
                    for n in (0, L + 1):
                        link(dve.memset(v[:, :, n:n + 1].bitcast(F), 0.0))

            dve.wait_ge(s_setup_in[1], 16)
            build_taps(dve, 0, link)
            dve.wait_ge(s_taps[0], 1)
            dve.wait_ge(s_squared, 2)
            for c in range(2):
                qv = csq[c][:, :, :].rearrange("p (l k) n -> p l k n", k=3)
                link(tt(qv[:, :, 0, :], qv[:, :, 0, :], qv[:, :, 1, :], ADD))
                link(tt(qv[:, :, 0, :], qv[:, :, 0, :], qv[:, :, 2, :], ADD))
            dve.wait_ge(s_sty, 1)
            dve.wait_ge(s_setup_in[0], 48)
            for c in range(2):
                for lay in range(LAYERS):
                    n = (c * LAYERS + lay) * NG
                    ins = ts(mod_s[:, c, lay, :], bank[0][:, n:n + NG], vec[:, c, 0, lay:lay + 1], None, ADD)
            link(ins)
            tt(dtmp[:, :, :, :], mod_s[:, :, :, :], mod_s[:, :, :, :], MUL).then_inc(s_sq, 1)
            dve.wait_ge(s_const, 64)
            dve.tensor_copy(gateT[:, 0, :, :], gateF[:, :, :])
            clear_pads()
            tt(gateT[:, 1, :, :], gateF[:, :, :], gateT[:, 0, :, :].bitcast(F), SUB)
            dve.memset(before[:, :], 0.0)
            dve.memset(nil[:, :], 0.0).then_inc(s_zero, 1)
            dve.wait_ge(s_zero, 1)
            dve.tensor_copy(tg[:, 0, 0:1], nil[:, :]).then_inc(s_pads, 1)
            chain0 = chain_vector(dve, 0)
            dsum = dem[:, :, :, :].rearrange("p c l g -> p (c l g)")
            dve.wait_ge(s_dsum, 1)
            ts(dsum, bank[7][:, 0:2 * LAYERS * NG], EPS, None, ADD).then_inc(s_dvar, 1)
            dve.wait_ge(s_dvar, 1)
            dve.wait_ge(s_root, 1)
            root = dtmp[:, :, :, :].rearrange("p c l g -> p (c l g)")
            r2 = scl[:, :, :, :].rearrange("p c l g -> p (c l g)")
            link(dve.reciprocal(root, root))
            link(tt(r2, root, root, MUL))
            link(tt(r2, r2, dsum, MUL))
            link(ts(r2, r2, -0.5, 1.5, MUL, ADD))
            link(tt(dsum, r2, root, MUL))
            for c in range(2):
                into = [mod_s[:, c, 0, :], dem[:, c, 1, :], mod_s[:, c, 2, :], mod_s[:, c, 3, :]]
                outof = [dem[:, c, 0, :], mod_s[:, c, 1, :], dem[:, c, 2, :], dem[:, c, 3, :]]
                for lay in range(LAYERS - 1):
                    tt(scl[:, c, lay, :], outof[lay], into[lay + 1], MUL)
                    link(ts(bia[:, c, lay, :], into[lay + 1], vec[:, c, 1, lay:lay + 1],
                            2.0 if lay == 1 else 1.0, MUL, MUL))
                dve.tensor_copy(scl[:, c, 3, :], outof[3])
                link(ts(edge[:, c, :], bia[:, c, 1, :], 1.75 / 2.0, None, MUL))
                dve.tensor_copy(tg[:, c, 0:1], nil[:, :]).then_inc(s_scales, 1)

            dve.sem_inc(s_slots, 1)
            STEPS = 12

            def late0(i):
                n = 0

                def step(ins, apart=False):
                    nonlocal n
                    n += 1
                    ins.then_inc(s_score, 1)
                    (hold if apart else wait)(dve, s_score, STEPS * i + n)

                shape = [P, 2, TOP0, E0]

                def gate_logits(first=6):
                    for u in range(2):
                        dve.wait_ge(s_gate[0], 2 * i + u + 1)
                        step(dve.tensor_copy(logit[:, u, :], bank[first + u][:, 0:E0]))
                        ins = tt(logit[:, u, :], logit[:, u, :], bank[first + u][:, E0:2 * E0], ADD)
                    ins.then_inc(s_logit, 1)

                def choose():
                    dve.wait_ge(s_tanh, i + 1)
                    step(ts(sc[:, :, :], tg[:, :, :], 0.5, 0.5, MUL, ADD))
                    step(tt(sc[:, :, :], sc[:, :, :], gbias[:, :].rearrange("p (a e) -> p a e", a=1)
                            .broadcast_to([P, 2, E0]), ADD), apart=True)
                    dve.max(m8[:, 0, :], sc[:, 0, :])
                    step(dve.max(m8[:, 1, :], sc[:, 1, :]), apart=True)
                    dve.max_index(i8[:, 0, :], m8[:, 0, :], sc[:, 0, :])
                    step(dve.max_index(i8[:, 1, :], m8[:, 1, :], sc[:, 1, :]))
                    step(dve.tensor_copy(itop[:, :, :], i8[:, :, :]), apart=True)
                    dve.tensor_copy(topv[:, ds(2 * i, 2), :], m8[:, :, :])
                    dve.tensor_copy(topi[:, ds(2 * i, 2), :], itop[:, :, 0:TOP0])
                    step(tt(hot[:, :, :, :], con[:, C_E:C_E + E0].rearrange("p (a b e) -> p a b e", a=1, b=1)
                            .broadcast_to(shape),
                            itop[:, :, 0:TOP0].rearrange("p u (k a) -> p u k a", a=1).broadcast_to(shape),
                            ALU.is_equal))
                    dve.tensor_reduce(picked[:, :, :], hot[:, :, :, :].rearrange("p u k e -> p u e k"), AX.X, ADD)\
                       .then_inc(s_hot, 1)

                def place_rows(b=6):
                    dve.wait_ge(s_rank, i + 1)
                    tt(rank[:, :, :], bank[b][:, RANK:RANK + 2 * E0].rearrange("p (u e) -> p u e", u=2),
                       con[:, C_FIRST:C_FIRST + E0].rearrange("p (a e) -> p a e", a=1)
                       .broadcast_to([P, 2, E0]), ADD)
                    step(tt(before[:, :], before[:, :], picked[:, 0, :], ADD))
                    step(tt(hot[:, :, :, :], hot[:, :, :, :],
                            rank[:, :, :].rearrange("p u (a e) -> p u a e", a=1).broadcast_to(shape), MUL))
                    step(tt(before[:, :], before[:, :], picked[:, 1, :], ADD))
                    step(dve.tensor_reduce(slotf[:, :, :], hot[:, :, :, :], AX.X, ADD), apart=True)
                    dve.tensor_copy(slot[:, ds(2 * i, 2), :], slotf[:, :, :]).then_inc(s_slots, 1)

                def late(k):
                    if k == 2:
                        chain_xt_low(dve, 0, i)
                    if k == 4:
                        gate_logits()
                        choose()
                    if k == 10:
                        place_rows()
                return late, gate_logits, choose, place_rows

            staggered(dve, chain0, lambda i: late0(i)[0])
            chain_xt_low(dve, 0, NB - 1)
            last_logits, last_choose, last_place = late0(NB - 1)[1:]
            last_logits(LAST)


            v = [plan[:, k, :] for k in range(10)]
            n_tiles, starts, t0, t1, inside = v[0], v[1], v[2], v[3], v[4]

            def plan_padding():
                dve.wait_ge(s_cnt, 1)
                link(dve.tensor_copy(counts[:, :], bank[LAST + 1][:, 0:E0]))
                link(ts(t0, counts[:, :], float(P - 1), None, ADD))
                link(dve.tensor_copy(plani[:, 0, :], t0))
                link(ts(plani[:, 1, :], plani[:, 0, :], 7, None, ALU.logical_shift_right))
                link(dve.tensor_copy(n_tiles, plani[:, 1, :]))
                link(ts(n_tiles, n_tiles, 1.0, None, ALU.max))
                link(ts(t0, counts[:, :], con[:, C_P:C_P + 1], None, ADD))
                link(ts(t1, n_tiles, float(P), None, MUL))
                link(tt(inside, t0, t1, ALU.is_lt))
                link(tt(t0, t0, con[:, C_FIRST:C_FIRST + E0], ADD))
                link(tt(t0, t0, con[:, C_SP:C_SP + E0], SUB))
                link(tt(t0, t0, inside, MUL))
                link(tt(t0, t0, con[:, C_SP:C_SP + E0], ADD))
                dve.tensor_copy(padi[:, :], t0).then_inc(s_padi, 1)
                dve.wait_ge(s_padi, 1)

            def plan_starts():
                src, dst, d = 0, 5, 1
                while d < E0:
                    dve.tensor_copy(plan[:, dst, 0:d], plan[:, src, 0:d])
                    link(tt(plan[:, dst, d:E0], plan[:, src, d:E0], plan[:, src, 0:E0 - d], ADD))
                    src, dst, d = dst, dst + 1, 2 * d
                assert src == 8
                link(tt(starts, v[8], n_tiles, SUB))
                dve.memset(plan[:, 9, 0:1], 0.0)
                link(tt(plan[:, 9, 1:E0], starts[:, 0:E0 - 1], starts[:, 1:E0], SUB))
                link(ts(plan[:, 9, 1:E0], plan[:, 9, 1:E0], float(P), float(CAP), MUL, ADD))

            t_iota = con[0:1, C_T:C_T + TILES]
            by_tile = [1, TILES, E0]

            def plan_packages():
                link(tt(cmp_t[:, :, :], t_iota.rearrange("p (t a) -> p t a", a=1).broadcast_to(by_tile),
                        starts[0:1, :].rearrange("p (a e) -> p a e", a=1).broadcast_to(by_tile), ALU.is_ge))
                link(dve.tensor_reduce(tabf[:, 0, :], cmp_t[:, :, :], AX.X, ADD))

            def plan_rows():
                link(tt(cmp_t[:, :, :], cmp_t[:, :, :],
                        plan[0:1, 9, :].rearrange("p (a e) -> p a e", a=1).broadcast_to(by_tile), MUL))
                link(dve.tensor_reduce(tabf[:, 2, :], cmp_t[:, :, :], AX.X, ADD))

            def plan_table():
                link(ts(t0[:, 0:1], v[8][:, E0 - 1:E0], -1.0, None, ADD))
                link(ts(tabf[:, 1, :], t_iota, t0[0:1, 0:1], float(P), ALU.min, MUL))
                link(tt(tabf[:, 1, :], tabf[:, 1, :], tabf[:, 2, :], ADD))
                link(ts(tabf[:, 2, 0:E0], starts[0:1, :], float(NG), None, ADD))
                dve.tensor_copy(tab[:, :, :], tabf[:, :, :]).then_inc(s_route, 1)
                dve.wait_ge(s_route, 1)

            chosen_all = [P, NG, TOP0, E0]

            def plan_results():
                link(ts(t0, starts, float(P), None, MUL))
                link(tt(t0, t0, con[:, C_FIRST:C_FIRST + E0], SUB))
                link(tt(hot_all[:, :, :, :], con[:, C_E:C_E + E0].rearrange("p (a b e) -> p a b e", a=1, b=1)
                        .broadcast_to(chosen_all),
                        topi[:, :, :].rearrange("p g (k a) -> p g k a", a=1).broadcast_to(chosen_all),
                        ALU.is_equal))

            def plan_results_rows():
                link(tt(hot_all[:, :, :, :], hot_all[:, :, :, :],
                        t0.rearrange("p (a b e) -> p a b e", a=1, b=1).broadcast_to(chosen_all), MUL))
                dve.tensor_copy(slots_f[:, :, :], slot[:, :, :])
                link(dve.tensor_reduce(moved[:, :, :], hot_all[:, :, :, :], AX.X, ADD))
                link(tt(moved[:, :, :], moved[:, :, :], slots_f[:, :, :], ADD))
                dve.tensor_copy(yslot[:, :, :], moved[:, :, :]).then_inc(s_yslot, 1)

            def xt_low(h, u):
                dve.wait_ge(s_txh, 2 * h + u + 1)
                tt(xT[:, u, 1, :, :].rearrange("p c t -> p (c t)"), bank[6 + u][:, :],
                   xT[:, u, 0, :, :].rearrange("p c t -> p (c t)").bitcast(F), SUB).then_inc(s_txl, 1)

            def zt_low(h, u):
                dve.wait_ge(s_tzh, 2 * h + u + 1)
                tt(zT[:, u, 1, :, :].rearrange("p c t -> p (c t)"), bank[2 + u][:, 0:I0],
                   zT[:, u, 0, :, :].rearrange("p c t -> p (c t)").bitcast(F), SUB).then_inc(s_tzl, 1)

            def gated(h, u):
                dve.wait_ge(s_tsg, 2 * h + u + 1)
                tt(z[:, u, :], bank[u][:, I0:GU], sg[:, u, :], MUL).then_inc(s_tz, 1)

            def tiles(h0, n, first=None, between=()):
                def pair(h):
                    xt_low(h + 1, 0)
                    zt_low(h, 0)
                    gated(h, 1)
                    xt_low(h + 1, 1)
                    zt_low(h, 1)
                    gated(h + 1, 0)

                xt_low(h0, 0)
                xt_low(h0, 1)
                if first:
                    first()
                gated(h0, 0)
                for k, part in enumerate(between):
                    pair(h0 + k)
                    part()
                if len(between) < n - 1:
                    with dve.Fori(len(between), n - 1) as i:
                        pair(h0 + i)
                h = h0 + n - 1
                zt_low(h, 0)
                gated(h, 1)
                zt_low(h, 1)

            tiles(0, NG // 2, last_choose,
                  (lambda: last_place(LAST + 1), plan_padding, plan_starts, plan_packages, plan_rows, plan_table))
            tiles(NG // 2, TILES // 2, None, (plan_results, plan_results_rows))

            dve.wait_ge(s_pk, 2 * NPACK)
            dve.wait_ge(s_tdn, NG + TILES)
            clear_pads()
            dve.tensor_copy(tg[:, 0, 0:1], nil[:, :]).then_inc(s_pads, 1)
            dve.sem_inc(s_fin, CREDIT)
            link(dve.tensor_reduce(wsum[:, :], topv[:, :, 0:TOP0], AX.X, ADD))
            link(ts(wsum[:, :], wsum[:, :], 1e-20, None, ADD))
            link(dve.reciprocal(wsum[:, :], wsum[:, :]))
            link(tt(wtok[:, :, :], topv[:, :, 0:TOP0], wsum[:, :].rearrange("p (g a) -> p g a", a=1)
                    .broadcast_to([P, NG, TOP0]), MUL))
            start1 = count[0] + 2 * (TOP0 - 1) + 1
            LOW_STEPS = 11

            def combine(h, step, us=(0, 1), first=False):
                for k in range(TOP0):
                    for u in us:
                        if k == 0:
                            dve.wait_ge(s_xsum, 2 * h + u + 1)
                        if first:
                            dve.wait_ge(s_first[u][k], 16)
                        elif k == 0:
                            dve.wait_ge(s_gat[u], 16 * TOP0 * h)
                        ins = dve.scalar_tensor_tensor(out=xrow[:, u, :], in0=gath[:, u, k, :],
                                                       scalar=wnow[:, u, k:k + 1], in1=xrow[:, u, :],
                                                       op0=MUL, op1=ADD)
                        if k == TOP0 - 1:
                            ins.then_inc(s_comb, 1)
                    if k < TOP0 - 1:
                        step(ins)

            link(dve.tensor_copy(wnow[:, :, :], wtok[:, 0:2, :]))
            chain1 = chain_vector(dve, 1, lambda u: combine(0, link, (u,), first=True))
            def body1(i, last, late):
                k = 0

                def step(ins):
                    nonlocal k
                    k += 1
                    ins.then_inc(s_chain, 1)
                    dve.wait_ge(s_chain, start1 + TOP0 * i + k)

                if not last:
                    hold(dve, s_comb, 2 * i + 2)
                    step(dve.tensor_copy(wnow[:, :, :], wtok[:, ds(2 * i + 2, 2), :]))

                chain1(i, last, late, lambda i_: combine(i_ + 1, step))

            def late1(i):
                n = 0

                def step(ins, apart=False):
                    nonlocal n
                    n += 1
                    ins.then_inc(s_low, 1)
                    (hold if apart else wait)(dve, s_low, LOW_STEPS * i + n)

                def largest():
                    dve.wait_ge(s_gate[1], 2 * i + 2)
                    dve.tensor_copy(low[:, 0, :], bank[6][:, 0:NA])
                    step(dve.tensor_copy(low[:, 1, :], bank[7][:, 0:NA]))
                    tt(low[:, 0, :], low[:, 0, :], bank[6][:, NA:2 * NA], ADD)
                    step(tt(low[:, 1, :], low[:, 1, :], bank[7][:, NA:2 * NA], ADD))
                    step(dve.tensor_reduce(lg[:, :, 0:1], low[:, :, 0:E1], AX.X, ALU.max))
                    ts(lg[:, :, 1:2], lg[:, :, 0:1], -1.0, None, MUL).then_inc(s_lmax, 1)

                both = lambda a_, b_: lg[:, :, a_:b_]
                one = lambda u, a_, b_: lg[:, u, a_:b_]
                e_iota = con[:, C_E:C_E + E1]

                def each(make, apart=False):
                    make(0)
                    step(make(1), apart)

                def likeliest():
                    dve.wait_ge(s_exp, 2 * i + 2)
                    step(dve.reciprocal(both(3, 4), both(2, 3)))
                    each(lambda u: ts(one(u, 16, 24), one(u, 8, 16), one(u, 3, 4), None, MUL), apart=True)
                    each(lambda u: dve.max(one(u, 24, 32), one(u, 16, 24)))
                    tt(both(4, 5), both(24, 25), both(25, 26), ADD)
                    each(lambda u: dve.max_index(i8b[:, u, :], one(u, 24, 32), one(u, 16, 24)))

                def weigh():
                    dve.reciprocal(both(5, 6), both(4, 5))
                    step(dve.tensor_copy(both(32, 40), i8b[:, :, :]))
                    each(lambda u: ts(one(u, 6, 8), one(u, 24, 26), one(u, 5, 6), None, MUL))
                    for u in range(2):
                        ts(one(u, 40, 48), e_iota, one(u, 32, 33), one(u, 6, 7), ALU.is_equal, MUL)
                    each(lambda u: ts(one(u, 48, 56), e_iota, one(u, 33, 34), one(u, 7, 8), ALU.is_equal, MUL))
                    step(tt(both(56, 64), both(40, 48), both(48, 56), ADD))
                    for u in range(2):
                        tt(hw[:, u, :].rearrange("p (e r) -> p e r", r=R1),
                           low[:, u, E1:NA].rearrange("p (e r) -> p e r", r=R1),
                           one(u, 56, 64).rearrange("p (e a) -> p e a", a=1).broadcast_to([P, E1, R1]), MUL)\
                            .then_inc(s_rw, 1)

                def rank_low(u):
                    dve.wait_ge(s_hth, 2 * i + u + 1)
                    tt(hwT[:, u, 1, :], bank[6 + u][:, HT:HT + P], hwT[:, u, 0, :].bitcast(F), SUB)\
                        .then_inc(s_htl, 1)

                def result(u):
                    first = 0 if isinstance(i, int) and i == NB - 1 else 6
                    dve.wait_ge(s_sum, 2 * i + u + 1)
                    dve.wait_ge(s_out[u], 16 * i + 16)
                    dve.wait_ge(s_bias, 2 * i + u + 1)
                    tt(yo[:, u, :], bank[first + u][:, :], res[:, u, :], ADD).then_inc(s_fin, 1)

                def late(k):
                    if k == 2:
                        chain_xt_low(dve, 1, i)
                    if k == 4:
                        largest()
                        likeliest()
                    if k == 6:
                        weigh()
                    for at_, part in ((6, rank_low), (BANKS, result)):
                        if k == at_:
                            for u in range(2):
                                part(u)
                return late

            staggered(dve, body1, late1)
            rest = late1(NB - 1)
            for k in range(BANKS + 1):
                rest(k)

        @block.gpsimd
        def _(pool):
            count = [0]

            def link(ins):
                count[0] += 1
                ins.then_inc(s_pchain, 1)
                pool.wait_ge(s_pchain, count[0])

            pool.wait_ge(s_setup_in[2], 16)
            build_taps(pool, 1, link)
            pool.wait_ge(s_taps[1], 1)
            pool.wait_ge(s_dsum, 1)
            pool.wait_ge(s_taps[0], 1)

            def whole(number):
                return a["packs"][ds(number, 1), :, :].rearrange("a p n -> p (a n)")

            HALVES = (slice(0, PACK // 2), slice(PACK // 2, PACK))

            def load_pack(h, b):
                pool.dma_start(raws[b], whole(3 * h + b)).then_inc(s_raw[b], 16)

            def high_pack(h, b):
                for k, cols in enumerate(HALVES):
                    pool.dma_start(pack[:, place(b), 0, cols], whole(3 * h + b)[:, cols]).then_inc(s_pk_hi[b][k], 16)

            def split_pack(h, b):
                hold(pool, s_raw[b], 16 * h + 16)
                for k, cols in enumerate(HALVES):
                    hold(pool, s_pk_hi[b][k], 16 * h + 16)
                    pool.tensor_tensor(pack[:, place(b), 1, cols], raws[b][:, cols],
                                       pack[:, place(b), 0, cols].bitcast(F), SUB).then_inc(s_pk, 1)
                pool.wait_ge(s_pk, 2 * (3 * h + b + 1))

            pool.wait_ge(s_val[0], 1)
            for b in (0, 2):
                load_pack(0, b)
                high_pack(0, b)
            split_pack(0, 0)
            load_pack(1, 0)

            def scatters(i, first=False):
                for u in range(2):
                    g = 2 * i + u
                    if not first:
                        hold(pool, s_scat[u], 16 * TOP0 * i)
                    hold(pool, s_saved[u], 16 * i + 32)
                    pool.dma_start(prow[:, u, :], xtok[ds(g * P, P), :]).then_inc(s_pool_in[u], 16)
                for u in range(2):
                    g = 2 * i + u
                    hold(pool, s_slots, i + 2)
                    pool.tensor_copy(idx[:, u, :], slot[:, ds(g, 1), :].rearrange("p a k -> p (a k)"))\
                        .then_inc(s_idx, 1)
                    pool.wait_ge(s_idx, g + 1)
                    hold(pool, s_pool_in[u], 16 * i + 16)
                    for k in range(TOP0):
                        pool.indirect_dma_start(out=xs,
                                                out_offset=bass.IndirectOffsetOnAxis(ap=idx[:, u, k:k + 1], axis=0),
                                                in_=prow[:, u, :], in_offset=None).then_inc(s_scat[u], 16)

            scatters(0, first=True)
            with pool.Fori(1, NB - 1) as i:
                scatters(i)
            pool.wait_ge(s_conv[0], BANKS * NB)
            pool.wait_ge(s_split[0], BANKS * NB)
            load_pack(0, 1)
            high_pack(0, 1)
            scatters(NB - 1)

            link(pool.memset(zero[:, :], 0.0))
            pool.wait_ge(s_padi, 1)
            for e in range(E0):
                pool.indirect_dma_start(out=xs, out_offset=bass.IndirectOffsetOnAxis(ap=padi[:, e:e + 1], axis=0),
                                        in_=zero[:, :], in_offset=None).then_inc(s_padded, 16)
            pool.wait_ge(s_route, 1)
            split_pack(0, 1)
            load_pack(1, 1)
            split_pack(0, 2)

            def package(h, b, more=True):
                through = pool.value_load(tab[0:1, 2, ds(3 * h + b - 3, 1)], min_val=NG, max_val=NG + TILES)
                hold(pool, s_tdn, through)
                high_pack(h, b)
                if more:
                    load_pack(h + (b + 2) // 3, (b + 2) % 3)
                split_pack(h, b)

            with pool.Fori(1, NPACK // 3 - 1) as h:
                for b in range(3):
                    package(h, b)
            for b in range(3):
                package(NPACK // 3 - 1, b, more=b == 0)

            def add_shared(h, u):
                hold(pool, s_x[1][u], 16 * h + 16)
                hold(pool, s_gsh[u], 16 * h + 16)
                pool.tensor_tensor(xrow[:, u, :], xrow[:, u, :], gath[:, u, TOP0, :], ADD).then_inc(s_xsum, 1)

            def add_bias(h, u):
                hold(pool, s_res[u], 16 * h + 16)
                pool.tensor_tensor(res[:, u, :], res[:, u, :], bb[:, :], ADD).then_inc(s_bias, 1)

            for u in range(2):
                add_shared(0, u)

            for u in range(2):
                pool.wait_ge(s_tys[u], 16 * ((NG + TILES) // 2 + 1))

            pool.wait_ge(s_yslot, 1)

            def gather(g, u, ready=None):
                pool.tensor_copy(idx[:, u, :], yslot[:, ds(g, 1), :].rearrange("p a k -> p (a k)"))\
                    .then_inc(s_idx, 1)
                hold(pool, s_idx, NG + g + 1)
                for k in range(TOP0):
                    pool.indirect_dma_start(out=gath[:, u, k, :], out_offset=None, in_=ys,
                                            in_offset=bass.IndirectOffsetOnAxis(ap=idx[:, u, k:k + 1], axis=0))\
                        .then_inc(ready[k] if ready else s_gat[u], 16)

            for u in range(2):
                gather(u, u, s_first[u])

            def body1(i, residual=True):
                for u in range(2):
                    pool.wait_ge(s_comb, 2 * i + u + 1)
                    gather(2 * i + 2 + u, u)
                for u in range(2):
                    add_shared(i + 1, u)
                if residual:
                    for u in range(2):
                        add_bias(i - 1, u)

            body1(0, residual=False)
            with pool.Fori(1, NB - 1) as i:
                body1(i)
            for i in (NB - 2, NB - 1):
                for u in range(2):
                    add_bias(i, u)


def laid_out(x, cond_512, w):
    f = np.float32
    arr = {}
    arr["x"] = np.ascontiguousarray(x).reshape(NG, P, L)
    con = np.zeros((P, C_END), f)
    con[:, C_ID:C_ID + P] = np.eye(P)
    con[:, C_TRI:C_TRI + P] = np.triu(np.ones((P, P)), 1)
    con[:, C_ONE:C_ONE + P] = 1
    con[:, C_E:C_E + E0] = np.arange(E0)
    con[:, C_T:C_T + TILES] = np.arange(TILES)
    con[:, C_P] = np.arange(P)
    con[:, C_SP:C_SP + E0] = SPARE + np.arange(E0) * P + np.arange(P)[:, None]
    con[:, C_FIRST:C_FIRST + E0] = np.arange(E0) * CAP
    arr["consts"] = con
    arr["style_t"] = np.ascontiguousarray(cond_512.T)
    mod = np.zeros((STYLE, 2, LAYERS, SPG, P), f)
    vec = np.zeros((P, 2, 2, LAYERS), f)
    for c in range(2):
        mw, mb = w[f"L{c}_cond_mod_w"], w[f"L{c}_cond_mod_b"]
        for b in range(SPG):
            mod[:, c, :, b, b * C:(b + 1) * C] = mw.transpose(2, 0, 1)
            vec[b * C:(b + 1) * C, c, 0, :] = mb.T
            vec[b * C:(b + 1) * C, c, 1, :] = w[f"L{c}_cond_biases"].T
        cw = w[f"L{c}_cond_weights"]
        conv = np.zeros((P, 15, P), f)
        for n, (layer, turned) in enumerate(((0, 1), (1, 0), (2, 1), (3, 1), (1, 1))):
            for k in range(TAPS):
                m = cw[layer, :, :, k].T if turned else cw[layer, :, :, k]
                for b in range(SPG):
                    conv[b * C:(b + 1) * C, 3 * n + k, b * C:(b + 1) * C] = m
        arr[f"conv{c}"] = conv
    arr["mod_t"], arr["vecs"] = mod, vec

    def rows(m, chunks):
        return m.reshape(chunks, P, -1).transpose(1, 0, 2)

    arr["gate_t"] = np.ascontiguousarray(rows(w["L0_ffn_gate_w"].T, HC))
    arr["gate_bias"] = np.ascontiguousarray(np.broadcast_to(w["L0_ffn_bias"], (P, E0)))
    arr["base_bias"] = np.ascontiguousarray(np.broadcast_to(w["L1_ffn_b_base"], (P, L)))
    packs = np.zeros((NPACK, P, PACK), f)

    def expert(m, wg, wu, wd):
        gu = np.concatenate([rows(wg.T, HC), rows(wu.T, HC)], axis=2)
        packs[m, :, 0:DOWN] = gu.reshape(P, -1)
        packs[m, :, DOWN:DOWN + IC * L] = rows(wd.T, IC).reshape(P, -1)

    expert(0, w["L0_ffn_Sg"], w["L0_ffn_Su"], w["L0_ffn_Sd"])
    for e in range(E0):
        expert(1 + e, w["L0_ffn_Wg"][e], w["L0_ffn_Wu"][e], w["L0_ffn_Wd"][e])
    low = np.concatenate([w["L1_ffn_W_gate"], w["L1_ffn_A"].reshape(E1 * R1, L)], axis=0)
    packs[NPACK - 1] = np.concatenate([
        rows(w["L1_ffn_W_base"].T, HC).reshape(P, -1), rows(low.T, HC).reshape(P, -1),
        w["L1_ffn_B"].transpose(0, 2, 1).reshape(E1 * R1, L)], axis=1)
    arr["packs"] = packs
    return arr


def kernel(x, cond_512, **weights):
    import concourse.bacc as bacc
    from concourse.bass_utils import run_bass_kernel_spmd

    w = {k: np.asarray(v) for k, v in weights.items()}
    arrays = laid_out(np.asarray(x), np.asarray(cond_512), w)
    nc = bacc.Bacc("TRN2", target_bir_lowering=False, num_devices=1)
    a = {k: nc.dram_tensor(f"in_{k}", v.shape, mybir.dt.float32, kind="ExternalInput").ap()
         for k, v in arrays.items()}
    out = nc.dram_tensor("out", (NG * P, L), mybir.dt.float32, kind="ExternalOutput").ap()
    build(nc, a, out)
    r = run_bass_kernel_spmd(nc, [{f"in_{k}": v for k, v in arrays.items()}], core_ids=[0])
    return r.results[0]["out"].reshape(B, C, L)
```
